# Optimizing a Trainium2 kernel written in Bass

```python
import numpy as np
import jax
import jax.numpy as jnp

def _softmax(x, axis=-1):
    return jax.nn.softmax(x, axis=axis)

def _gelu(x):
    return jax.nn.gelu(x, approximate=True)

def _silu(x):
    return jax.nn.silu(x)

def _sigmoid(x):
    return jax.nn.sigmoid(x)

def _layernorm(x, axis=-1, eps=1e-05):
    m = jnp.mean(x, axis=axis, keepdims=True)
    v = jnp.var(x, axis=axis, keepdims=True)
    return (x - m) / jnp.sqrt(v + eps)

def _scatter_add(tgt, idx, src, axis=0):
    return tgt.at[idx].add(src)

def _segment_sum(src, seg, n):
    return jax.ops.segment_sum(src, seg, n)
kernel_name = 'mk_gnn_resnorm_d4_gnn_r32_a03d55'

def setup_inputs(seed: int=0):
    np.random.seed(seed)
    _w = jnp.asarray

    def _rec_inputs():
        import jax
        import jax.numpy as jnp
        _gk = jax.random.key(seed)
        x = -0.000202 + 1 * jax.random.normal(jax.random.fold_in(_gk, 1), (3125, 64), jnp.float32)
        _s = jax.random.randint(jax.random.fold_in(_gk, 2), (50000,), 0, 3125, jnp.int32)
        _d = jax.random.randint(jax.random.fold_in(_gk, 3), (50000,), 0, 3125, jnp.int32)
        _loop = jnp.arange(3125, dtype=jnp.int32)
        src = jnp.concatenate([_s, _d, _loop])
        dst = jnp.concatenate([_d, _s, _loop])
        _o = jnp.argsort(dst, stable=True)
        src = src[_o]
        dst = dst[_o]
        edge_attr_64 = 7.68618e-05 + 1.00005 * jax.random.normal(jax.random.fold_in(_gk, 13), (103125, 64), jnp.float32)
        edge_weight = jax.random.uniform(jax.random.fold_in(_gk, 15), (103125,), jnp.float32, 0.0, 1)
        return (x, src, dst, edge_attr_64, edge_weight)
    x, src, dst, edge_attr_64, edge_weight = _rec_inputs()

    def _L0_gnn_setup():
        import jax, jax.numpy as jnp
        import numpy as np
        N_NODES = 3125
        N_EDGES = 31250
        D_IN = 64
        D_OUT = 64
        key = jax.random.key(seed)
        k_x, k_ei, k_ea, k_w, k_b = jax.random.split(key, 5)
        x = jax.random.normal(k_x, (N_NODES, D_IN), dtype=jnp.float32)
        edge_index = jax.random.randint(k_ei, (2, N_EDGES), 0, N_NODES, dtype=jnp.int64)
        edge_attr = jax.random.normal(k_ea, (N_EDGES, D_IN), dtype=jnp.float32)
        bound = 1.0 / np.sqrt(D_IN)
        W = jax.random.uniform(k_w, (D_OUT, D_IN), dtype=jnp.float32, minval=-bound, maxval=bound)
        b = jax.random.uniform(k_b, (D_OUT,), dtype=jnp.float32, minval=-bound, maxval=bound)
        eps = jnp.zeros((), dtype=jnp.float32)
        return {'x': x, 'edge_index': edge_index, 'edge_attr': edge_attr, 'W': W, 'b': b, 'eps': eps}
    _L0_gnn_all = _L0_gnn_setup()
    _L0_gnn_in = {k: v for k, v in _L0_gnn_all.items() if k in ('W', 'b', 'eps')}
    del _L0_gnn_all

    def _L1_gnn_setup():
        import jax, jax.numpy as jnp
        import numpy as np
        import math
        N_NODES = 3125
        D = 64
        N_EDGES = 40000
        LN_EPS = 1e-05
        key = jax.random.key(seed)
        ks = jax.random.split(key, 8)
        x = jax.random.normal(ks[0], (N_NODES, D), dtype=jnp.float32)
        edge_index = jax.random.randint(ks[1], (2, N_EDGES), 0, N_NODES, dtype=jnp.int64)
        limit = 0.1 * math.sqrt(6.0 / (D + D))
        qk_w = jax.random.uniform(ks[2], (D, D), dtype=jnp.float32, minval=-limit, maxval=limit)
        v_w = jax.random.uniform(ks[3], (D, D), dtype=jnp.float32, minval=-limit, maxval=limit)
        o_w = jax.random.uniform(ks[4], (D, D), dtype=jnp.float32, minval=-limit, maxval=limit)
        qk_b = jnp.zeros((D,), dtype=jnp.float32)
        v_b = jnp.zeros((D,), dtype=jnp.float32)
        o_b = jnp.zeros((D,), dtype=jnp.float32)
        ln_g = jnp.ones((D,), dtype=jnp.float32)
        ln_b = jnp.zeros((D,), dtype=jnp.float32)
        return {'x': x, 'edge_index': edge_index, 'qk_w': qk_w, 'qk_b': qk_b, 'v_w': v_w, 'v_b': v_b, 'o_w': o_w, 'o_b': o_b, 'ln_g': ln_g, 'ln_b': ln_b}
    _L1_gnn_all = _L1_gnn_setup()
    _L1_gnn_in = {k: v for k, v in _L1_gnn_all.items() if k in ('qk_w', 'qk_b', 'v_w', 'v_b', 'o_w', 'o_b', 'ln_g', 'ln_b')}
    del _L1_gnn_all

    def _L2_gnn_setup():
        import jax, jax.numpy as jnp
        import numpy as np
        N_NODES = 3125
        N_EDGES = 50000
        DIM = 64
        LAYERS = 2
        key = jax.random.key(seed)
        k1, k2, k3, k4 = jax.random.split(key, 4)
        h = jax.random.normal(k1, (N_NODES, DIM), dtype=jnp.float32)
        w = jax.random.uniform(k2, (N_EDGES,), dtype=jnp.float32)
        src = jax.random.randint(k3, (N_EDGES,), 0, N_NODES, dtype=jnp.int32)
        dst = jax.random.randint(k4, (N_EDGES,), 0, N_NODES, dtype=jnp.int32)
        return {'h': h, 'w': w, 'src': src, 'dst': dst}
    _L2_gnn_all = _L2_gnn_setup()
    _L2_gnn_in = {k: v for k, v in _L2_gnn_all.items() if k in ()}
    del _L2_gnn_all

    def _L3_gnn_setup():
        import jax, jax.numpy as jnp
        import numpy as np
        N = 2048
        E = 32768
        DIN = 64
        DOUT = 64

        def _linear(x, W, b):
            return x @ W.T + b

        def _mean_agg(h, norm, src, dst, n_nodes):
            msg = (h * norm)[src]
            summed = jax.ops.segment_sum(msg, dst, num_segments=n_nodes)
            deg = jax.ops.segment_sum(jnp.ones((dst.shape[0],), h.dtype), dst, num_segments=n_nodes)
            return summed / jnp.maximum(deg, 1.0)[:, None]
        key = jax.random.key(seed)
        ks = jax.random.split(key, 16)
        inp = {'feat': jax.random.normal(ks[0], (N, DIN), dtype=jnp.float32), 'norm': jax.random.uniform(ks[1], (N, 1), dtype=jnp.float32), 'src': jax.random.randint(ks[2], (E,), 0, N, dtype=jnp.int32), 'dst': jax.random.randint(ks[3], (E,), 0, N, dtype=jnp.int32)}
        s = 0.05
        inp['W_self'] = jax.random.normal(ks[4], (DOUT, DIN)) * s
        inp['b_self'] = jnp.zeros((DOUT,), jnp.float32)
        inp['W_self_high'] = jax.random.normal(ks[5], (DOUT, DIN)) * s
        inp['b_self_high'] = jnp.zeros((DOUT,), jnp.float32)
        inp['W_neigh'] = jax.random.normal(ks[6], (DOUT, DIN)) * s
        inp['b_neigh'] = jnp.zeros((DOUT,), jnp.float32)
        inp['W_neigh_high'] = jax.random.normal(ks[7], (DOUT, DIN)) * s
        inp['b_neigh_high'] = jnp.zeros((DOUT,), jnp.float32)
        inp['W_id'] = jax.random.normal(ks[8], (DOUT, DIN)) * s
        inp['b_id'] = jnp.zeros((DOUT,), jnp.float32)
        inp['w_att_low'] = jax.random.normal(ks[9], (1, DOUT)) * s
        inp['w_att_high'] = jax.random.normal(ks[10], (1, DOUT)) * s
        inp['w_att_mlp'] = jax.random.normal(ks[11], (1, DOUT)) * s
        inp['W_att'] = jax.random.normal(ks[12], (3, 3)) * s
        return inp
    _L3_gnn_all = _L3_gnn_setup()
    _L3_gnn_in = {k: v for k, v in _L3_gnn_all.items() if k in ('W_self', 'b_self', 'W_self_high', 'b_self_high', 'W_neigh', 'b_neigh', 'W_neigh_high', 'b_neigh_high', 'W_id', 'b_id', 'w_att_low', 'w_att_high', 'w_att_mlp', 'W_att')}
    del _L3_gnn_all
    return {'x': x, 'src': src, 'dst': dst, 'edge_attr_64': edge_attr_64, 'edge_weight': edge_weight, 'L0_gnn_W': _L0_gnn_in['W'], 'L0_gnn_b': _L0_gnn_in['b'], 'L0_gnn_eps': _L0_gnn_in['eps'], 'L1_gnn_qk_w': _L1_gnn_in['qk_w'], 'L1_gnn_qk_b': _L1_gnn_in['qk_b'], 'L1_gnn_v_w': _L1_gnn_in['v_w'], 'L1_gnn_v_b': _L1_gnn_in['v_b'], 'L1_gnn_o_w': _L1_gnn_in['o_w'], 'L1_gnn_o_b': _L1_gnn_in['o_b'], 'L1_gnn_ln_g': _L1_gnn_in['ln_g'], 'L1_gnn_ln_b': _L1_gnn_in['ln_b'], 'L3_gnn_W_self': _L3_gnn_in['W_self'], 'L3_gnn_b_self': _L3_gnn_in['b_self'], 'L3_gnn_W_self_high': _L3_gnn_in['W_self_high'], 'L3_gnn_b_self_high': _L3_gnn_in['b_self_high'], 'L3_gnn_W_neigh': _L3_gnn_in['W_neigh'], 'L3_gnn_b_neigh': _L3_gnn_in['b_neigh'], 'L3_gnn_W_neigh_high': _L3_gnn_in['W_neigh_high'], 'L3_gnn_b_neigh_high': _L3_gnn_in['b_neigh_high'], 'L3_gnn_W_id': _L3_gnn_in['W_id'], 'L3_gnn_b_id': _L3_gnn_in['b_id'], 'L3_gnn_w_att_low': _L3_gnn_in['w_att_low'], 'L3_gnn_w_att_high': _L3_gnn_in['w_att_high'], 'L3_gnn_w_att_mlp': _L3_gnn_in['w_att_mlp'], 'L3_gnn_W_att': _L3_gnn_in['W_att']}

def reference(x, src, dst, edge_attr_64, edge_weight, L0_gnn_W, L0_gnn_b, L0_gnn_eps, L1_gnn_qk_w, L1_gnn_qk_b, L1_gnn_v_w, L1_gnn_v_b, L1_gnn_o_w, L1_gnn_o_b, L1_gnn_ln_g, L1_gnn_ln_b, L3_gnn_W_self, L3_gnn_b_self, L3_gnn_W_self_high, L3_gnn_b_self_high, L3_gnn_W_neigh, L3_gnn_b_neigh, L3_gnn_W_neigh_high, L3_gnn_b_neigh_high, L3_gnn_W_id, L3_gnn_b_id, L3_gnn_w_att_low, L3_gnn_w_att_high, L3_gnn_w_att_mlp, L3_gnn_W_att):
    import jax
    import jax.numpy as jnp

    def _L0_gnn_ref(x, edge_index, edge_attr, W, b, eps):
        import jax, jax.numpy as jnp
        import numpy as np
        N_NODES = 3125
        N_EDGES = 31250
        D_IN = 64
        D_OUT = 64
        src = edge_index[0]
        dst = edge_index[1]
        msg = jax.nn.relu(x[src] + edge_attr)
        agg = jax.ops.segment_sum(msg, dst, num_segments=x.shape[0])
        h = (1.0 + eps) * x + agg
        out = h @ W.T + b
        return jax.nn.relu(out)

    def _L1_gnn_ref(x, edge_index, qk_w, qk_b, v_w, v_b, o_w, o_b, ln_g, ln_b):
        import jax, jax.numpy as jnp
        import numpy as np
        import math
        N_NODES = 3125
        D = 64
        N_EDGES = 40000
        LN_EPS = 1e-05
        n = x.shape[0]
        qk = x @ qk_w.T + qk_b
        v = x @ v_w.T + v_b
        src = edge_index[0]
        dst = edge_index[1]
        scores = jnp.sum(qk[dst] * qk[src], axis=-1) / math.sqrt(v.shape[-1])
        scores = jnp.clip(scores, -5.0, 5.0)
        seg_max = jax.ops.segment_max(scores, dst, num_segments=n)
        e = jnp.exp(scores - seg_max[dst])
        seg_sum = jax.ops.segment_sum(e, dst, num_segments=n)
        attn = e / seg_sum[dst]
        out = jax.ops.segment_sum(attn[:, None] * v[src], dst, num_segments=n)
        out = out @ o_w.T + o_b
        h = out + x
        mu = jnp.mean(h, axis=-1, keepdims=True)
        var = jnp.mean(jnp.square(h - mu), axis=-1, keepdims=True)
        h = (h - mu) * jax.lax.rsqrt(var + LN_EPS)
        return h * ln_g + ln_b

    def _L2_gnn_ref(h, w, src, dst):
        import jax, jax.numpy as jnp
        import numpy as np
        N_NODES = 3125
        N_EDGES = 50000
        DIM = 64
        LAYERS = 2
        N = h.shape[0]
        deg = jnp.maximum(jax.ops.segment_sum(w, dst, num_segments=N), 1.0)
        norm = deg[:, None] ** (-0.5)
        embs = [h]
        for _ in range(LAYERS):
            h_norm = h * norm
            m = h_norm[src] * w[:, None]
            neigh_sum = jax.ops.segment_sum(m, dst, num_segments=N)
            h = neigh_sum * norm
            embs.append(h)
        return jnp.mean(jnp.stack(embs, axis=1), axis=1)

    def _L3_gnn_ref(feat, norm, src, dst, W_self, b_self, W_self_high, b_self_high, W_neigh, b_neigh, W_neigh_high, b_neigh_high, W_id, b_id, w_att_low, w_att_high, w_att_mlp, W_att):
        import jax, jax.numpy as jnp
        import numpy as np
        N = 2048
        E = 32768
        DIN = 64
        DOUT = 64

        def _linear(x, W, b):
            return x @ W.T + b

        def _mean_agg(h, norm, src, dst, n_nodes):
            msg = (h * norm)[src]
            summed = jax.ops.segment_sum(msg, dst, num_segments=n_nodes)
            deg = jax.ops.segment_sum(jnp.ones((dst.shape[0],), h.dtype), dst, num_segments=n_nodes)
            return summed / jnp.maximum(deg, 1.0)[:, None]
        n = feat.shape[0]
        self_low = jax.nn.relu(_linear(feat, W_self, b_self))
        self_high = jax.nn.relu(_linear(feat, W_self_high, b_self_high))
        neigh_low = _mean_agg(jax.nn.relu(_linear(feat, W_neigh, b_neigh)), norm, src, dst, n)
        neigh_high = _mean_agg(jax.nn.relu(_linear(feat, W_neigh_high, b_neigh_high)), norm, src, dst, n)
        low = self_low + neigh_low
        high = self_high - neigh_high
        identity = jax.nn.relu(_linear(feat, W_id, b_id))
        logits = jnp.concatenate([low @ w_att_low.T, high @ w_att_high.T, identity @ w_att_mlp.T], axis=1)
        att = jax.nn.softmax(jax.nn.sigmoid(logits) @ W_att.T / 3.0, axis=1)
        rst = 3.0 * (att[:, 0:1] * low + att[:, 1:2] * high + att[:, 2:3] * identity)
        return rst
    edge_index = jnp.stack([src, dst])
    deg = jnp.maximum(jax.ops.segment_sum(jnp.ones(dst.shape, jnp.float32), dst, num_segments=3125), 1.0)
    deg_isqrt = deg ** (-0.5)
    x = _layernorm(x + _L0_gnn_ref(x, edge_index, edge_attr_64, L0_gnn_W, L0_gnn_b, L0_gnn_eps), axis=-1)
    x = _layernorm(x + _L1_gnn_ref(x, edge_index, L1_gnn_qk_w, L1_gnn_qk_b, L1_gnn_v_w, L1_gnn_v_b, L1_gnn_o_w, L1_gnn_o_b, L1_gnn_ln_g, L1_gnn_ln_b), axis=-1)
    x = _layernorm(x + _L2_gnn_ref(x, edge_weight, src, dst), axis=-1)
    x = _layernorm(x + _L3_gnn_ref(x, deg_isqrt[:, None], src, dst, L3_gnn_W_self, L3_gnn_b_self, L3_gnn_W_self_high, L3_gnn_b_self_high, L3_gnn_W_neigh, L3_gnn_b_neigh, L3_gnn_W_neigh_high, L3_gnn_b_neigh_high, L3_gnn_W_id, L3_gnn_b_id, L3_gnn_w_att_low, L3_gnn_w_att_high, L3_gnn_w_att_mlp, L3_gnn_W_att), axis=-1)
    return x

_drawn_inputs = setup_inputs


def setup_inputs(seed=0):
    import zlib

    import numpy as np

    out = dict(_drawn_inputs(seed))
    spreads = {'L1_gnn_qk_b': (0.0, 2.0),
     'L1_gnn_v_b': (0.0, 0.8),
     'L1_gnn_o_b': (0.0, 0.1),
     'L1_gnn_ln_g': (1.0, 0.2),
     'L1_gnn_ln_b': (0.0, 0.1),
     'L3_gnn_b_self': (0.0, 0.1),
     'L3_gnn_b_self_high': (0.0, 0.1),
     'L3_gnn_b_neigh': (0.0, 0.638),
     'L3_gnn_b_neigh_high': (0.0, 0.631),
     'L3_gnn_b_id': (0.0, 0.1)}
    factors = {'edge_weight': 42.453,
     'L0_gnn_b': 6.469,
     'L1_gnn_qk_w': 8.0,
     'L1_gnn_v_w': 8.0,
     'L1_gnn_o_w': 5.806,
     'L3_gnn_w_att_low': 64.0,
     'L3_gnn_w_att_high': 64.0,
     'L3_gnn_w_att_mlp': 64.0,
     'L3_gnn_W_att': 64.0}
    for name, (base, spread) in spreads.items():
        noise = np.random.default_rng([zlib.crc32(name.encode()), seed]).standard_normal(out[name].shape)
        drawn = base * np.exp(spread * noise) if base else spread * noise
        out[name] = jnp.asarray(drawn.astype(out[name].dtype))
    for name, factor in factors.items():
        out[name] = (out[name] * factor).astype(out[name].dtype)
    return out
```

```python
from contextlib import ExitStack

import concourse.bass as bass
from concourse import mybir

P = 128
D = 64
NODES = 3125
EDGES = 103125
CHUNKS = -(-NODES // P)
NPAD = CHUNKS * P
LAST_NODES = NODES - (CHUNKS - 1) * P
FULL_TILES = EDGES // P
TILES = -(-EDGES // P)
TAIL_EDGES = EDGES - FULL_TILES * P
G = 8
GROUPS = -(-TILES // G)
LAST_TILES = TILES - (GROUPS - 1) * G
U = 4
ROUNDS = (GROUPS - 1) // U
TBLK = -(-TILES // P)
LAST_BLK_TILES = FULL_TILES - (TBLK - 1) * P
TCOLS = TBLK * P
AGG = NPAD + P
BANK = 512
PER_BANK = BANK // P
assert GROUPS == ROUNDS * U + 1 and TCOLS >= (GROUPS + 1) * G

F32 = mybir.dt.float32
I32 = mybir.dt.int32
ALU = mybir.AluOpType
ACT = mybir.ActivationFunctionType
AX_X = mybir.AxisListType.X
DVE_ONLY = (mybir.EngineType.DVE,)
PE_ONLY = (mybir.EngineType.PE,)
LN_EPS = 1e-5
IN_RANGE = "a first destination is a node's number"

LINEAR = [("L0_gnn_W", "L0_gnn_b"), ("L1_gnn_qk_w", "L1_gnn_qk_b"), ("L1_gnn_v_w", "L1_gnn_v_b"),
          ("L3_gnn_W_neigh", "L3_gnn_b_neigh"), ("L3_gnn_W_neigh_high", "L3_gnn_b_neigh_high"),
          ("L3_gnn_W_self", "L3_gnn_b_self"), ("L3_gnn_W_self_high", "L3_gnn_b_self_high"),
          ("L3_gnn_W_id", "L3_gnn_b_id"), ("L1_gnn_o_w", None)]
W_L0, W_QK, W_V, W_NEIGH, W_SELF, W_ID, W_O = 0, 1, 2, 3, 5, 7, 8
ROWS = ["L1_gnn_o_b", "L1_gnn_ln_g", "L1_gnn_ln_b", "L3_gnn_w_att_low", "L3_gnn_w_att_high",
        "L3_gnn_w_att_mlp"]
R_OB, R_LNG, R_LNB, R_ATT = 0, 1, 2, 3


def gnn_program(nc, ins, out):
    with ExitStack() as ctx:
        def sb(name, shape, dt=F32):
            return ctx.enter_context(nc.sbuf_tensor(name, shape, dt))

        def sem(name):
            return ctx.enter_context(nc.semaphore(name))

        qkv_table = nc.dram_tensor("qkv_table", [NPAD, 2 * D], F32, kind="Internal").ap()
        h0_table = nc.dram_tensor("h0_table", [NPAD, D], F32, kind="Internal").ap()
        h1_table = nc.dram_tensor("h1_table", [NPAD, D], F32, kind="Internal").ap()
        neigh_table = nc.dram_tensor("neigh_table", [NPAD, 2 * D], F32, kind="Internal").ap()

        ident = sb("ident", [P, P])
        iota_i = sb("iota_i", [P, P], I32)
        iota = sb("iota", [P, P])
        src_idx = sb("src_idx", [P, TCOLS], I32)
        dst_rel = sb("dst_rel", [P, TCOLS])
        weight = sb("weight", [P, TCOLS])
        first_dst = sb("first_dst", [1, GROUPS * G], I32)
        w_stage = sb("w_stage", [D, len(LINEAR), D])
        w_t = sb("w_t", [D + 1, 8, D])
        o_t = sb("o_t", [D + 1, D + 1])
        rows = sb("rows", [P, len(ROWS), D])
        w_att = sb("w_att", [P, 9])
        eps0 = sb("eps0", [P, 1])
        eps0_p1 = sb("eps0_p1", [P, 1])
        x = sb("x", [P, CHUNKS, D])
        y = sb("y", [P, CHUNKS, D])
        y2 = sb("y2", [P, CHUNKS, D])
        y3 = sb("y3", [P, CHUNKS, D])
        table = sb("table", [P, CHUNKS, 2 * D])
        low = sb("low", [P, 3, CHUNKS, D])
        stat = sb("stat", [P, 16, CHUNKS])
        att = sb("att", [P, 3, CHUNKS])
        sig = sb("sig", [P, 3, CHUNKS])
        degs = sb("degs", [P, CHUNKS, 2])
        norm2 = sb("norm2", [P, CHUNKS])
        norm3 = sb("norm3", [P, CHUNKS])
        rdeg = sb("rdeg", [P, CHUNKS])
        x_t = sb("x_t", [D + 1, NPAD])
        h_t = sb("h_t", [D + 1, NPAD])
        qk_t = sb("qk_t", [D, AGG])
        agg = sb("agg", [P, AGG])
        idx = [sb(f"idx{k}", [P, G], I32) for k in range(U)]
        rows_g = sb("rows_g", [P, U, G, 2 * D + 1])
        attr = sb("attr", [P, U, G, D])
        msg = sb("msg", [P, U, G, D + 2])
        onehot = sb("onehot", [P, U, G, P])
        src_t = sb("src_t", [D, G, P])
        scores = sb("scores", [P, G, P])
        probs = sb("probs", [P, G, P])

        ps = ctx.enter_context(nc.psum_tensor("ps", [P, 8 * BANK], F32))

        src_d, dst_d, w_d = ins["src"], ins["dst"], ins["edge_weight"]

        def edge_blocks(a):
            full = (TBLK - 1) * P * P
            return (a[0:full].rearrange("(b r e) -> r b e", r=P, e=P),
                    a[full:FULL_TILES * P].rearrange("(r e) -> r e", e=P),
                    a[FULL_TILES * P:EDGES].rearrange("(r e) -> r e", r=1))

        def node_rows(a):
            full = (CHUNKS - 1) * P
            return a[0:full, :].rearrange("(c p) d -> p c d", p=P), a[full:NODES, :]

        def over_features(a):
            return a.unsqueeze(2).broadcast_to([P, CHUNKS, D])

        def over_chunks(a):
            return a.unsqueeze(1).broadcast_to([P, CHUNKS, D])

        ld_edges, ld_w, ld_x, ld_base = sem("ld_edges"), sem("ld_w"), sem("ld_x"), sem("ld_base")
        cleared, consts, made = sem("cleared"), sem("consts"), sem("made")
        edges_f, edges_t, w_done, x_done, base0 = (sem("edges_f"), sem("edges_t"), sem("w_done"),
                                                   sem("x_done"), sem("base0"))
        stage_i = attr[:, :, :, :].rearrange("p k j d -> p (k j d)")[:, 0:2 * TCOLS].bitcast(I32).rearrange(
            "p (n b e) -> p n b e", n=2, e=P)
        stage_f = onehot[:, :, :, :].rearrange("p k j d -> p (k j d)")[:, 0:3 * TCOLS].rearrange(
            "p (n b e) -> p n b e", n=3, e=P)
        stage_w = stage_f[:, 2, :, :]
        PS_EDGE = [0, 2 * BANK, 4 * BANK]
        PS_W = 6 * BANK
        with nc.Block() as block:
            @block.sync
            def _(sp):
                sp.wait_ge(cleared, 4)
                for n, (a, stage) in enumerate(((src_d, stage_i[:, 0, :, :]), (dst_d, stage_i[:, 1, :, :]),
                                                (w_d, stage_w))):
                    full, part, tail = edge_blocks(a)
                    sp.dma_start(stage[:, 0:TBLK - 1, :], full).then_inc(ld_edges, 16)
                    sp.dma_start(stage[0:LAST_BLK_TILES, TBLK - 1, :], part).then_inc(ld_edges, 16)
                    sp.dma_start(stage[LAST_BLK_TILES:LAST_BLK_TILES + 1, TBLK - 1, 0:TAIL_EDGES],
                                 tail).then_inc(ld_edges, 16)
                for n, (w, b) in enumerate(LINEAR):
                    sp.dma_start(w_stage[:, n, :], ins[w]).then_inc(ld_w, 16)
                    if b:
                        sp.dma_start(w_t[D:D + 1, n, :], ins[b].rearrange("(a d) -> a d", a=1)).then_inc(ld_w, 16)

            @block.scalar
            def _(act):
                act.wait_ge(base0, 1)
                firsts = dst_d[0:FULL_TILES * P].rearrange("(t e) -> e t", e=P)[0:1, :]
                with nc.allow_non_contiguous_dma(reason="one element of each tile, once"):
                    act.dma_start(first_dst[0:1, 0:FULL_TILES], firsts).then_inc(ld_base, 16)
                act.dma_start(first_dst[0:1, FULL_TILES:FULL_TILES + 1],
                              dst_d[FULL_TILES * P:FULL_TILES * P + 1].rearrange("(a e) -> a e", a=1)
                              ).then_inc(ld_base, 16)
                full, last = node_rows(ins["x"])
                act.wait_ge(cleared, 5)
                act.dma_start(x[:, 0:CHUNKS - 1, :], full).then_inc(ld_x, 16)
                act.dma_start(x[0:LAST_NODES, CHUNKS - 1, :], last).then_inc(ld_x, 16)
                for n, name in enumerate(ROWS):
                    act.dma_start(rows[:, n, :], ins[name].partition_broadcast(P)).then_inc(ld_w, 16)
                act.dma_start(w_att[:, :], ins["L3_gnn_W_att"].partition_broadcast(P)).then_inc(ld_w, 16)
                act.dma_start(eps0[:, :], ins["L0_gnn_eps"].partition_broadcast(P)).then_inc(ld_w, 16)
                act.wait_ge(ld_x, 32)
                act.wait_ge(ld_base, 32)

            LD_W = 16 * (2 * len(LINEAR) - 1 + len(ROWS) + 2)

            @block.gpsimd
            def _(pool):
                pool.memset(ident[:, :], 0.0).then_inc(consts, 1)
                pool.wait_ge(consts, 1)
                pool.iota(iota_i[:, :], pattern=[[1, P]], base=0, channel_multiplier=0).then_inc(consts, 1)
                pool.wait_ge(consts, 2)
                pool.affine_select(out=ident[:, :], in_=ident[:, :], compare_op=ALU.not_equal, fill=1.0,
                                   base=0, pattern=[[-1, P]], channel_multiplier=1).then_inc(made, 1)
                pool.wait_ge(made, 1)
                pool.memset(o_t[:, :], 0.0).then_inc(consts, 1)
                pool.wait_ge(consts, 3)
                for n, (view, value) in enumerate(((o_t[D:D + 1, D:D + 1], 1.0), (x_t[D:D + 1, :], 1.0),
                                                   (h_t[D:D + 1, :], 1.0), (msg[:, :, :, :], 1.0),
                                                   (rows_g[:, :, :, :], 1.0), (qk_t[:, NPAD:AGG], 0.0))):
                    pool.memset(view, value).then_inc(made, 1)
                    pool.wait_ge(made, n + 2)

            @block.vector
            def _(dve):
                dve.memset(stage_i[:, :, TBLK - 1, :], -1).then_inc(cleared, 1)
                dve.memset(stage_w[:, TBLK - 1, :], 0.0).then_inc(cleared, 1)
                dve.memset(first_dst[:, :], 0).then_inc(base0, 1)
                dve.memset(agg[:, :], 0.0).then_inc(cleared, 1)
                dve.memset(w_t[:, :, :], 0.0).then_inc(cleared, 1)
                dve.memset(x[:, CHUNKS - 1, :], 0.0).then_inc(cleared, 1)
                dve.wait_ge(ld_edges, 9 * 16)
                dve.tensor_scalar(stage_f[:, 0, :, :], stage_i[:, 0, :, :], 0.0, None, ALU.max).then_inc(edges_f, 1)
                dve.tensor_copy(stage_f[:, 1, :, :], stage_i[:, 1, :, :]).then_inc(edges_f, 1)
                dve.wait_ge(edges_f, 2)
                for b in range(TBLK):
                    dve.tensor_copy(stat[:, 0, b:b + 1], stage_f[:, 1, b, 0:1]).then_inc(edges_f, 1)
                dve.wait_ge(edges_f, 2 + TBLK)
                for b in range(TBLK):
                    dve.tensor_scalar(stage_f[:, 1, b, :], stage_f[:, 1, b, :], stat[:, 0, b:b + 1], None,
                                      ALU.subtract).then_inc(edges_f, 1)
                dve.wait_ge(consts, 2)
                dve.tensor_copy(iota[:, :], iota_i[:, :]).then_inc(edges_f, 1)
                for n, to in enumerate((src_idx, dst_rel, weight)):
                    dve.wait_ge(edges_t, n + 1)
                    dve.tensor_copy(to[:, :], ps[:, PS_EDGE[n]:PS_EDGE[n] + TCOLS]).then_inc(edges_f, 1)
                dve.wait_ge(w_done, 1)
                dve.wait_ge(made, 2)
                dve.tensor_copy(w_t[0:D, :, :], ps[0:D, PS_W:PS_W + 8 * D].rearrange("p (n d) -> p n d", d=D)
                                ).then_inc(edges_f, 1)
                dve.tensor_copy(o_t[0:D, 0:D], ps[0:D, PS_W + BANK:PS_W + BANK + D]).then_inc(edges_f, 1)
                dve.tensor_scalar(eps0_p1[:, :], eps0[:, :], 1.0, None, ALU.add).then_inc(edges_f, 1)
                dve.wait_ge(edges_f, 2 + 2 * TBLK + 1 + 3 + 3)

            @block.tensor
            def _(pe):
                pe.wait_ge(made, 1)
                pe.wait_ge(edges_f, 2 + 2 * TBLK)
                for n in range(3):
                    for b in range(TBLK):
                        t = pe.transpose(ps[:, PS_EDGE[n] + b * P:PS_EDGE[n] + (b + 1) * P],
                                         stage_f[:, n, b, :], ident[:, :])
                    t.then_inc(edges_t, 1)
                pe.wait_ge(ld_w, LD_W)
                for n in range(len(LINEAR)):
                    t = pe.transpose(ps[0:D, PS_W + n * D:PS_W + (n + 1) * D], w_stage[:, n, :],
                                     ident[0:D, 0:D])
                t.then_inc(w_done, 1)

        def transpose_nodes(name):
            t_done, t_copied = sem(f"{name}_t_done"), sem(f"{name}_t_copied")
            banks = -(-CHUNKS // PER_BANK)
            with nc.Block() as block:
                @block.tensor
                def _(pe):
                    for c in range(CHUNKS):
                        t = pe.transpose(ps[0:D, c * P:(c + 1) * P], x[:, c, :], ident[:, :])
                        if c % PER_BANK == PER_BANK - 1 or c == CHUNKS - 1:
                            t.then_inc(t_done, 1)

                @block.scalar
                def _(act):
                    for b in range(banks):
                        end = min((b + 1) * BANK, NPAD)
                        act.wait_ge(t_done, b + 1)
                        nc.scalar.copy(x_t[0:D, b * BANK:end], ps[0:D, b * BANK:end]).then_inc(t_copied, 1)
                    act.wait_ge(t_copied, banks)

        def edge_pass(name, source, width, with_attr=False, weighted=False):
            gathered = [sem(f"{name}_gathered{k}") for k in range(U)]
            attr_in = [sem(f"{name}_attr_in{k}") for k in range(U)]
            tail_in = sem(f"{name}_tail_in")
            staged, mm_done, onehot_in, hot, agg_free, added = (
                sem(f"{name}_staged"), sem(f"{name}_mm_done"), sem(f"{name}_onehot_in"), sem(f"{name}_hot"),
                sem(f"{name}_agg_free"), sem(f"{name}_added"))
            summed, msg_in, relu_in = sem(f"{name}_summed"), sem(f"{name}_msg_in"), sem(f"{name}_relu_in")
            out_rows = D + 2 if with_attr else width
            lhs = msg if with_attr else rows_g

            def window_sums(b):
                return ps[0:out_rows, (b % 2) * G * P:(b % 2 + 1) * G * P]

            with nc.Block() as block:
                @block.gpsimd
                def _(pool):
                    def stage(g, k):
                        pool.tensor_copy(idx[k][:, :], src_idx[:, bass.ds(g * G, G)]).then_inc(staged, 1)

                    def gather(g, k):
                        for j in range(G):
                            pool.indirect_dma_start(rows_g[:, k, j, 0:width], None, source,
                                                    bass.IndirectOffsetOnAxis(ap=idx[k][:, j:j + 1], axis=0)
                                                    ).then_inc(gathered[k], 16)

                    stage(0, 0)
                    with pool.Fori(0, ROUNDS) as r:
                        for k in range(U):
                            g = r * U + k
                            pool.wait_ge(mm_done, g + 1)
                            pool.wait_ge(staged, g + 1)
                            stage(g + 1, (k + 1) % U)
                            gather(g, k)
                    pool.wait_ge(mm_done, GROUPS)
                    pool.wait_ge(staged, GROUPS)
                    gather(GROUPS - 1, 0)

                if with_attr:
                    @block.sync
                    def _(sp):
                        by_tile = ins["edge_attr_64"][0:FULL_TILES * P, :].rearrange("(t p) d -> p t d", p=P)
                        with sp.Fori(0, ROUNDS) as r:
                            for k in range(U):
                                g = r * U + k
                                sp.wait_ge(msg_in, g + 1)
                                sp.dma_start(attr[:, k, :, :], by_tile[:, bass.ds(g * G, G), :]
                                             ).then_inc(attr_in[k], 16)
                        sp.wait_ge(msg_in, GROUPS)
                        sp.dma_start(attr[0:TAIL_EDGES, 0, LAST_TILES - 1, :],
                                     ins["edge_attr_64"][FULL_TILES * P:EDGES, :]).then_inc(tail_in, 16)
                        sp.wait_ge(tail_in, 16)
                        sp.dma_start(attr[:, 0, 0:LAST_TILES - 1, :], by_tile[:, (GROUPS - 1) * G:FULL_TILES, :]
                                     ).then_inc(attr_in[0], 16)

                    @block.scalar
                    def _(act):
                        act.sem_inc(msg_in, U)

                        def relu_group(g, k):
                            act.wait_ge(summed, g + 1)
                            act.wait_ge(mm_done, g + 1)
                            nc.scalar.activation(msg[:, k, :, 0:D], attr[:, k, :, :], ACT.Relu).then_inc(relu_in, 1)
                            act.wait_ge(relu_in, g + 1)
                            nc.scalar.copy(msg[:, k, :, D + 1:D + 2],
                                           weight[:, bass.ds(g * G, G)].unsqueeze(2)).then_inc(msg_in, 1)

                        with act.Fori(0, ROUNDS) as r:
                            for k in range(U):
                                relu_group(r * U + k, k)
                        relu_group(GROUPS - 1, 0)

                @block.tensor
                def _(pe):
                    pe.sem_inc(mm_done, 3)

                    def products(g, k, r, tiles):
                        if with_attr:
                            pe.wait_ge(msg_in, g + 1 + U)
                        else:
                            pe.wait_ge(gathered[k], (r + 1) * 16 * G)
                        pe.wait_ge(onehot_in, g + 1)
                        pe.wait_ge(agg_free, g + 1)
                        for j in range(tiles):
                            mm = pe.matmul(window_sums(k)[:, j * P:(j + 1) * P], lhsT=lhs[:, k, j, 0:out_rows],
                                           rhs=onehot[:, k, j, :], start=True, stop=True)
                        mm.then_inc(mm_done, 1)

                    with pe.Fori(0, ROUNDS) as r:
                        for k in range(U):
                            products(r * U + k, k, r, G)
                    products(GROUPS - 1, 0, ROUNDS, LAST_TILES)

                @block.vector
                def _(dve):
                    dve.sem_inc(agg_free, 2)

                    def prepare(g, k, r):
                        if with_attr:
                            dve.wait_ge(gathered[k], (r + 1) * 16 * G)
                            dve.wait_ge(attr_in[k], (r + 1) * 16)
                            dve.tensor_tensor(attr[:, k, :, :], attr[:, k, :, :], rows_g[:, k, :, 0:D],
                                              ALU.add).then_inc(summed, 1)
                        dve.wait_ge(mm_done, g + 1)
                        hot_k = onehot[:, k, :, :]
                        eq = dve.tensor_tensor(hot_k, iota[:, :].unsqueeze(1).broadcast_to([P, G, P]),
                                               dst_rel[:, bass.ds(g * G, G)].unsqueeze(2).broadcast_to([P, G, P]),
                                               ALU.is_equal)
                        if weighted:
                            eq.then_inc(hot, 1)
                            dve.wait_ge(hot, g + 1)
                            dve.tensor_tensor(hot_k, hot_k,
                                              weight[:, bass.ds(g * G, G)].unsqueeze(2).broadcast_to([P, G, P]),
                                              ALU.mult).then_inc(onehot_in, 1)
                        else:
                            eq.then_inc(onehot_in, 1)

                    def accumulate(g, k, tiles):
                        _, bases = nc.values_load_multi_w_load_instructions(
                            first_dst[0:1, bass.ds(g * G, tiles)], engines=DVE_ONLY, min_val=0,
                            max_val=NODES - 1, skip_runtime_bounds_check_because=IN_RANGE)
                        dve.wait_ge(mm_done, g + 4)
                        for j in range(tiles):
                            window = agg[0:out_rows, bass.ds(bases[j], P)]
                            add = dve.tensor_tensor(window, window, window_sums(k)[:, j * P:(j + 1) * P], ALU.add)
                            if j < tiles - 1:
                                add.then_inc(added, 1)
                                dve.wait_ge(added, g * (G - 1) + (j + 1))
                        add.then_inc(agg_free, 1)
                        dve.wait_ge(agg_free, g + 3)

                    prepare(0, 0, 0)
                    with dve.Fori(0, ROUNDS) as r:
                        for k in range(U):
                            g = r * U + k
                            k1 = (k + 1) % U
                            prepare(g + 1, k1, r + (k + 1) // U)
                            accumulate(g, k, G)
                    accumulate(GROUPS - 1, 0, LAST_TILES)

        def attention_pass(name, source):
            gathered = [sem(f"{name}_gathered{k}") for k in range(U)]
            staged, mm_done, hot, agg_free, added = (
                sem(f"{name}_staged"), sem(f"{name}_mm_done"), sem(f"{name}_hot"),
                sem(f"{name}_agg_free"), sem(f"{name}_added"))
            t_done, src_t_in, s_done, clipped, exped, probs_in = (
                sem(f"{name}_t_done"), sem(f"{name}_src_t_in"), sem(f"{name}_s_done"), sem(f"{name}_clipped"),
                sem(f"{name}_exped"), sem(f"{name}_probs_in"))
            ps_t = ps[:, 0:G * P]
            ps_s = ps[:, G * P:2 * G * P]
            ps_o = ps[0:D + 1, 2 * G * P:3 * G * P]

            with nc.Block() as block:
                @block.gpsimd
                def _(pool):
                    def stage(g, k):
                        pool.tensor_copy(idx[k][:, :], src_idx[:, bass.ds(g * G, G)]).then_inc(staged, 1)

                    def gather(g, k):
                        for j in range(G):
                            pool.indirect_dma_start(rows_g[:, k, j, 0:2 * D], None, source,
                                                    bass.IndirectOffsetOnAxis(ap=idx[k][:, j:j + 1], axis=0)
                                                    ).then_inc(gathered[k], 16)

                    stage(0, 0)
                    with pool.Fori(0, ROUNDS) as r:
                        for k in range(U):
                            g = r * U + k
                            pool.wait_ge(mm_done, g + 1)
                            pool.wait_ge(staged, g + 1)
                            stage(g + 1, (k + 1) % U)
                            gather(g, k)
                    pool.wait_ge(mm_done, GROUPS)
                    pool.wait_ge(staged, GROUPS)
                    gather(GROUPS - 1, 0)

                @block.tensor
                def _(pe):
                    pe.sem_inc(mm_done, 3)

                    def turn(g, k, r):
                        pe.wait_ge(gathered[k], (r + 1) * 16 * G)
                        pe.wait_ge(src_t_in, g + 1)
                        for j in range(G):
                            t = pe.transpose(ps_t[:, j * P:(j + 1) * P], rows_g[:, k, j, 0:P], ident[:, :])
                        t.then_inc(t_done, 1)

                    def score(g):
                        _, bases = nc.values_load_multi_w_load_instructions(
                            first_dst[0:1, bass.ds(g * G, G)], engines=PE_ONLY, min_val=0,
                            max_val=NODES - 1, skip_runtime_bounds_check_because=IN_RANGE)
                        pe.wait_ge(src_t_in, g + 2)
                        pe.wait_ge(clipped, g + 1)
                        for j in range(G):
                            mm = pe.matmul(ps_s[:, j * P:(j + 1) * P], lhsT=src_t[:, j, :],
                                           rhs=qk_t[:, bass.ds(bases[j], P)], start=True, stop=True)
                        mm.then_inc(s_done, 1)

                    def products(g, k, tiles):
                        pe.wait_ge(probs_in, g + 1)
                        pe.wait_ge(agg_free, g + 1)
                        for j in range(tiles):
                            mm = pe.matmul(ps_o[:, j * P:(j + 1) * P], lhsT=rows_g[:, k, j, D:2 * D + 1],
                                           rhs=probs[:, j, :], start=True, stop=True)
                        mm.then_inc(mm_done, 1)

                    turn(0, 0, 0)
                    score(0)
                    with pe.Fori(0, ROUNDS) as r:
                        for k in range(U):
                            g = r * U + k
                            turn(g + 1, (k + 1) % U, r + (k + 1) // U)
                            score(g + 1)
                            products(g, k, G)
                    products(GROUPS - 1, 0, LAST_TILES)

                @block.scalar
                def _(act):
                    act.sem_inc(src_t_in, 1)

                    def group(g):
                        act.wait_ge(t_done, g + 1)
                        act.wait_ge(s_done, g + 1)
                        nc.scalar.copy(src_t[:, :, :], ps_t[0:D, :].rearrange("p (j e) -> p j e", e=P)).then_inc(src_t_in, 1)
                        act.wait_ge(clipped, g + 2)
                        nc.scalar.activation(scores[:, :, :], scores[:, :, :], ACT.Exp, scale=1.0 / 8.0
                                             ).then_inc(exped, 1)

                    group(0)
                    with act.Fori(1, GROUPS) as g:
                        group(g)

                @block.vector
                def _(dve):
                    dve.sem_inc(agg_free, 1)
                    dve.sem_inc(clipped, 1)
                    dve.sem_inc(s_done, 1)

                    def clip(g, k):
                        dve.tensor_tensor(onehot[:, k, :, :], iota[:, :].unsqueeze(1).broadcast_to([P, G, P]),
                                          dst_rel[:, bass.ds(g * G, G)].unsqueeze(2).broadcast_to([P, G, P]),
                                          ALU.is_equal).then_inc(hot, 1)
                        dve.wait_ge(s_done, g + 2)
                        dve.tensor_scalar(scores[:, :, :], ps_s.rearrange("p (j e) -> p j e", e=P), 40.0, -40.0,
                                          ALU.min, ALU.max).then_inc(clipped, 1)

                    def pick(g, k):
                        dve.wait_ge(exped, g + 1)
                        dve.wait_ge(hot, g + 1)
                        dve.tensor_tensor(probs[:, :, :], scores[:, :, :], onehot[:, k, :, :], ALU.mult
                                          ).then_inc(probs_in, 1)

                    def accumulate(g, tiles):
                        _, bases = nc.values_load_multi_w_load_instructions(
                            first_dst[0:1, bass.ds(g * G, tiles)], engines=DVE_ONLY, min_val=0,
                            max_val=NODES - 1, skip_runtime_bounds_check_because=IN_RANGE)
                        dve.wait_ge(mm_done, g + 4)
                        for j in range(tiles):
                            window = agg[0:D + 1, bass.ds(bases[j], P)]
                            add = dve.tensor_tensor(window, window, ps_o[:, j * P:(j + 1) * P], ALU.add)
                            if j < tiles - 1:
                                add.then_inc(added, 1)
                                dve.wait_ge(added, g * (G - 1) + (j + 1))
                        add.then_inc(agg_free, 1)
                        dve.wait_ge(agg_free, g + 2)

                    clip(0, 0)
                    pick(0, 0)
                    with dve.Fori(0, ROUNDS) as r:
                        for k in range(U):
                            g = r * U + k
                            dve.wait_ge(probs_in, g + 1)
                            clip(g + 1, (k + 1) % U)
                            accumulate(g, G)
                            pick(g + 1, (k + 1) % U)
                    accumulate(GROUPS - 1, LAST_TILES)

        def layer_norm(dve, link, into, of, sqrt_in, sqrt_out, n, eps=LN_EPS):
            mean, var, rstd = stat[:, 1, :], stat[:, 2, :], stat[:, 3, :]
            link(dve.tensor_reduce(mean, of[:, :, :], AX_X, ALU.add))
            link(dve.tensor_scalar(mean, mean, 1.0 / D, None, ALU.mult))
            link(dve.tensor_tensor(of[:, :, :], of[:, :, :], over_features(mean), ALU.subtract))
            link(dve.tensor_tensor(y3[:, :, :], of[:, :, :], of[:, :, :], ALU.mult))
            link(dve.tensor_reduce(var, y3[:, :, :], AX_X, ALU.add))
            dve.tensor_scalar(var, var, 1.0 / D, eps, ALU.mult, ALU.add).then_inc(sqrt_in, 1)
            dve.wait_ge(sqrt_out, n + 1)
            link(dve.reciprocal(rstd, stat[:, 4, :]))
            link(dve.tensor_tensor(into[:, :, :], of[:, :, :], over_features(rstd), ALU.mult))

        def take_roots(act, sqrt_in, sqrt_out, count):
            for n in range(count):
                act.wait_ge(sqrt_in, n + 1)
                nc.scalar.activation(stat[:, 4, :], stat[:, 2, :], ACT.Sqrt).then_inc(sqrt_out, 1)

        def chained(dve, name):
            done, count = sem(f"{name}_chain"), [0]

            def link(instruction):
                count[0] += 1
                instruction.then_inc(done, 1)
                dve.wait_ge(done, count[0])
            return link

        transpose_nodes("x0")
        edge_pass("p0", ins["x"], D, with_attr=True)

        h_in, mm0, sq_in, sq_out, deg_in, deg_out = (sem("h_in"), sem("mm0"), sem("n0_sq_in"), sem("n0_sq_out"),
                                                     sem("deg_in"), sem("deg_out"))
        PS_DEG = 4 * BANK
        with nc.Block() as block:
            @block.vector
            def _(dve):
                link = chained(dve, "n0")
                dve.scalar_tensor_tensor(h_t[0:D, :], x_t[0:D, :], eps0_p1[0:D, 0:1], agg[0:D, 0:NPAD],
                                         ALU.mult, ALU.add).then_inc(h_in, 1)
                dve.wait_ge(mm0, 1)
                link(dve.tensor_copy(degs[:, :, :],
                                     ps[:, PS_DEG:PS_DEG + 2 * CHUNKS].rearrange("p (c k) -> p c k", k=2)))
                edges_n, weights_n = stat[:, 5, :], stat[:, 6, :]
                link(dve.tensor_scalar(edges_n, degs[:, :, 0], 1.0, None, ALU.max))
                dve.tensor_scalar(weights_n, degs[:, :, 1], 1.0, None, ALU.max).then_inc(deg_in, 1)
                link(dve.reciprocal(rdeg[:, :], edges_n))
                dve.wait_ge(deg_out, 2)
                link(dve.reciprocal(norm3[:, :], stat[:, 7, :]))
                link(dve.reciprocal(norm2[:, :], stat[:, 8, :]))
                dve.wait_ge(mm0, 2)
                link(dve.tensor_scalar(y[:, :, :], ps[:, 0:CHUNKS * D].rearrange("p (c d) -> p c d", d=D), 0.0,
                                       None, ALU.max))
                link(dve.tensor_tensor(y[:, :, :], y[:, :, :], x[:, :, :], ALU.add))
                layer_norm(dve, link, x, y, sq_in, sq_out, 0)
                link(dve.memset(agg[:, :], 0.0))

            @block.scalar
            def _(act):
                act.wait_ge(deg_in, 1)
                nc.scalar.activation(stat[:, 7, :], stat[:, 5, :], ACT.Sqrt).then_inc(deg_out, 1)
                nc.scalar.activation(stat[:, 8, :], stat[:, 6, :], ACT.Sqrt).then_inc(deg_out, 1)
                take_roots(act, sq_in, sq_out, 1)

            @block.tensor
            def _(pe):
                for c in range(CHUNKS):
                    t = pe.transpose(ps[:, PS_DEG + 2 * c:PS_DEG + 2 * c + 2], agg[D:D + 2, c * P:(c + 1) * P],
                                     ident[D:D + 2, D:D + 2])
                t.then_inc(mm0, 1)
                pe.wait_ge(h_in, 1)
                for c in range(CHUNKS):
                    t = pe.matmul(ps[:, c * D:(c + 1) * D], lhsT=h_t[:, c * P:(c + 1) * P], rhs=w_t[:, W_L0, :],
                                  start=True, stop=True)
                t.then_inc(mm0, 1)

        def to_table(name, slot, relu_norm, dram):
            lin, lin_in, written = sem(f"{name}_lin"), sem(f"{name}_lin_in"), sem(f"{name}_written")
            banks = -(-CHUNKS // PER_BANK)
            with nc.Block() as block:
                @block.tensor
                def _(pe):
                    for c in range(CHUNKS):
                        t = pe.matmul(ps[:, c * P:(c + 1) * P], lhsT=x_t[:, c * P:(c + 1) * P],
                                      rhs=w_t[:, slot:slot + 2, :], start=True, stop=True)
                        if c % PER_BANK == PER_BANK - 1 or c == CHUNKS - 1:
                            t.then_inc(lin, 1)

                @block.vector
                def _(dve):
                    link = chained(dve, name)
                    for b in range(banks):
                        c0, c1 = b * PER_BANK, min((b + 1) * PER_BANK, CHUNKS)
                        view = ps[:, c0 * P:c1 * P].rearrange("p (c d) -> p c d", d=P)
                        dve.wait_ge(lin, b + 1)
                        if relu_norm:
                            link(dve.tensor_scalar(table[:, c0:c1, :], view, 0.0, None, ALU.max))
                            dve.tensor_tensor(table[:, c0:c1, :], table[:, c0:c1, :],
                                              norm3[:, c0:c1].unsqueeze(2).broadcast_to([P, c1 - c0, P]),
                                              ALU.mult).then_inc(lin_in, 1)
                        else:
                            dve.tensor_copy(table[:, c0:c1, :], view).then_inc(lin_in, 1)

                @block.sync
                def _(sp):
                    sp.wait_ge(lin_in, banks)
                    sp.dma_start(dram.rearrange("(c p) d -> p c d", p=P), table[:, :, :]).then_inc(written, 16)
                    sp.wait_ge(written, 16)

        transpose_nodes("x1")
        to_table("qkv", W_QK, False, qkv_table)
        qt_done, qt_in = sem("qt_done"), sem("qt_in")
        with nc.Block() as block:
            @block.tensor
            def _(pe):
                for b in range(-(-NPAD // BANK)):
                    end = min((b + 1) * BANK, NPAD)
                    pe.matmul(ps[0:D, b * BANK:end], lhsT=w_t[:, W_QK, :], rhs=x_t[:, b * BANK:end],
                              start=True, stop=True).then_inc(qt_done, 1)

            @block.scalar
            def _(act):
                for b in range(-(-NPAD // BANK)):
                    end = min((b + 1) * BANK, NPAD)
                    act.wait_ge(qt_done, b + 1)
                    nc.scalar.copy(qk_t[:, b * BANK:end], ps[0:D, b * BANK:end]).then_inc(qt_in, 1)
                act.wait_ge(qt_in, -(-NPAD // BANK))

        attention_pass("p1", qkv_table)

        mm1, sq1_in, sq1_out, num_in, h0_in, h0_written = (sem("mm1"), sem("n1_sq_in"), sem("n1_sq_out"),
                                                           sem("num_in"), sem("h0_in"), sem("h0_written"))
        with nc.Block() as block:
            @block.tensor
            def _(pe):
                for c in range(CHUNKS):
                    t = pe.matmul(ps[:, c * P:c * P + D + 1], lhsT=agg[0:D + 1, c * P:(c + 1) * P], rhs=o_t[:, :],
                                  start=True, stop=True)
                t.then_inc(mm1, 1)

            @block.vector
            def _(dve):
                link = chained(dve, "n1")
                view = ps[:, 0:NPAD].rearrange("p (c d) -> p c d", d=P)
                den = stat[:, 5, :]
                dve.wait_ge(mm1, 1)
                link(dve.tensor_scalar(den, view[:, :, D], 1e-3, None, ALU.max))
                link(dve.reciprocal(den, den))
                link(dve.tensor_tensor(y[:, :, :], view[:, :, 0:D], over_features(den), ALU.mult))
                link(dve.tensor_tensor(y[:, :, :], y[:, :, :], over_chunks(rows[:, R_OB, :]), ALU.add))
                link(dve.tensor_tensor(y[:, :, :], y[:, :, :], x[:, :, :], ALU.add))
                layer_norm(dve, link, y, y, sq1_in, sq1_out, 0)
                link(dve.tensor_tensor(y[:, :, :], y[:, :, :], over_chunks(rows[:, R_LNG, :]), ALU.mult))
                link(dve.tensor_tensor(y[:, :, :], y[:, :, :], over_chunks(rows[:, R_LNB, :]), ALU.add))
                link(dve.tensor_tensor(y[:, :, :], y[:, :, :], x[:, :, :], ALU.add))
                layer_norm(dve, link, x, y, sq1_in, sq1_out, 1)
                dve.tensor_tensor(y2[:, :, :], x[:, :, :], over_features(norm2[:, :]), ALU.mult).then_inc(h0_in, 1)
                link(dve.memset(agg[:, :], 0.0))

            @block.scalar
            def _(act):
                take_roots(act, sq1_in, sq1_out, 2)

            @block.sync
            def _(sp):
                sp.wait_ge(h0_in, 1)
                sp.dma_start(h0_table.rearrange("(c p) d -> p c d", p=P), y2[:, :, :]).then_inc(h0_written, 16)
                sp.wait_ge(h0_written, 16)

        def agg_by_node(pe, done, features):
            for c in range(CHUNKS):
                t = pe.transpose(ps[:, c * P:c * P + features], agg[0:features, c * P:(c + 1) * P],
                                 ident[0:features, 0:features])
            t.then_inc(done, 1)

        edge_pass("p2", h0_table, D, weighted=True)
        turned2, h1_in, h1_written = sem("turned2"), sem("h1_in"), sem("h1_written")
        with nc.Block() as block:
            @block.tensor
            def _(pe):
                agg_by_node(pe, turned2, D)

            @block.vector
            def _(dve):
                link = chained(dve, "n2")
                dve.wait_ge(turned2, 1)
                view = ps[:, 0:NPAD].rearrange("p (c d) -> p c d", d=P)[:, :, 0:D]
                link(dve.tensor_tensor(y[:, :, :], view, over_features(norm2[:, :]), ALU.mult))
                dve.tensor_tensor(y2[:, :, :], y[:, :, :], over_features(norm2[:, :]), ALU.mult).then_inc(h1_in, 1)
                link(dve.tensor_tensor(low[:, 0, :, :], x[:, :, :], y[:, :, :], ALU.add))
                link(dve.memset(agg[:, :], 0.0))

            @block.sync
            def _(sp):
                sp.wait_ge(h1_in, 1)
                sp.dma_start(h1_table.rearrange("(c p) d -> p c d", p=P), y2[:, :, :]).then_inc(h1_written, 16)
                sp.wait_ge(h1_written, 16)

        edge_pass("p3", h1_table, D, weighted=True)
        turned3, sq3_in, sq3_out = sem("turned3"), sem("n3_sq_in"), sem("n3_sq_out")
        with nc.Block() as block:
            @block.tensor
            def _(pe):
                agg_by_node(pe, turned3, D)

            @block.vector
            def _(dve):
                link = chained(dve, "n3")
                dve.wait_ge(turned3, 1)
                view = ps[:, 0:NPAD].rearrange("p (c d) -> p c d", d=P)[:, :, 0:D]
                link(dve.tensor_tensor(y[:, :, :], view, over_features(norm2[:, :]), ALU.mult))
                link(dve.tensor_tensor(y[:, :, :], y[:, :, :], low[:, 0, :, :], ALU.add))
                link(dve.scalar_tensor_tensor(y[:, :, :], y[:, :, :], 1.0 / 3.0, x[:, :, :], ALU.mult, ALU.add))
                layer_norm(dve, link, x, y, sq3_in, sq3_out, 0)
                link(dve.memset(agg[:, :], 0.0))

            @block.scalar
            def _(act):
                take_roots(act, sq3_in, sq3_out, 1)

        transpose_nodes("x3")
        to_table("neigh", W_NEIGH, True, neigh_table)
        own, own_in = sem("own"), sem("own_in")
        with nc.Block() as block:
            @block.tensor
            def _(pe):
                for n in range(3):
                    if n:
                        pe.wait_ge(own_in, n)
                    for c in range(CHUNKS):
                        t = pe.matmul(ps[:, c * D:(c + 1) * D], lhsT=x_t[:, c * P:(c + 1) * P],
                                      rhs=w_t[:, W_SELF + n, :], start=True, stop=True)
                    t.then_inc(own, 1)

            @block.scalar
            def _(act):
                for n in range(3):
                    act.wait_ge(own, n + 1)
                    nc.scalar.activation(low[:, n, :, :], ps[:, 0:CHUNKS * D].rearrange("p (c d) -> p c d", d=D),
                                         ACT.Relu).then_inc(own_in, 1)
                act.wait_ge(own_in, 3)

        edge_pass("p4", neigh_table, 2 * D)
        turned4, sq4_in, sq4_out, logits_in, sig_in, shifted, expd, out_in, written = (
            sem("turned4"), sem("n4_sq_in"), sem("n4_sq_out"), sem("logits_in"), sem("sig_in"), sem("shifted"),
            sem("expd"), sem("out_in"), sem("out_written"))
        with nc.Block() as block:
            @block.tensor
            def _(pe):
                agg_by_node(pe, turned4, 2 * D)

            @block.vector
            def _(dve):
                link = chained(dve, "n4")
                dve.wait_ge(turned4, 1)
                view = ps[:, 0:NPAD].rearrange("p (c d) -> p c d", d=P)
                for n, op in enumerate((ALU.add, ALU.subtract)):
                    link(dve.tensor_tensor(y[:, :, :], view[:, :, n * D:(n + 1) * D], over_features(rdeg[:, :]),
                                           ALU.mult))
                    link(dve.tensor_tensor(low[:, n, :, :], low[:, n, :, :], y[:, :, :], op))
                for n in range(3):
                    link(dve.tensor_tensor(y[:, :, :], low[:, n, :, :], over_chunks(rows[:, R_ATT + n, :]), ALU.mult))
                    red = dve.tensor_reduce(att[:, n, :], y[:, :, :], AX_X, ALU.add)
                    if n < 2:
                        link(red)
                red.then_inc(logits_in, 1)
                dve.wait_ge(sig_in, 1)
                for k in range(3):
                    link(dve.tensor_scalar(att[:, k, :], sig[:, 0, :], w_att[:, 3 * k:3 * k + 1], None, ALU.mult))
                    for j in range(1, 3):
                        link(dve.scalar_tensor_tensor(att[:, k, :], sig[:, j, :], w_att[:, 3 * k + j:3 * k + j + 1],
                                                      att[:, k, :], ALU.mult, ALU.add))
                top, total = stat[:, 5, :], stat[:, 6, :]
                link(dve.tensor_tensor(top, att[:, 0, :], att[:, 1, :], ALU.max))
                link(dve.tensor_tensor(top, top, att[:, 2, :], ALU.max))
                dve.tensor_tensor(att[:, :, :], att[:, :, :], top.unsqueeze(1).broadcast_to([P, 3, CHUNKS]),
                                  ALU.subtract).then_inc(shifted, 1)
                dve.wait_ge(expd, 1)
                link(dve.tensor_tensor(total, att[:, 0, :], att[:, 1, :], ALU.add))
                link(dve.tensor_tensor(total, total, att[:, 2, :], ALU.add))
                link(dve.reciprocal(total, total))
                link(dve.tensor_tensor(att[:, :, :], att[:, :, :], total.unsqueeze(1).broadcast_to([P, 3, CHUNKS]),
                                       ALU.mult))
                link(dve.tensor_tensor(y[:, :, :], low[:, 0, :, :], over_features(att[:, 0, :]), ALU.mult))
                for n in range(1, 3):
                    link(dve.tensor_tensor(y2[:, :, :], low[:, n, :, :], over_features(att[:, n, :]), ALU.mult))
                    link(dve.tensor_tensor(y[:, :, :], y[:, :, :], y2[:, :, :], ALU.add))
                link(dve.scalar_tensor_tensor(y[:, :, :], y[:, :, :], 3.0, x[:, :, :], ALU.mult, ALU.add))
                layer_norm(dve, link, x, y, sq4_in, sq4_out, 0)
                dve.sem_inc(out_in, 1)

            @block.scalar
            def _(act):
                act.wait_ge(logits_in, 1)
                nc.scalar.activation(sig[:, :, :], att[:, :, :], ACT.Sigmoid).then_inc(sig_in, 1)
                act.wait_ge(shifted, 1)
                nc.scalar.activation(att[:, :, :], att[:, :, :], ACT.Exp, scale=1.0 / 3.0).then_inc(expd, 1)
                take_roots(act, sq4_in, sq4_out, 1)

            @block.sync
            def _(sp):
                sp.wait_ge(out_in, 1)
                full, last = node_rows(out)
                sp.dma_start(full, x[:, 0:CHUNKS - 1, :]).then_inc(written, 16)
                sp.dma_start(last, x[0:LAST_NODES, CHUNKS - 1, :]).then_inc(written, 16)
                sp.wait_ge(written, 32)


_INS = (["x", "src", "dst", "edge_attr_64", "edge_weight", "L0_gnn_eps", "L3_gnn_W_att"] + ROWS
        + [w for w, _ in LINEAR] + [b for _, b in LINEAR if b])
_FLAT = set(ROWS) | {"L0_gnn_eps", "L3_gnn_W_att"}


def kernel(**inputs):
    import numpy as _np
    import concourse.bacc as _bacc
    from concourse import mybir as _mybir
    from concourse.bass_utils import run_bass_kernel_spmd as _run

    nc = _bacc.Bacc("TRN2", target_bir_lowering=False, num_devices=1)
    arrays, args = {}, {}
    for name in _INS:
        a = _np.ascontiguousarray(inputs[name])
        if name in _FLAT:
            a = a.reshape(-1)
        arrays[f"in_{name}"] = a
        args[name] = nc.dram_tensor(f"in_{name}", a.shape, _mybir.dt.from_np(a.dtype), kind="ExternalInput").ap()
    out = nc.dram_tensor("out_0", (NODES, D), _mybir.dt.float32, kind="ExternalOutput").ap()
    gnn_program(nc, args, out)
    r = _run(nc, [arrays], core_ids=[0])
    return r.results[0]["out_0"]
```

```python
from contextlib import ExitStack

import concourse.bass as bass
from concourse import mybir

P = 128
D = 64
NODES = 3125
EDGES = 103125
CHUNKS = -(-NODES // P)
NPAD = CHUNKS * P
LAST_NODES = NODES - (CHUNKS - 1) * P
FULL_TILES = EDGES // P
TILES = -(-EDGES // P)
TAIL_EDGES = EDGES - FULL_TILES * P
G = 8
GROUPS = -(-TILES // G)
LAST_TILES = TILES - (GROUPS - 1) * G
U = 4
ROUNDS = (GROUPS - 1) // U
TBLK = -(-TILES // P)
LAST_BLK_TILES = FULL_TILES - (TBLK - 1) * P
TCOLS = TBLK * P
AGG = NPAD + P
BANK = 512
PER_BANK = BANK // P
assert GROUPS == ROUNDS * U + 1 and TCOLS >= (GROUPS + 1) * G

GB = 9
WD = 42
NG = -(-TILES // GB)
LAST_GB = TILES - (NG - 1) * GB
UB = 4
BROUNDS = (NG - 2) // UB
BT = 3
NB = GB // BT
LAST_BLOCKS = -(-LAST_GB // BT)
HALF = 12
CENTRE = NPAD // 2
MID = 2048.0
WB = 3
NWB = NG // WB
WBUF = 3
DB = 512
NDB = NPAD // DB
W_MAX = 32768.0
assert NG == BROUNDS * UB + 2 and NG % WB == 0 and NWB % WBUF == 0 and 3 * WD <= P

F32 = mybir.dt.float32
F16 = mybir.dt.float16
U8 = mybir.dt.uint8
I32 = mybir.dt.int32
ALU = mybir.AluOpType
ACT = mybir.ActivationFunctionType
AX_X = mybir.AxisListType.X
DVE_ONLY = (mybir.EngineType.DVE,)
POOL_ONLY = (mybir.EngineType.Pool,)
PE_ONLY = (mybir.EngineType.PE,)
LN_EPS = 1e-5
IN_RANGE = "a first destination is a node's number"

LINEAR = [("L0_gnn_W", "L0_gnn_b"), ("L1_gnn_qk_w", "L1_gnn_qk_b"), ("L1_gnn_v_w", "L1_gnn_v_b"),
          ("L3_gnn_W_neigh", "L3_gnn_b_neigh"), ("L3_gnn_W_neigh_high", "L3_gnn_b_neigh_high"),
          ("L3_gnn_W_self", "L3_gnn_b_self"), ("L3_gnn_W_self_high", "L3_gnn_b_self_high"),
          ("L3_gnn_W_id", "L3_gnn_b_id"), ("L1_gnn_o_w", None)]
W_L0, W_QK, W_V, W_NEIGH, W_SELF, W_ID, W_O = 0, 1, 2, 3, 5, 7, 8
ROWS = ["L1_gnn_o_b", "L1_gnn_ln_g", "L1_gnn_ln_b", "L3_gnn_w_att_low", "L3_gnn_w_att_high",
        "L3_gnn_w_att_mlp"]
R_OB, R_LNG, R_LNB, R_ATT = 0, 1, 2, 3


def slot(k, b):
    return (k * NB + b) % 2 * BT


def gnn_program(nc, ins, out):
    with ExitStack() as ctx:
        def sb(name, shape, dt=F32):
            return ctx.enter_context(nc.sbuf_tensor(name, shape, dt))

        def sem(name):
            return ctx.enter_context(nc.semaphore(name))

        qkv_table = nc.dram_tensor("qkv_table", [NPAD, 2 * D], F32, kind="Internal").ap()
        h0_table = nc.dram_tensor("h0_table", [NPAD, D], F32, kind="Internal").ap()
        h1_table = nc.dram_tensor("h1_table", [NPAD, D], F32, kind="Internal").ap()
        neigh_table = nc.dram_tensor("neigh_table", [NPAD, 2 * D], F32, kind="Internal").ap()

        weights_d = nc.dram_tensor("weight_matrix", [NG, P, CHUNKS * WD], F32, kind="Internal").ap()

        ident = sb("ident", [P, P])
        ones = sb("ones", [1, P])
        iota_i = sb("iota_i", [P, P], I32)
        iota = sb("iota", [P, P])
        src_idx = sb("src_idx", [P, TCOLS], I32)
        dst_rel = sb("dst_rel", [P, TCOLS])
        weight = sb("weight", [P, TCOLS])
        first_dst = sb("first_dst", [1, GROUPS * G + 4], I32)
        group_dst = sb("group_dst", [1, NG + 2], I32)
        flag = sb("flag", [1, 1], I32)
        w_t = sb("w_t", [D + 1, 8, D])
        o_t = sb("o_t", [D + 1, D + 1])
        rows = sb("rows", [P, len(ROWS), D])
        w_att = sb("w_att", [P, 9])
        eps0 = sb("eps0", [P, 1])
        eps0_p1 = sb("eps0_p1", [P, 1])
        x = sb("x", [P, CHUNKS, D])
        stat = sb("stat", [P, 9, CHUNKS])
        att = sb("att", [P, 3, CHUNKS])
        sig = sb("sig", [P, 3, CHUNKS])
        degs = sb("degs", [P, CHUNKS, 2])
        norm2 = sb("norm2", [P, CHUNKS])
        norm3 = sb("norm3", [P, CHUNKS])
        rdeg = sb("rdeg", [P, CHUNKS])
        agg = sb("agg", [P, AGG])
        arena = sb("arena", [P, CHUNKS * NPAD // 4])
        adj = arena[:, :].bitcast(U8).rearrange("p (c n) -> p c n", n=NPAD)
        taken = [0]

        def ring(*shape):
            n = 1
            for d in shape:
                n *= d
            names = "abcd"[:len(shape)]
            view = arena[:, taken[0]:taken[0] + n].rearrange(
                f"p ({' '.join(names)}) -> p {' '.join(names)}", **dict(zip(names, shape)))
            taken[0] += n
            return view

        idx = [sb(f"idx{k}", [P, max(G, GB)], I32) for k in range(U)]
        rows_g = ring(U, G, 2 * D + 1)
        attr = ring(U, G, D)
        msg = ring(U, G, D + 2)
        onehot = ring(U, G, P)
        src_t = ring(G, P)[0:D, :, :]
        scores = ring(G, P)
        probs = ring(G, P)

        ps = ctx.enter_context(nc.psum_tensor("ps", [P, 8 * BANK], F32))

        src_d, dst_d, w_d = ins["src"], ins["dst"], ins["edge_weight"]

        def edge_blocks(a):
            full = (TBLK - 1) * P * P
            return (a[0:full].rearrange("(b r e) -> r b e", r=P, e=P),
                    a[full:FULL_TILES * P].rearrange("(r e) -> r e", e=P),
                    a[FULL_TILES * P:EDGES].rearrange("(r e) -> r e", r=1))

        def node_rows(a):
            full = (CHUNKS - 1) * P
            return a[0:full, :].rearrange("(c p) d -> p c d", p=P), a[full:NODES, :]

        def over_features(a):
            return a.unsqueeze(2).broadcast_to([P, CHUNKS, D])

        def over_chunks(a):
            return a.unsqueeze(1).broadcast_to([P, CHUNKS, D])

        def chained(dve, name):
            done, count = sem(f"{name}_chain"), [0]

            def link(instruction):
                count[0] += 1
                instruction.then_inc(done, 1)
                dve.wait_ge(done, count[0])
            return link

        GENERAL, USUAL = 1, 0

        def when(eng, way):
            return eng.If(eng.value_load(flag[0:1, 0:1], min_val=0, max_val=1) == way)

        build = ExitStack()

        def build_sb(name, shape, dt=F32):
            return build.enter_context(nc.sbuf_tensor(name, shape, dt))

        src_c = build_sb("src_c", [P, TCOLS])
        dst_g = build_sb("dst_g", [P, NG * GB])
        w_hi = build_sb("w_hi", [P, TCOLS])
        w_mid = build_sb("w_mid", [P, TCOLS])
        iota_c = build_sb("iota_c", [P, NPAD], F16)

        ld_edges, ld_w, ld_x, ld_base = sem("ld_edges"), sem("ld_w"), sem("ld_x"), sem("ld_base")
        cleared, consts, made = sem("cleared"), sem("consts"), sem("made")
        numbers_in, edges_t, edges_in, w_done, base0 = (sem("numbers_in"), sem("edges_t"), sem("edges_in"),
                                                        sem("w_done"), sem("base0"))
        counted = sem("counted")
        with ExitStack() as setup:
            def setup_sb(name, shape, dt=F32):
                return setup.enter_context(nc.sbuf_tensor(name, shape, dt))

            stage_i = setup_sb("stage_i", [P, 2, TBLK, P], I32)
            stage_f = setup_sb("stage_f", [P, 4, TBLK, P])
            w_stage = setup_sb("w_stage", [D, len(LINEAR), D])
            firsts = setup_sb("firsts", [1, 2 * TILES])
            wmax = setup_sb("wmax", [P, 2])
            w16 = setup_sb("w16", [P, TCOLS], F16)
            block_first = setup_sb("block_first", [P, TBLK])
            checks = setup_sb("checks", [1, 8])
            stage_w = stage_f[:, 2, :, :]
            counts_i = agg[:, 0:NPAD].bitcast(I32)
            PS_EDGE = [0, 2 * BANK, 4 * BANK, 0]
            PS_GROUP, PS_WMAX = 2 * BANK, 4 * BANK
            PS_W = 6 * BANK
            with nc.Block() as block:
                @block.sync
                def _(sp):
                    sp.wait_ge(cleared, 3)
                    for a, stage in ((src_d, stage_i[:, 0, :, :]), (dst_d, stage_i[:, 1, :, :]), (w_d, stage_w)):
                        full, part, tail = edge_blocks(a)
                        sp.dma_start(stage[:, 0:TBLK - 1, :], full).then_inc(ld_edges, 16)
                        sp.dma_start(stage[0:LAST_BLK_TILES, TBLK - 1, :], part).then_inc(ld_edges, 16)
                        sp.dma_start(stage[LAST_BLK_TILES:LAST_BLK_TILES + 1, TBLK - 1, 0:TAIL_EDGES],
                                     tail).then_inc(ld_edges, 16)
                    for n, (w, b) in enumerate(LINEAR):
                        sp.dma_start(w_stage[:, n, :], ins[w]).then_inc(ld_w, 16)
                        if b:
                            sp.dma_start(w_t[D:D + 1, n, :], ins[b].rearrange("(a d) -> a d", a=1)).then_inc(ld_w, 16)
                    full, last = node_rows(ins["x"])
                    sp.wait_ge(cleared, 4)
                    sp.dma_start(x[:, 0:CHUNKS - 1, :], full).then_inc(ld_x, 16)
                    sp.dma_start(x[0:LAST_NODES, CHUNKS - 1, :], last).then_inc(ld_x, 16)
                    sp.wait_ge(ld_x, 32)

                @block.scalar
                def _(act):
                    act.wait_ge(base0, 1)
                    with nc.allow_non_contiguous_dma(reason="one element of each tile, once"):
                        act.dma_start(first_dst[0:1, 0:FULL_TILES],
                                      dst_d[0:FULL_TILES * P].rearrange("(t e) -> e t", e=P)[0:1, :]
                                      ).then_inc(ld_base, 16)
                        act.dma_start(group_dst[0:1, 0:NG - 1],
                                      dst_d[0:(NG - 1) * GB * P].rearrange("(g e) -> e g", e=GB * P)[0:1, :]
                                      ).then_inc(ld_base, 16)
                    for to, at in ((first_dst[0:1, FULL_TILES:FULL_TILES + 1], FULL_TILES * P),
                                   (group_dst[0:1, NG - 1:NG], (NG - 1) * GB * P),
                                   (group_dst[0:1, NG:NG + 1], EDGES - 1)):
                        act.dma_start(to, dst_d[at:at + 1].rearrange("(a e) -> a e", a=1)).then_inc(ld_base, 16)
                    for n, name in enumerate(ROWS):
                        act.dma_start(rows[:, n, :], ins[name].partition_broadcast(P)).then_inc(ld_w, 16)
                    act.dma_start(w_att[:, :], ins["L3_gnn_W_att"].partition_broadcast(P)).then_inc(ld_w, 16)
                    act.dma_start(eps0[:, :], ins["L0_gnn_eps"].partition_broadcast(P)).then_inc(ld_w, 16)
                    act.wait_ge(ld_base, 5 * 16)

                LD_W = 16 * (2 * len(LINEAR) - 1 + len(ROWS) + 2)

                @block.gpsimd
                def _(pool):
                    pool.memset(ident[:, :], 0.0).then_inc(consts, 1)
                    pool.wait_ge(consts, 1)
                    pool.iota(iota_i[:, :], pattern=[[1, P]], base=0, channel_multiplier=0).then_inc(consts, 1)
                    pool.wait_ge(consts, 2)
                    pool.affine_select(out=ident[:, :], in_=ident[:, :], compare_op=ALU.not_equal, fill=1.0,
                                       base=0, pattern=[[-1, P]], channel_multiplier=1).then_inc(made, 1)
                    pool.wait_ge(made, 1)
                    pool.iota(counts_i, pattern=[[1, NPAD]], base=-CENTRE, channel_multiplier=0).then_inc(counted, 1)
                    pool.wait_ge(counted, 1)
                    pool.memset(o_t[:, :], 0.0).then_inc(consts, 1)
                    pool.wait_ge(consts, 3)
                    for n, (view, value) in enumerate(((ones[:, :], 1.0), (o_t[D:D + 1, D:D + 1], 1.0),
                                                       (arena[:, :], 0.0))):
                        pool.memset(view, value).then_inc(made, 1)
                        pool.wait_ge(made, n + 2)

                @block.vector
                def _(dve):
                    link = chained(dve, "setup")
                    dve.memset(first_dst[:, :], 0)
                    dve.memset(group_dst[:, :], 0).then_inc(base0, 1)
                    dve.memset(stage_i[:, :, TBLK - 1, :], -1).then_inc(cleared, 1)
                    dve.memset(stage_w[:, TBLK - 1, :], 0.0).then_inc(cleared, 1)
                    dve.memset(w_t[:, :, :], 0.0).then_inc(cleared, 1)
                    dve.memset(x[:, CHUNKS - 1, :], 0.0).then_inc(cleared, 1)
                    dve.wait_ge(ld_edges, 9 * 16)
                    dve.tensor_scalar(stage_f[:, 0, :, :], stage_i[:, 0, :, :], 0.0, None, ALU.max
                                      ).then_inc(numbers_in, 1)
                    dve.tensor_copy(stage_f[:, 1, :, :], stage_i[:, 1, :, :]).then_inc(numbers_in, 1)
                    dve.wait_ge(numbers_in, 2)
                    link(dve.tensor_copy(block_first[:, :], stage_f[:, 1, :, 0]))
                    for b in range(TBLK):
                        last = dve.tensor_scalar(stage_f[:, 3, b, :], stage_f[:, 1, b, :], block_first[:, b:b + 1],
                                                 None, ALU.subtract)
                    last.then_inc(numbers_in, 1)
                    dve.wait_ge(consts, 2)
                    dve.tensor_copy(iota[:, :], iota_i[:, :])
                    dve.wait_ge(counted, 1)
                    link(dve.tensor_copy(iota_c[:, :], counts_i))
                    link(dve.memset(agg[:, :], 0.0))
                    dve.wait_ge(edges_t, 1)
                    dve.tensor_copy(src_idx[:, :], ps[:, PS_EDGE[0]:PS_EDGE[0] + TCOLS])
                    dve.tensor_scalar(src_c[:, :], ps[:, PS_EDGE[0]:PS_EDGE[0] + TCOLS], float(CENTRE), None,
                                      ALU.subtract).then_inc(edges_in, 1)
                    dve.wait_ge(edges_t, 2)
                    dve.tensor_copy(dst_g[:, :], ps[:, PS_EDGE[1]:PS_EDGE[1] + NG * GB]).then_inc(edges_in, 1)
                    dve.wait_ge(edges_t, 3)
                    link(dve.tensor_copy(weight[:, :], ps[:, PS_EDGE[2]:PS_EDGE[2] + TCOLS]))
                    link(dve.tensor_copy(w16[:, :], weight[:, :]))
                    link(dve.tensor_copy(w_hi[:, :], w16[:, :]))
                    link(dve.tensor_tensor(w_mid[:, :], weight[:, :], w_hi[:, :], ALU.subtract))
                    link(dve.tensor_scalar(w_mid[:, :], w_mid[:, :], MID, None, ALU.mult))
                    link(dve.tensor_reduce(wmax[:, 0:1], weight[:, :], AX_X, ALU.max))
                    link(dve.tensor_reduce(wmax[:, 1:2], weight[:, :], AX_X, ALU.min))
                    link(dve.tensor_scalar(wmax[:, 1:2], wmax[:, 1:2], -1.0, None, ALU.mult))
                    dve.tensor_tensor(wmax[:, 0:1], wmax[:, 0:1], wmax[:, 1:2], ALU.max).then_inc(edges_in, 1)
                    dve.wait_ge(ld_base, 5 * 16)
                    numbers, groups = firsts[0:1, 0:TILES], firsts[0:1, TILES:TILES + NG + 1]
                    link(dve.tensor_copy(numbers, first_dst[0:1, 0:TILES]))
                    dve.tensor_copy(groups, group_dst[0:1, 0:NG + 1]).then_inc(numbers_in, 1)
                    steps = stage_i[0:1, 0, :, :].rearrange("p b e -> p (b e)").bitcast(F32)
                    link(dve.tensor_tensor(steps[0:1, 0:TILES - 1], numbers[0:1, 1:TILES], numbers[0:1, 0:TILES - 1],
                                           ALU.subtract))
                    link(dve.tensor_reduce(checks[0:1, 0:1], steps[0:1, 0:TILES - 1], AX_X, ALU.min))
                    link(dve.tensor_scalar(checks[0:1, 4:5], checks[0:1, 0:1], 1.0, None, ALU.is_lt))
                    dve.wait_ge(numbers_in, 4)
                    link(dve.tensor_tensor(steps[0:1, 0:NG], groups[0:1, 1:NG + 1], groups[0:1, 0:NG], ALU.subtract))
                    link(dve.tensor_reduce(checks[0:1, 1:2], steps[0:1, 0:NG], AX_X, ALU.max))
                    link(dve.tensor_scalar(checks[0:1, 5:6], checks[0:1, 1:2], float(WD - 1), None, ALU.is_gt))
                    dve.wait_ge(edges_t, 6)
                    link(dve.tensor_reduce(checks[0:1, 2:3], ps[0:1, PS_WMAX:PS_WMAX + P], AX_X, ALU.max))
                    link(dve.tensor_scalar(checks[0:1, 6:7], checks[0:1, 2:3], W_MAX, None, ALU.is_gt))
                    link(dve.tensor_reduce(checks[0:1, 3:4], checks[0:1, 4:7], AX_X, ALU.max))
                    link(dve.tensor_copy(flag[:, :], checks[0:1, 3:4]))
                    group_cols = ps[:, PS_GROUP:PS_GROUP + NG].unsqueeze(2).broadcast_to([P, NG, GB])
                    by_group = dst_g[:, :].rearrange("p (g j) -> p g j", j=GB)
                    link(dve.tensor_tensor(by_group, by_group, group_cols, ALU.subtract))
                    link(dve.tensor_copy(dst_rel[:, :], ps[:, PS_EDGE[3]:PS_EDGE[3] + TCOLS]))
                    dve.wait_ge(w_done, 1)
                    dve.wait_ge(made, 3)
                    dve.tensor_copy(w_t[0:D, :, :], ps[0:D, PS_W:PS_W + 8 * D].rearrange("p (n d) -> p n d", d=D))
                    dve.tensor_copy(o_t[0:D, 0:D], ps[0:D, PS_W + BANK:PS_W + BANK + D])
                    link(dve.tensor_scalar(eps0_p1[:, :], eps0[:, :], 1.0, None, ALU.add))

                @block.tensor
                def _(pe):
                    def turn(n):
                        for b in range(TBLK):
                            t = pe.transpose(ps[:, PS_EDGE[n] + b * P:PS_EDGE[n] + (b + 1) * P],
                                             stage_f[:, n, b, :], ident[:, :])
                        t.then_inc(edges_t, 1)

                    pe.wait_ge(made, 1)
                    pe.wait_ge(numbers_in, 2)
                    turn(0)
                    turn(1)
                    turn(2)
                    pe.wait_ge(ld_w, LD_W)
                    for n in range(len(LINEAR)):
                        t = pe.transpose(ps[0:D, PS_W + n * D:PS_W + (n + 1) * D], w_stage[:, n, :],
                                         ident[0:D, 0:D])
                    t.then_inc(w_done, 1)
                    pe.wait_ge(numbers_in, 3)
                    pe.wait_ge(edges_in, 1)
                    turn(3)
                    pe.wait_ge(numbers_in, 4)
                    pe.wait_ge(made, 2)
                    pe.wait_ge(edges_in, 2)
                    pe.matmul(ps[:, PS_GROUP:PS_GROUP + NG], lhsT=ones[0:1, :], rhs=firsts[0:1, TILES:TILES + NG],
                              start=True, stop=True).then_inc(edges_t, 1)
                    pe.wait_ge(edges_in, 3)
                    pe.transpose(ps[0:1, PS_WMAX:PS_WMAX + P], wmax[:, 0:1], ident[:, :]).then_inc(edges_t, 1)

        def transpose_nodes(name):
            t_done, t_copied = sem(f"{name}_t_done"), sem(f"{name}_t_copied")
            banks = -(-CHUNKS // PER_BANK)
            with nc.Block() as block:
                @block.tensor
                def _(pe):
                    for c in range(CHUNKS):
                        t = pe.transpose(ps[0:D, c * P:(c + 1) * P], x[:, c, :], ident[:, :])
                        if c % PER_BANK == PER_BANK - 1 or c == CHUNKS - 1:
                            t.then_inc(t_done, 1)

                @block.scalar
                def _(act):
                    for b in range(banks):
                        end = min((b + 1) * BANK, NPAD)
                        act.wait_ge(t_done, b + 1)
                        nc.scalar.copy(x_t[0:D, b * BANK:end], ps[0:D, b * BANK:end]).then_inc(t_copied, 1)
                    act.wait_ge(t_copied, banks)

        pass_sems = {}

        def pass_sem(name):
            if name not in pass_sems:
                pass_sems[name] = sem(name)
            return pass_sems[name]

        def clear_pass_sems():
            with nc.Block() as block:
                @block.sync
                def _(sp):
                    with when(sp, GENERAL):
                        for s in pass_sems.values():
                            sp.sem_clear(s)

        def edge_pass(name, source, width, with_attr=False, weighted=False):
            gathered = [pass_sem(f"general_gathered{k}") for k in range(U)]
            attr_in = [pass_sem(f"general_attr_in{k}") for k in range(U)]
            tail_in = pass_sem("general_tail_in")
            staged, mm_done, onehot_in, hot, agg_free, added = (
                pass_sem("general_staged"), pass_sem("general_mm_done"), pass_sem("general_onehot_in"), pass_sem("general_hot"),
                pass_sem("general_agg_free"), pass_sem("general_added"))
            summed, msg_in, relu_in = pass_sem("general_summed"), pass_sem("general_msg_in"), pass_sem("general_relu_in")
            out_rows = D + 2 if with_attr else width
            lhs = msg if with_attr else rows_g

            def window_sums(b):
                return ps[0:out_rows, (b % 2) * G * P:(b % 2 + 1) * G * P]

            with nc.Block() as block:
                @block.gpsimd
                def _(pool):
                    with when(pool, GENERAL):
                        def stage(g, k):
                            pool.tensor_copy(idx[k][:, 0:G], src_idx[:, bass.ds(g * G, G)]).then_inc(staged, 1)

                        def gather(g, k):
                            for j in range(G):
                                pool.indirect_dma_start(rows_g[:, k, j, 0:width], None, source,
                                                        bass.IndirectOffsetOnAxis(ap=idx[k][:, j:j + 1], axis=0)
                                                        ).then_inc(gathered[k], 16)

                        stage(0, 0)
                        with pool.Fori(0, ROUNDS) as r:
                            for k in range(U):
                                g = r * U + k
                                pool.wait_ge(mm_done, g + 1)
                                pool.wait_ge(staged, g + 1)
                                stage(g + 1, (k + 1) % U)
                                gather(g, k)
                        pool.wait_ge(mm_done, GROUPS)
                        pool.wait_ge(staged, GROUPS)
                        gather(GROUPS - 1, 0)

                if with_attr:
                    @block.sync
                    def _(sp):
                        with when(sp, GENERAL):
                            by_tile = ins["edge_attr_64"][0:FULL_TILES * P, :].rearrange("(t p) d -> p t d", p=P)
                            with sp.Fori(0, ROUNDS) as r:
                                for k in range(U):
                                    g = r * U + k
                                    sp.wait_ge(msg_in, g + 1)
                                    sp.dma_start(attr[:, k, :, :], by_tile[:, bass.ds(g * G, G), :]
                                                 ).then_inc(attr_in[k], 16)
                            sp.wait_ge(msg_in, GROUPS)
                            sp.dma_start(attr[0:TAIL_EDGES, 0, LAST_TILES - 1, :],
                                         ins["edge_attr_64"][FULL_TILES * P:EDGES, :]).then_inc(tail_in, 16)
                            sp.wait_ge(tail_in, 16)
                            sp.dma_start(attr[:, 0, 0:LAST_TILES - 1, :], by_tile[:, (GROUPS - 1) * G:FULL_TILES, :]
                                         ).then_inc(attr_in[0], 16)

                    @block.scalar
                    def _(act):
                        with when(act, GENERAL):
                            act.sem_inc(msg_in, U)

                            def relu_group(g, k):
                                act.wait_ge(summed, g + 1)
                                act.wait_ge(mm_done, g + 1)
                                nc.scalar.activation(msg[:, k, :, 0:D], attr[:, k, :, :], ACT.Relu).then_inc(relu_in, 1)
                                act.wait_ge(relu_in, g + 1)
                                nc.scalar.copy(msg[:, k, :, D + 1:D + 2],
                                               weight[:, bass.ds(g * G, G)].unsqueeze(2)).then_inc(msg_in, 1)

                            with act.Fori(0, ROUNDS) as r:
                                for k in range(U):
                                    relu_group(r * U + k, k)
                            relu_group(GROUPS - 1, 0)

                @block.tensor
                def _(pe):
                    with when(pe, GENERAL):
                        pe.sem_inc(mm_done, 3)

                        def products(g, k, r, tiles):
                            if with_attr:
                                pe.wait_ge(msg_in, g + 1 + U)
                            else:
                                pe.wait_ge(gathered[k], (r + 1) * 16 * G)
                            pe.wait_ge(onehot_in, g + 1)
                            pe.wait_ge(agg_free, g + 1)
                            for j in range(tiles):
                                mm = pe.matmul(window_sums(k)[:, j * P:(j + 1) * P], lhsT=lhs[:, k, j, 0:out_rows],
                                               rhs=onehot[:, k, j, :], start=True, stop=True)
                            mm.then_inc(mm_done, 1)

                        with pe.Fori(0, ROUNDS) as r:
                            for k in range(U):
                                products(r * U + k, k, r, G)
                        products(GROUPS - 1, 0, ROUNDS, LAST_TILES)

                @block.vector
                def _(dve):
                    with when(dve, GENERAL):
                        dve.sem_inc(agg_free, 2)

                        def prepare(g, k, r):
                            if with_attr:
                                dve.wait_ge(gathered[k], (r + 1) * 16 * G)
                                dve.wait_ge(attr_in[k], (r + 1) * 16)
                                dve.tensor_tensor(attr[:, k, :, :], attr[:, k, :, :], rows_g[:, k, :, 0:D],
                                                  ALU.add).then_inc(summed, 1)
                            dve.wait_ge(mm_done, g + 1)
                            hot_k = onehot[:, k, :, :]
                            eq = dve.tensor_tensor(hot_k, iota[:, :].unsqueeze(1).broadcast_to([P, G, P]),
                                                   dst_rel[:, bass.ds(g * G, G)].unsqueeze(2).broadcast_to([P, G, P]),
                                                   ALU.is_equal)
                            if weighted:
                                eq.then_inc(hot, 1)
                                dve.wait_ge(hot, g + 1)
                                dve.tensor_tensor(hot_k, hot_k,
                                                  weight[:, bass.ds(g * G, G)].unsqueeze(2).broadcast_to([P, G, P]),
                                                  ALU.mult).then_inc(onehot_in, 1)
                            else:
                                eq.then_inc(onehot_in, 1)

                        def accumulate(g, k, tiles):
                            _, bases = nc.values_load_multi_w_load_instructions(
                                first_dst[0:1, bass.ds(g * G, tiles)], engines=DVE_ONLY, min_val=0,
                                max_val=NODES - 1, skip_runtime_bounds_check_because=IN_RANGE)
                            dve.wait_ge(mm_done, g + 4)
                            for j in range(tiles):
                                window = agg[0:out_rows, bass.ds(bases[j], P)]
                                add = dve.tensor_tensor(window, window, window_sums(k)[:, j * P:(j + 1) * P], ALU.add)
                                if j < tiles - 1:
                                    add.then_inc(added, 1)
                                    dve.wait_ge(added, g * (G - 1) + (j + 1))
                            add.then_inc(agg_free, 1)
                            dve.wait_ge(agg_free, g + 3)

                        prepare(0, 0, 0)
                        with dve.Fori(0, ROUNDS) as r:
                            for k in range(U):
                                g = r * U + k
                                k1 = (k + 1) % U
                                prepare(g + 1, k1, r + (k + 1) // U)
                                accumulate(g, k, G)
                        accumulate(GROUPS - 1, 0, LAST_TILES)

        def attention_pass(name, source):
            gathered = [pass_sem(f"general_gathered{k}") for k in range(U)]
            staged, mm_done, hot, agg_free, added = (
                pass_sem("general_staged"), pass_sem("general_mm_done"), pass_sem("general_hot"),
                pass_sem("general_agg_free"), pass_sem("general_added"))
            t_done, src_t_in, s_done, clipped, exped, probs_in = (
                pass_sem("general_t_done"), pass_sem("general_src_t_in"), pass_sem("general_s_done"), pass_sem("general_clipped"),
                pass_sem("general_exped"), pass_sem("general_probs_in"))
            ps_t = ps[:, 0:G * P]
            ps_s = ps[:, G * P:2 * G * P]
            ps_o = ps[0:D + 1, 2 * G * P:3 * G * P]

            with nc.Block() as block:
                @block.gpsimd
                def _(pool):
                    with when(pool, GENERAL):
                        def stage(g, k):
                            pool.tensor_copy(idx[k][:, 0:G], src_idx[:, bass.ds(g * G, G)]).then_inc(staged, 1)

                        def gather(g, k):
                            for j in range(G):
                                pool.indirect_dma_start(rows_g[:, k, j, 0:2 * D], None, source,
                                                        bass.IndirectOffsetOnAxis(ap=idx[k][:, j:j + 1], axis=0)
                                                        ).then_inc(gathered[k], 16)

                        stage(0, 0)
                        with pool.Fori(0, ROUNDS) as r:
                            for k in range(U):
                                g = r * U + k
                                pool.wait_ge(mm_done, g + 1)
                                pool.wait_ge(staged, g + 1)
                                stage(g + 1, (k + 1) % U)
                                gather(g, k)
                        pool.wait_ge(mm_done, GROUPS)
                        pool.wait_ge(staged, GROUPS)
                        gather(GROUPS - 1, 0)

                @block.tensor
                def _(pe):
                    with when(pe, GENERAL):
                        pe.sem_inc(mm_done, 3)

                        def turn(g, k, r):
                            pe.wait_ge(gathered[k], (r + 1) * 16 * G)
                            pe.wait_ge(src_t_in, g + 1)
                            for j in range(G):
                                t = pe.transpose(ps_t[:, j * P:(j + 1) * P], rows_g[:, k, j, 0:P], ident[:, :])
                            t.then_inc(t_done, 1)

                        def score(g):
                            _, bases = nc.values_load_multi_w_load_instructions(
                                first_dst[0:1, bass.ds(g * G, G)], engines=PE_ONLY, min_val=0,
                                max_val=NODES - 1, skip_runtime_bounds_check_because=IN_RANGE)
                            pe.wait_ge(src_t_in, g + 2)
                            pe.wait_ge(clipped, g + 1)
                            for j in range(G):
                                mm = pe.matmul(ps_s[:, j * P:(j + 1) * P], lhsT=src_t[:, j, :],
                                               rhs=qk_t[0:D, bass.ds(bases[j], P)], start=True, stop=True)
                            mm.then_inc(s_done, 1)

                        def products(g, k, tiles):
                            pe.wait_ge(probs_in, g + 1)
                            pe.wait_ge(agg_free, g + 1)
                            for j in range(tiles):
                                mm = pe.matmul(ps_o[:, j * P:(j + 1) * P], lhsT=rows_g[:, k, j, D:2 * D + 1],
                                               rhs=probs[:, j, :], start=True, stop=True)
                            mm.then_inc(mm_done, 1)

                        turn(0, 0, 0)
                        score(0)
                        with pe.Fori(0, ROUNDS) as r:
                            for k in range(U):
                                g = r * U + k
                                turn(g + 1, (k + 1) % U, r + (k + 1) // U)
                                score(g + 1)
                                products(g, k, G)
                        products(GROUPS - 1, 0, LAST_TILES)

                @block.scalar
                def _(act):
                    with when(act, GENERAL):
                        act.sem_inc(src_t_in, 1)

                        def group(g):
                            act.wait_ge(t_done, g + 1)
                            act.wait_ge(s_done, g + 1)
                            nc.scalar.copy(src_t[:, :, :], ps_t[0:D, :].rearrange("p (j e) -> p j e", e=P)).then_inc(src_t_in, 1)
                            act.wait_ge(clipped, g + 2)
                            nc.scalar.activation(scores[:, :, :], scores[:, :, :], ACT.Exp, scale=1.0 / 8.0
                                                 ).then_inc(exped, 1)

                        group(0)
                        with act.Fori(1, GROUPS) as g:
                            group(g)

                @block.vector
                def _(dve):
                    with when(dve, GENERAL):
                        dve.sem_inc(agg_free, 1)
                        dve.sem_inc(clipped, 1)
                        dve.sem_inc(s_done, 1)

                        def clip(g, k):
                            dve.tensor_tensor(onehot[:, k, :, :], iota[:, :].unsqueeze(1).broadcast_to([P, G, P]),
                                              dst_rel[:, bass.ds(g * G, G)].unsqueeze(2).broadcast_to([P, G, P]),
                                              ALU.is_equal).then_inc(hot, 1)
                            dve.wait_ge(s_done, g + 2)
                            dve.tensor_scalar(scores[:, :, :], ps_s.rearrange("p (j e) -> p j e", e=P), 40.0, -40.0,
                                              ALU.min, ALU.max).then_inc(clipped, 1)

                        def pick(g, k):
                            dve.wait_ge(exped, g + 1)
                            dve.wait_ge(hot, g + 1)
                            dve.tensor_tensor(probs[:, :, :], scores[:, :, :], onehot[:, k, :, :], ALU.mult
                                              ).then_inc(probs_in, 1)

                        def accumulate(g, tiles):
                            _, bases = nc.values_load_multi_w_load_instructions(
                                first_dst[0:1, bass.ds(g * G, tiles)], engines=DVE_ONLY, min_val=0,
                                max_val=NODES - 1, skip_runtime_bounds_check_because=IN_RANGE)
                            dve.wait_ge(mm_done, g + 4)
                            for j in range(tiles):
                                window = agg[0:D + 1, bass.ds(bases[j], P)]
                                add = dve.tensor_tensor(window, window, ps_o[:, j * P:(j + 1) * P], ALU.add)
                                if j < tiles - 1:
                                    add.then_inc(added, 1)
                                    dve.wait_ge(added, g * (G - 1) + (j + 1))
                            add.then_inc(agg_free, 1)
                            dve.wait_ge(agg_free, g + 2)

                        clip(0, 0)
                        pick(0, 0)
                        with dve.Fori(0, ROUNDS) as r:
                            for k in range(U):
                                g = r * U + k
                                dve.wait_ge(probs_in, g + 1)
                                clip(g + 1, (k + 1) % U)
                                accumulate(g, G)
                                pick(g + 1, (k + 1) % U)
                        accumulate(GROUPS - 1, LAST_TILES)

        def ring_memsets():
            ones_in = sem("ones_in")
            with nc.Block() as block:
                @block.vector
                def _(dve):
                    with when(dve, GENERAL):
                        dve.memset(msg, 1.0).then_inc(ones_in, 1)
                        dve.memset(rows_g, 1.0).then_inc(ones_in, 1)
                        dve.wait_ge(ones_in, 2)

        def build_pass():
            onehot_src = build_sb("onehot_src", [P, 2 * BT, NPAD], F16)
            hot_dst = build_sb("hot_dst", [P, 2, GB, WD])
            cols = build_sb("cols", [P, 2, GB, 3, WD], F16)
            rows_b = build_sb("rows_b", [P, 2, GB, D])
            attr_b = build_sb("attr_b", [P, 2, GB, D])
            msg_b = build_sb("msg_b", [P, 2, GB, D + 2])
            w_out = build_sb("w_out", [P, 2, CHUNKS, WD])
            gathered = [sem(f"b_gathered{k}") for k in range(2)]
            attr_in = [sem(f"b_attr_in{k}") for k in range(2)]
            stored = [sem(f"b_stored{k}") for k in range(2)]
            staged, summed, msg_in, tail_in, relu_in, ones_b = (
                sem("b_staged"), sem("b_summed"), sem("b_msg_in"), sem("b_tail_in"), sem("b_relu_in"), sem("b_ones"))
            hot_in, cols_in, source_in, block_done, half_done = (
                sem("b_hot_in"), sem("b_cols_in"), sem("b_source_in"), sem("b_block_done"), sem("b_half_done"))
            hi_in, moved, w_free, agg_mm, agg_in = (
                sem("b_hi_in"), sem("b_moved"), sem("b_w_free"), sem("b_agg_mm"), sem("b_agg_in"))
            HALVES = ((0, HALF), (HALF, CHUNKS))
            area = ps[:, 0:CHUNKS * P].rearrange("p (c n) -> p c n", n=P)
            ps_agg = ps[0:D + 2, 7 * BANK:7 * BANK + WD]

            def parity_count(r, k):
                return r * (UB // 2) + k // 2 + 1

            with nc.Block() as block:
                @block.gpsimd
                def _(pool):
                    with when(pool, USUAL):
                        pool.sem_inc(summed, 2)

                        def stage(g, k):
                            pool.tensor_copy(idx[k % UB][:, 0:GB], src_idx[:, bass.ds(g * GB, GB)]).then_inc(staged, 1)

                        def gather(g, k, tiles=GB):
                            pool.wait_ge(summed, g + 1)
                            pool.wait_ge(staged, g + 1)
                            stage(g + 1, k + 1)
                            for j in range(tiles):
                                pool.indirect_dma_start(rows_b[:, k % 2, j, :], None, ins["x"],
                                                        bass.IndirectOffsetOnAxis(ap=idx[k % UB][:, j:j + 1], axis=0)
                                                        ).then_inc(gathered[k % 2], 16)

                        def add(r, k, rows_now, tiles=GB):
                            pool.wait_ge(gathered[k % 2], rows_now)
                            pool.wait_ge(attr_in[k % 2], 16 * parity_count(r, k))
                            pool.tensor_tensor(attr_b[:, k % 2, 0:tiles, :], attr_b[:, k % 2, 0:tiles, :],
                                               rows_b[:, k % 2, 0:tiles, :], ALU.add).then_inc(summed, 1)

                        stage(0, 0)
                        gather(0, 0)
                        with pool.Fori(0, BROUNDS) as r:
                            for k in range(UB):
                                gather(r * UB + k + 1, k + 1)
                                add(r, k, 16 * GB * parity_count(r, k))
                        gather(NG - 1, 1, LAST_GB)
                        add(BROUNDS, 0, 16 * GB * parity_count(BROUNDS, 0))
                        add(BROUNDS, 1, 16 * GB * parity_count(BROUNDS, -1) + 16 * LAST_GB, LAST_GB)

                @block.sync
                def _(sp):
                    with when(sp, USUAL):
                        by_tile = ins["edge_attr_64"][0:FULL_TILES * P, :].rearrange("(t p) d -> p t d", p=P)

                        def load(g, k):
                            sp.wait_ge(msg_in, g + 1)
                            sp.dma_start(attr_b[:, k % 2, :, :], by_tile[:, bass.ds(g * GB, GB), :]
                                         ).then_inc(attr_in[k % 2], 16)

                        def store(g, k, r):
                            sp.wait_ge(moved, 2 * g + 4)
                            sp.dma_start(weights_d[bass.ds(g, 1), :, :].rearrange("a p n -> p (a n)"),
                                         w_out[:, k % 2, :, :].rearrange("p c n -> p (c n)")
                                         ).then_inc(stored[k % 2], 16)
                            sp.wait_ge(stored[k % 2], 16 * parity_count(r, k))
                            sp.sem_inc(w_free, 1)

                        load(0, 0)
                        with sp.Fori(0, BROUNDS) as r:
                            for k in range(UB):
                                g = r * UB + k
                                load(g + 1, k + 1)
                                store(g, k, r)
                        sp.wait_ge(msg_in, NG)
                        sp.dma_start(attr_b[0:TAIL_EDGES, 1, LAST_GB - 1, :],
                                     ins["edge_attr_64"][FULL_TILES * P:EDGES, :]).then_inc(tail_in, 16)
                        sp.wait_ge(tail_in, 16)
                        sp.dma_start(attr_b[:, 1, 0:LAST_GB - 1, :], by_tile[:, (NG - 1) * GB:FULL_TILES, :]
                                     ).then_inc(attr_in[1], 16)
                        store(NG - 2, 0, BROUNDS)
                        store(NG - 1, 1, BROUNDS)

                @block.scalar
                def _(act):
                    with when(act, USUAL):
                        act.sem_inc(msg_in, 2)
                        act.sem_inc(w_free, 2)

                        def columns(g, k, tiles=GB):
                            act.wait_ge(hot_in, g + 1)
                            act.wait_ge(block_done, 3 * g + 3)
                            nc.scalar.copy(cols[:, k % 2, :, 0, :], hot_dst[:, k % 2, :, :])
                            for j in range(tiles):
                                for n, part in enumerate((w_hi, w_mid)):
                                    last = nc.scalar.activation(cols[:, k % 2, j, n + 1, :], hot_dst[:, k % 2, j, :],
                                                                ACT.Copy, scale=part[:, bass.ds(g * GB + j, 1)])
                            last.then_inc(cols_in, 1)

                        def relu(g, k, tiles=GB):
                            act.wait_ge(summed, g + 3)
                            act.wait_ge(agg_mm, g + 1)
                            nc.scalar.activation(msg_b[:, k % 2, 0:tiles, 0:D], attr_b[:, k % 2, 0:tiles, :], ACT.Relu)
                            nc.scalar.copy(msg_b[:, k % 2, 0:tiles, D + 1:D + 2],
                                           weight[:, bass.ds(g * GB, tiles)].unsqueeze(2)).then_inc(msg_in, 1)

                        def take_hi(g, k, half_at, blocks_at):
                            act.wait_ge(w_free, g + 1)
                            act.wait_ge(half_done, half_at)
                            for h, (c0, c1) in enumerate(HALVES):
                                if h:
                                    act.wait_ge(block_done, blocks_at)
                                nc.scalar.copy(w_out[:, k % 2, c0:c1, :], area[:, c0:c1, WD:2 * WD]).then_inc(hi_in, 1)

                        columns(0, 0)
                        with act.Fori(0, BROUNDS) as r:
                            for k in range(UB):
                                g = r * UB + k
                                columns(g + 1, k + 1)
                                relu(g, k)
                                take_hi(g, k, g + 1, 3 * g + 9)
                        columns(NG - 1, 1, LAST_GB)
                        relu(NG - 2, 0)
                        take_hi(NG - 2, 0, NG - 1, 3 * (NG - 2) + 9)
                        relu(NG - 1, 1, LAST_GB)
                        take_hi(NG - 1, 1, NG, 3 * (NG - 1) + 6 + LAST_BLOCKS)

                @block.tensor
                def _(pe):
                    with when(pe, USUAL):
                        pe.sem_inc(block_done, 6)
                        pe.sem_inc(agg_mm, 2)

                        def products(g, k, b, tiles, last):
                            pe.wait_ge(source_in, g * GB + b * BT + tiles)
                            if b == 0:
                                pe.wait_ge(cols_in, g + 1)
                            for h, (c0, c1) in enumerate(HALVES):
                                if b == 0:
                                    pe.wait_ge(moved, 2 * g + 1 + h)
                                for j in range(tiles):
                                    rhs = cols[:, k % 2, b * BT + j, :, :]
                                    for c in range(c0, c1):
                                        mm = pe.matmul(area[:, c, 0:3 * WD],
                                                       lhsT=onehot_src[:, slot(k, b) + j, c * P:(c + 1) * P], rhs=rhs,
                                                       start=(b == 0 and j == 0 and c % PER_BANK == 0),
                                                       stop=(last and j == tiles - 1), skip_group_check=True)
                                if last and h == 0:
                                    mm.then_inc(half_done, 1)
                            mm.then_inc(block_done, 1)

                        def sums(g, k, tiles):
                            pe.wait_ge(msg_in, g + 3)
                            pe.wait_ge(agg_in, g + 1)
                            for j in range(tiles):
                                mm = pe.matmul(ps_agg, lhsT=msg_b[:, k % 2, j, :], rhs=hot_dst[:, k % 2, j, :],
                                               start=(j == 0), stop=(j == tiles - 1))
                            mm.then_inc(agg_mm, 1)

                        with pe.Fori(0, BROUNDS) as r:
                            for k in range(UB):
                                g = r * UB + k
                                for b in range(NB):
                                    products(g, k, b, BT, b == NB - 1)
                                sums(g, k, GB)
                        for b in range(NB):
                            products(NG - 2, 0, b, BT, b == NB - 1)
                        sums(NG - 2, 0, GB)
                        for b in range(LAST_BLOCKS):
                            products(NG - 1, 1, b, min(BT, LAST_GB - b * BT), b == LAST_BLOCKS - 1)
                        sums(NG - 1, 1, LAST_GB)

                @block.vector
                def _(dve):
                    with when(dve, USUAL):
                        dve.memset(msg_b[:, :, :, :], 1.0).then_inc(ones_b, 1)
                        dve.wait_ge(ones_b, 1)
                        dve.sem_inc(moved, 2)
                        dve.sem_inc(agg_in, 1)

                        def destinations(g, k):
                            dve.tensor_tensor(hot_dst[:, k % 2, :, :], iota[:, 0:WD].unsqueeze(1).broadcast_to([P, GB, WD]),
                                              dst_g[:, bass.ds(g * GB, GB)].unsqueeze(2).broadcast_to([P, GB, WD]),
                                              ALU.is_equal).then_inc(hot_in, 1)

                        def sources(g, k, b, tiles=BT):
                            if not (isinstance(g, int) and g * NB + b < 2):
                                dve.wait_ge(block_done, 3 * g + b + 5)
                            for j in range(tiles):
                                dve.tensor_scalar(onehot_src[:, slot(k, b) + j, :], iota_c[:, :],
                                                  src_c[:, bass.ds(g * GB + b * BT + j, 1)], None,
                                                  ALU.is_equal).then_inc(source_in, 1)

                        def move(g, k, base):
                            for h, (c0, c1) in enumerate(HALVES):
                                dve.wait_ge(hi_in, 2 * g + 1 + h)
                                dve.wait_ge(moved, 2 * g + 2 + h)
                                window = adj[:, c0:c1, bass.ds(base, WD)]
                                dve.tensor_tensor(window, window, area[:, c0:c1, 0:WD], ALU.add)
                                dve.scalar_tensor_tensor(w_out[:, k % 2, c0:c1, :], area[:, c0:c1, 2 * WD:3 * WD],
                                                         1.0 / MID, w_out[:, k % 2, c0:c1, :], ALU.mult, ALU.add
                                                         ).then_inc(moved, 1)

                        def add_sums(g, base):
                            dve.wait_ge(agg_mm, g + 3)
                            window = agg[0:D + 2, bass.ds(base, WD)]
                            dve.tensor_tensor(window, window, ps_agg, ALU.add).then_inc(agg_in, 1)

                        def bases_of(g, n):
                            return nc.values_load_multi_w_load_instructions(
                                group_dst[0:1, bass.ds(g, n)], engines=DVE_ONLY, min_val=0, max_val=NODES - 1,
                                skip_runtime_bounds_check_because=IN_RANGE)[1]

                        destinations(0, 0)
                        for b in range(NB):
                            if b == 1:
                                destinations(1, 1)
                            sources(0, 0, b)
                        sources(1, 1, 0)
                        with dve.Fori(0, BROUNDS) as r:
                            bases = bases_of(r * UB, UB)
                            for k in range(UB):
                                g = r * UB + k
                                move(g, k, bases[k])
                                sources(g + 1, k + 1, 1)
                                add_sums(g, bases[k])
                                destinations(g + 2, k + 2)
                                sources(g + 1, k + 1, 2)
                                sources(g + 2, k + 2, 0)
                        bases = bases_of(NG - 2, 2)
                        move(NG - 2, 0, bases[0])
                        sources(NG - 1, 1, 1, LAST_GB - BT)
                        add_sums(NG - 2, bases[0])
                        move(NG - 1, 1, bases[1])
                        add_sums(NG - 1, bases[1])

        def dense_attention():
            SR = 5
            LAG = 3
            s_done, clipped, exped, probs_in, sum_mm, sum_in = (
                sem("d1_s_done"), sem("d1_clipped"), sem("d1_exped"), sem("d1_probs_in"), sem("d1_sum_mm"),
                sem("d1_sum_in"))
            with ExitStack() as scope:
                sc = scope.enter_context(nc.sbuf_tensor("sc", [P, SR, DB], F32))
                ps_s = [ps[:, n * BANK:(n + 1) * BANK] for n in range(SR)]
                ps_v = ps[0:D + 1, SR * BANK:SR * BANK + DB]

                with nc.Block() as block:
                    @block.tensor
                    def _(pe):
                        with when(pe, USUAL):
                            def dests(b, w):
                                def score(c):
                                    pe.wait_ge(clipped, b * CHUNKS + c + 1)
                                    pe.matmul(ps_s[c % SR][:, 0:w], lhsT=qk_t[:, c * P:(c + 1) * P],
                                              rhs=qk_t[:, bass.ds(b * DB, w)], start=True, stop=True
                                              ).then_inc(s_done, 1)

                                def total(c):
                                    if c == 0:
                                        pe.wait_ge(sum_in, b + 1)
                                    pe.wait_ge(probs_in, b * CHUNKS + c + 1 + SR)
                                    mm = pe.matmul(ps_v[:, 0:w], lhsT=v_one[:, c, :], rhs=sc[:, c % SR, 0:w],
                                                   start=(c == 0), stop=(c == CHUNKS - 1))
                                    mm.then_inc(sum_mm, 1)

                                for c in range(CHUNKS + LAG):
                                    if c < CHUNKS:
                                        score(c)
                                    if c >= LAG:
                                        total(c - LAG)

                            with pe.Fori(0, NDB) as b:
                                dests(b, DB)
                            dests(NDB, NPAD - NDB * DB)

                    @block.scalar
                    def _(act):
                        with when(act, USUAL):
                            act.sem_inc(sum_in, 1)

                            def dests(b, w):
                                for c in range(CHUNKS):
                                    act.wait_ge(clipped, b * CHUNKS + c + 1 + SR)
                                    nc.scalar.activation(sc[:, c % SR, 0:w], sc[:, c % SR, 0:w], ACT.Exp,
                                                         scale=1.0 / 8.0).then_inc(exped, 1)
                                act.wait_ge(sum_mm, (b + 1) * CHUNKS + SR)
                                nc.scalar.copy(agg[0:D + 1, bass.ds(b * DB, w)], ps_v[:, 0:w]).then_inc(sum_in, 1)

                            with act.Fori(0, NDB) as b:
                                dests(b, DB)
                            dests(NDB, NPAD - NDB * DB)
                            act.wait_ge(sum_in, NDB + 2)

                    @block.vector
                    def _(dve):
                        with when(dve, USUAL):
                            dve.sem_inc(clipped, SR)
                            dve.sem_inc(probs_in, SR)
                            dve.sem_inc(sum_mm, SR)

                            def dests(b, w):
                                def clip(c):
                                    s = b * CHUNKS + c
                                    dve.wait_ge(s_done, s + 1)
                                    dve.wait_ge(sum_mm, s + 1)
                                    dve.tensor_scalar(sc[:, c % SR, 0:w], ps_s[c % SR][:, 0:w], 40.0, -40.0,
                                                      ALU.min, ALU.max).then_inc(clipped, 1)

                                def pick(c):
                                    s = b * CHUNKS + c
                                    dve.wait_ge(exped, s + 1)
                                    dve.tensor_tensor(sc[:, c % SR, 0:w], sc[:, c % SR, 0:w],
                                                      adj[:, c, bass.ds(b * DB, w)], ALU.mult).then_inc(probs_in, 1)

                                for c in range(CHUNKS + 2):
                                    if c < CHUNKS:
                                        clip(c)
                                    if c >= 2:
                                        pick(c - 2)

                            with dve.Fori(0, NDB) as b:
                                dests(b, DB)
                            dests(NDB, NPAD - NDB * DB)

        def dense_weighted(name, nodes):
            loaded = [sem(f"{name}_loaded{k}") for k in range(WBUF)]
            mm_done, added, free = sem(f"{name}_mm_done"), sem(f"{name}_added"), sem(f"{name}_free")
            with ExitStack() as scope:
                wm = scope.enter_context(nc.sbuf_tensor(f"{name}_wm", [P, WBUF, WB, CHUNKS, WD], F32))
                ps_w = [ps[0:D, n * BANK:n * BANK + WB * WD] for n in range(WBUF)]
                with nc.Block() as block:
                    @block.sync
                    def _(sp):
                        with when(sp, USUAL):
                            with sp.Fori(0, NWB // WBUF) as r:
                                for k in range(WBUF):
                                    n = r * WBUF + k
                                    sp.wait_ge(mm_done, n + 1)
                                    sp.dma_start(wm[:, k, :, :, :].rearrange("p g c n -> p g (c n)"),
                                                 weights_d[bass.ds(n * WB, WB), :, :].rearrange("g p n -> p g n")
                                                 ).then_inc(loaded[k], 16)

                    @block.tensor
                    def _(pe):
                        with when(pe, USUAL):
                            pe.sem_inc(mm_done, WBUF)
                            with pe.Fori(0, NWB // WBUF) as r:
                                for k in range(WBUF):
                                    n = r * WBUF + k
                                    pe.wait_ge(loaded[k], 16 * (r + 1))
                                    pe.wait_ge(free, n + 1)
                                    for c in range(CHUNKS):
                                        mm = pe.matmul(ps_w[k].rearrange("p (g n) -> p g n", n=WD),
                                                       lhsT=nodes[:, c, :], rhs=wm[:, k, :, c, :],
                                                       start=(c == 0), stop=(c == CHUNKS - 1))
                                    mm.then_inc(mm_done, 1)

                    @block.vector
                    def _(dve):
                        with when(dve, USUAL):
                            dve.sem_inc(free, WBUF)
                            dve.sem_inc(added, 1)
                            with dve.Fori(0, NWB // WBUF) as r:
                                for k in range(WBUF):
                                    n = r * WBUF + k
                                    _, bases = nc.values_load_multi_w_load_instructions(
                                        group_dst[0:1, bass.ds(n * WB, WB)], engines=DVE_ONLY, min_val=0,
                                        max_val=NODES - 1, skip_runtime_bounds_check_because=IN_RANGE)
                                    dve.wait_ge(mm_done, n + 1 + WBUF)
                                    for j in range(WB):
                                        dve.wait_ge(added, n * WB + j + 1)
                                        window = agg[0:D, bass.ds(bases[j], WD)]
                                        dve.tensor_tensor(window, window, ps_w[k][:, j * WD:(j + 1) * WD], ALU.add
                                                          ).then_inc(added, 1)
                                    dve.wait_ge(added, n * WB + WB + 1)
                                    dve.sem_inc(free, 1)

        def dense_neighbours():
            CR = 5
            EVEN, ODD = (CHUNKS + 1) // 2, CHUNKS // 2
            counts_a, counts_v, mm_done, out_in = sem("d4_counts_a"), sem("d4_counts_v"), sem("d4_mm"), sem("d4_out")
            with ExitStack() as scope:
                cf = scope.enter_context(nc.sbuf_tensor("cf", [P, CR, DB], F32))
                with nc.Block() as block:
                    @block.scalar
                    def _(act):
                        with when(act, USUAL):
                            act.sem_inc(out_in, 1)

                            def dests(b, w):
                                for c in range(0, CHUNKS, 2):
                                    act.wait_ge(mm_done, b * CHUNKS + c + 1)
                                    nc.scalar.copy(cf[:, c % CR, 0:w], adj[:, c, bass.ds(b * DB, w)]
                                                   ).then_inc(counts_a, 1)
                                act.wait_ge(mm_done, (b + 1) * CHUNKS + CR)
                                nc.scalar.copy(agg[:, bass.ds(b * DB, w)], ps[:, 0:w]).then_inc(out_in, 1)

                            with act.Fori(0, NDB) as b:
                                dests(b, DB)
                            dests(NDB, NPAD - NDB * DB)
                            act.wait_ge(out_in, NDB + 2)

                    @block.vector
                    def _(dve):
                        with when(dve, USUAL):
                            def dests(b, w):
                                for c in range(1, CHUNKS, 2):
                                    dve.wait_ge(mm_done, b * CHUNKS + c + 1)
                                    dve.tensor_copy(cf[:, c % CR, 0:w], adj[:, c, bass.ds(b * DB, w)]
                                                    ).then_inc(counts_v, 1)

                            with dve.Fori(0, NDB) as b:
                                dests(b, DB)
                            dests(NDB, NPAD - NDB * DB)

                    @block.tensor
                    def _(pe):
                        with when(pe, USUAL):
                            pe.sem_inc(mm_done, CR)

                            def dests(b, w):
                                pe.wait_ge(out_in, b + 1)
                                for c in range(CHUNKS):
                                    if c % 2 == 0:
                                        pe.wait_ge(counts_a, b * EVEN + c // 2 + 1)
                                    else:
                                        pe.wait_ge(counts_v, b * ODD + c // 2 + 1)
                                    pe.matmul(ps[:, 0:w], lhsT=table[:, c, :], rhs=cf[:, c % CR, 0:w],
                                              start=(c == 0), stop=(c == CHUNKS - 1)).then_inc(mm_done, 1)

                            with pe.Fori(0, NDB) as b:
                                dests(b, DB)
                            dests(NDB, NPAD - NDB * DB)

        def layer_norm(dve, link, into, of, sqrt_in, sqrt_out, n, eps=LN_EPS):
            mean, var, rstd = stat[:, 1, :], stat[:, 2, :], stat[:, 3, :]
            link(dve.tensor_reduce(mean, of[:, :, :], AX_X, ALU.add))
            link(dve.tensor_scalar(mean, mean, 1.0 / D, None, ALU.mult))
            link(dve.tensor_tensor(of[:, :, :], of[:, :, :], over_features(mean), ALU.subtract))
            link(dve.tensor_tensor(y3[:, :, :], of[:, :, :], of[:, :, :], ALU.mult))
            link(dve.tensor_reduce(var, y3[:, :, :], AX_X, ALU.add))
            dve.tensor_scalar(var, var, 1.0 / D, eps, ALU.mult, ALU.add).then_inc(sqrt_in, 1)
            dve.wait_ge(sqrt_out, n + 1)
            link(dve.reciprocal(rstd, stat[:, 4, :]))
            link(dve.tensor_tensor(into[:, :, :], of[:, :, :], over_features(rstd), ALU.mult))

        def take_roots(act, sqrt_in, sqrt_out, count):
            for n in range(count):
                act.wait_ge(sqrt_in, n + 1)
                nc.scalar.activation(stat[:, 4, :], stat[:, 2, :], ACT.Sqrt).then_inc(sqrt_out, 1)

        ring_memsets()
        edge_pass("p0", ins["x"], D, with_attr=True)
        clear_pass_sems()
        build_pass()
        build.close()
        x_t = sb("x_t", [D + 1, NPAD])
        table = sb("table", [P, CHUNKS, 2 * D])
        h01 = sb("h01", [P, CHUNKS, D])
        y = sb("y", [P, CHUNKS, D])
        y2 = sb("y2", [P, CHUNKS, D])
        y3 = sb("y3", [P, CHUNKS, D])
        layer0 = ExitStack()
        h_t = layer0.enter_context(nc.sbuf_tensor("h_t", [D + 1, NPAD], F32))
        bias_ones = sem("bias_ones")
        with nc.Block() as block:
            @block.vector
            def _(dve):
                dve.memset(x_t[D:D + 1, :], 1.0).then_inc(bias_ones, 1)
                dve.memset(h_t[D:D + 1, :], 1.0).then_inc(bias_ones, 1)
                dve.wait_ge(bias_ones, 2)
        transpose_nodes("x0")

        h_in, mm0, sq_in, sq_out, deg_in, deg_out = (sem("h_in"), sem("mm0"), sem("n0_sq_in"), sem("n0_sq_out"),
                                                     sem("deg_in"), sem("deg_out"))
        PS_DEG = 4 * BANK
        with nc.Block() as block:
            @block.vector
            def _(dve):
                link = chained(dve, "n0")
                dve.scalar_tensor_tensor(h_t[0:D, :], x_t[0:D, :], eps0_p1[0:D, 0:1], agg[0:D, 0:NPAD],
                                         ALU.mult, ALU.add).then_inc(h_in, 1)
                dve.wait_ge(mm0, 1)
                link(dve.tensor_copy(degs[:, :, :],
                                     ps[:, PS_DEG:PS_DEG + 2 * CHUNKS].rearrange("p (c k) -> p c k", k=2)))
                edges_n, weights_n = stat[:, 5, :], stat[:, 6, :]
                link(dve.tensor_scalar(edges_n, degs[:, :, 0], 1.0, None, ALU.max))
                dve.tensor_scalar(weights_n, degs[:, :, 1], 1.0, None, ALU.max).then_inc(deg_in, 1)
                link(dve.reciprocal(rdeg[:, :], edges_n))
                dve.wait_ge(deg_out, 2)
                link(dve.reciprocal(norm3[:, :], stat[:, 7, :]))
                link(dve.reciprocal(norm2[:, :], stat[:, 8, :]))
                dve.wait_ge(mm0, 2)
                link(dve.tensor_scalar(y[:, :, :], ps[:, 0:CHUNKS * D].rearrange("p (c d) -> p c d", d=D), 0.0,
                                       None, ALU.max))
                link(dve.tensor_tensor(y[:, :, :], y[:, :, :], x[:, :, :], ALU.add))
                layer_norm(dve, link, x, y, sq_in, sq_out, 0)
                link(dve.memset(agg[:, :], 0.0))

            @block.scalar
            def _(act):
                act.wait_ge(deg_in, 1)
                nc.scalar.activation(stat[:, 7, :], stat[:, 5, :], ACT.Sqrt).then_inc(deg_out, 1)
                nc.scalar.activation(stat[:, 8, :], stat[:, 6, :], ACT.Sqrt).then_inc(deg_out, 1)
                take_roots(act, sq_in, sq_out, 1)

            @block.tensor
            def _(pe):
                for c in range(CHUNKS):
                    t = pe.transpose(ps[:, PS_DEG + 2 * c:PS_DEG + 2 * c + 2], agg[D:D + 2, c * P:(c + 1) * P],
                                     ident[D:D + 2, D:D + 2])
                t.then_inc(mm0, 1)
                pe.wait_ge(h_in, 1)
                for c in range(CHUNKS):
                    t = pe.matmul(ps[:, c * D:(c + 1) * D], lhsT=h_t[:, c * P:(c + 1) * P], rhs=w_t[:, W_L0, :],
                                  start=True, stop=True)
                t.then_inc(mm0, 1)

        def to_table(name, slot, relu_norm, dram):
            lin, lin_in, written = sem(f"{name}_lin"), sem(f"{name}_lin_in"), sem(f"{name}_written")
            banks = -(-CHUNKS // PER_BANK)
            with nc.Block() as block:
                @block.tensor
                def _(pe):
                    for c in range(CHUNKS):
                        t = pe.matmul(ps[:, c * P:(c + 1) * P], lhsT=x_t[:, c * P:(c + 1) * P],
                                      rhs=w_t[:, slot:slot + 2, :], start=True, stop=True)
                        if c % PER_BANK == PER_BANK - 1 or c == CHUNKS - 1:
                            t.then_inc(lin, 1)

                @block.vector
                def _(dve):
                    link = chained(dve, name)
                    for b in range(banks):
                        c0, c1 = b * PER_BANK, min((b + 1) * PER_BANK, CHUNKS)
                        view = ps[:, c0 * P:c1 * P].rearrange("p (c d) -> p c d", d=P)
                        dve.wait_ge(lin, b + 1)
                        if relu_norm:
                            link(dve.tensor_scalar(table[:, c0:c1, :], view, 0.0, None, ALU.max))
                            dve.tensor_tensor(table[:, c0:c1, :], table[:, c0:c1, :],
                                              norm3[:, c0:c1].unsqueeze(2).broadcast_to([P, c1 - c0, P]),
                                              ALU.mult).then_inc(lin_in, 1)
                        else:
                            dve.tensor_copy(table[:, c0:c1, :], view).then_inc(lin_in, 1)

                @block.sync
                def _(sp):
                    sp.wait_ge(lin_in, banks)
                    sp.dma_start(dram.rearrange("(c p) d -> p c d", p=P), table[:, :, :]).then_inc(written, 16)
                    sp.wait_ge(written, 16)

        layer0.close()
        layer1 = ExitStack()
        qk_t = layer1.enter_context(nc.sbuf_tensor("qk_t", [P, AGG], F32))
        v_one = layer1.enter_context(nc.sbuf_tensor("v_one", [P, CHUNKS, D + 1], F32))
        transpose_nodes("x1")
        to_table("qkv", W_QK, False, qkv_table)
        qt_done, qt_in = sem("qt_done"), sem("qt_in")
        with nc.Block() as block:
            @block.tensor
            def _(pe):
                for b in range(-(-NPAD // BANK)):
                    end = min((b + 1) * BANK, NPAD)
                    pe.matmul(ps[0:D, b * BANK:end], lhsT=w_t[:, W_QK, :], rhs=x_t[:, b * BANK:end],
                              start=True, stop=True).then_inc(qt_done, 1)

            @block.scalar
            def _(act):
                for b in range(-(-NPAD // BANK)):
                    end = min((b + 1) * BANK, NPAD)
                    act.wait_ge(qt_done, b + 1)
                    nc.scalar.copy(qk_t[0:D, b * BANK:end], ps[0:D, b * BANK:end]).then_inc(qt_in, 1)
                act.wait_ge(qt_in, -(-NPAD // BANK))

        v_in = sem("v_in")
        with nc.Block() as block:
            @block.vector
            def _(dve):
                dve.memset(qk_t[0:D, NPAD:AGG], 0.0).then_inc(v_in, 1)
                dve.memset(qk_t[D:P, :], 0.0).then_inc(v_in, 1)
                dve.memset(v_one[:, :, D:D + 1], 1.0).then_inc(v_in, 1)
                dve.tensor_copy(v_one[:, :, 0:D], table[:, :, D:2 * D]).then_inc(v_in, 1)
                dve.wait_ge(v_in, 4)
        attention_pass("p1", qkv_table)
        clear_pass_sems()
        dense_attention()
        layer1.close()

        mm1, sq1_in, sq1_out, num_in, h0_in, h0_written = (sem("mm1"), sem("n1_sq_in"), sem("n1_sq_out"),
                                                           sem("num_in"), sem("h0_in"), sem("h0_written"))
        with nc.Block() as block:
            @block.tensor
            def _(pe):
                for c in range(CHUNKS):
                    t = pe.matmul(ps[:, c * P:c * P + D + 1], lhsT=agg[0:D + 1, c * P:(c + 1) * P], rhs=o_t[:, :],
                                  start=True, stop=True)
                t.then_inc(mm1, 1)

            @block.vector
            def _(dve):
                link = chained(dve, "n1")
                view = ps[:, 0:NPAD].rearrange("p (c d) -> p c d", d=P)
                den = stat[:, 5, :]
                dve.wait_ge(mm1, 1)
                link(dve.tensor_scalar(den, view[:, :, D], 1e-3, None, ALU.max))
                link(dve.reciprocal(den, den))
                link(dve.tensor_tensor(y[:, :, :], view[:, :, 0:D], over_features(den), ALU.mult))
                link(dve.tensor_tensor(y[:, :, :], y[:, :, :], over_chunks(rows[:, R_OB, :]), ALU.add))
                link(dve.tensor_tensor(y[:, :, :], y[:, :, :], x[:, :, :], ALU.add))
                layer_norm(dve, link, y, y, sq1_in, sq1_out, 0)
                link(dve.tensor_tensor(y[:, :, :], y[:, :, :], over_chunks(rows[:, R_LNG, :]), ALU.mult))
                link(dve.tensor_tensor(y[:, :, :], y[:, :, :], over_chunks(rows[:, R_LNB, :]), ALU.add))
                link(dve.tensor_tensor(y[:, :, :], y[:, :, :], x[:, :, :], ALU.add))
                layer_norm(dve, link, x, y, sq1_in, sq1_out, 1)
                dve.tensor_tensor(y2[:, :, :], x[:, :, :], over_features(norm2[:, :]), ALU.mult).then_inc(h0_in, 1)
                link(dve.memset(agg[:, :], 0.0))

            @block.scalar
            def _(act):
                take_roots(act, sq1_in, sq1_out, 2)

            @block.sync
            def _(sp):
                sp.wait_ge(h0_in, 1)
                sp.dma_start(h0_table.rearrange("(c p) d -> p c d", p=P), y2[:, :, :]).then_inc(h0_written, 16)
                sp.wait_ge(h0_written, 16)

        def agg_by_node(pe, done, features):
            for c in range(CHUNKS):
                t = pe.transpose(ps[:, c * P:c * P + features], agg[0:features, c * P:(c + 1) * P],
                                 ident[0:features, 0:features])
            t.then_inc(done, 1)

        edge_pass("p2", h0_table, D, weighted=True)
        clear_pass_sems()
        dense_weighted("d2", y2)
        turned2, h1_in, h1_written = sem("turned2"), sem("h1_in"), sem("h1_written")
        with nc.Block() as block:
            @block.tensor
            def _(pe):
                agg_by_node(pe, turned2, D)

            @block.vector
            def _(dve):
                link = chained(dve, "n2")
                dve.wait_ge(turned2, 1)
                view = ps[:, 0:NPAD].rearrange("p (c d) -> p c d", d=P)[:, :, 0:D]
                link(dve.tensor_tensor(y[:, :, :], view, over_features(norm2[:, :]), ALU.mult))
                dve.tensor_tensor(y2[:, :, :], y[:, :, :], over_features(norm2[:, :]), ALU.mult).then_inc(h1_in, 1)
                link(dve.tensor_tensor(h01[:, :, :], x[:, :, :], y[:, :, :], ALU.add))
                link(dve.memset(agg[:, :], 0.0))

            @block.sync
            def _(sp):
                sp.wait_ge(h1_in, 1)
                sp.dma_start(h1_table.rearrange("(c p) d -> p c d", p=P), y2[:, :, :]).then_inc(h1_written, 16)
                sp.wait_ge(h1_written, 16)

        edge_pass("p3", h1_table, D, weighted=True)
        clear_pass_sems()
        dense_weighted("d3", y2)
        turned3, sq3_in, sq3_out = sem("turned3"), sem("n3_sq_in"), sem("n3_sq_out")
        with nc.Block() as block:
            @block.tensor
            def _(pe):
                agg_by_node(pe, turned3, D)

            @block.vector
            def _(dve):
                link = chained(dve, "n3")
                dve.wait_ge(turned3, 1)
                view = ps[:, 0:NPAD].rearrange("p (c d) -> p c d", d=P)[:, :, 0:D]
                link(dve.tensor_tensor(y[:, :, :], view, over_features(norm2[:, :]), ALU.mult))
                link(dve.tensor_tensor(y[:, :, :], y[:, :, :], h01[:, :, :], ALU.add))
                link(dve.scalar_tensor_tensor(y[:, :, :], y[:, :, :], 1.0 / 3.0, x[:, :, :], ALU.mult, ALU.add))
                layer_norm(dve, link, x, y, sq3_in, sq3_out, 0)
                link(dve.memset(agg[:, :], 0.0))

            @block.scalar
            def _(act):
                take_roots(act, sq3_in, sq3_out, 1)

        transpose_nodes("x3")
        to_table("neigh", W_NEIGH, True, neigh_table)
        edge_pass("p4", neigh_table, 2 * D)
        clear_pass_sems()
        dense_neighbours()
        low = sb("low", [P, 3, CHUNKS, D])
        own, own_in = sem("own"), sem("own_in")
        with nc.Block() as block:
            @block.tensor
            def _(pe):
                for n in range(3):
                    if n:
                        pe.wait_ge(own_in, n)
                    for c in range(CHUNKS):
                        t = pe.matmul(ps[:, c * D:(c + 1) * D], lhsT=x_t[:, c * P:(c + 1) * P],
                                      rhs=w_t[:, W_SELF + n, :], start=True, stop=True)
                    t.then_inc(own, 1)

            @block.scalar
            def _(act):
                for n in range(3):
                    act.wait_ge(own, n + 1)
                    nc.scalar.activation(low[:, n, :, :], ps[:, 0:CHUNKS * D].rearrange("p (c d) -> p c d", d=D),
                                         ACT.Relu).then_inc(own_in, 1)
                act.wait_ge(own_in, 3)

        turned4, sq4_in, sq4_out, logits_in, sig_in, shifted, expd, out_in, written = (
            sem("turned4"), sem("n4_sq_in"), sem("n4_sq_out"), sem("logits_in"), sem("sig_in"), sem("shifted"),
            sem("expd"), sem("out_in"), sem("out_written"))
        with nc.Block() as block:
            @block.tensor
            def _(pe):
                agg_by_node(pe, turned4, 2 * D)

            @block.vector
            def _(dve):
                link = chained(dve, "n4")
                dve.wait_ge(turned4, 1)
                view = ps[:, 0:NPAD].rearrange("p (c d) -> p c d", d=P)
                for n, op in enumerate((ALU.add, ALU.subtract)):
                    link(dve.tensor_tensor(y[:, :, :], view[:, :, n * D:(n + 1) * D], over_features(rdeg[:, :]),
                                           ALU.mult))
                    link(dve.tensor_tensor(low[:, n, :, :], low[:, n, :, :], y[:, :, :], op))
                for n in range(3):
                    link(dve.tensor_tensor(y[:, :, :], low[:, n, :, :], over_chunks(rows[:, R_ATT + n, :]), ALU.mult))
                    red = dve.tensor_reduce(att[:, n, :], y[:, :, :], AX_X, ALU.add)
                    if n < 2:
                        link(red)
                red.then_inc(logits_in, 1)
                dve.wait_ge(sig_in, 1)
                for k in range(3):
                    link(dve.tensor_scalar(att[:, k, :], sig[:, 0, :], w_att[:, 3 * k:3 * k + 1], None, ALU.mult))
                    for j in range(1, 3):
                        link(dve.scalar_tensor_tensor(att[:, k, :], sig[:, j, :], w_att[:, 3 * k + j:3 * k + j + 1],
                                                      att[:, k, :], ALU.mult, ALU.add))
                top, total = stat[:, 5, :], stat[:, 6, :]
                link(dve.tensor_tensor(top, att[:, 0, :], att[:, 1, :], ALU.max))
                link(dve.tensor_tensor(top, top, att[:, 2, :], ALU.max))
                dve.tensor_tensor(att[:, :, :], att[:, :, :], top.unsqueeze(1).broadcast_to([P, 3, CHUNKS]),
                                  ALU.subtract).then_inc(shifted, 1)
                dve.wait_ge(expd, 1)
                link(dve.tensor_tensor(total, att[:, 0, :], att[:, 1, :], ALU.add))
                link(dve.tensor_tensor(total, total, att[:, 2, :], ALU.add))
                link(dve.reciprocal(total, total))
                link(dve.tensor_tensor(att[:, :, :], att[:, :, :], total.unsqueeze(1).broadcast_to([P, 3, CHUNKS]),
                                       ALU.mult))
                link(dve.tensor_tensor(y[:, :, :], low[:, 0, :, :], over_features(att[:, 0, :]), ALU.mult))
                for n in range(1, 3):
                    link(dve.tensor_tensor(y2[:, :, :], low[:, n, :, :], over_features(att[:, n, :]), ALU.mult))
                    link(dve.tensor_tensor(y[:, :, :], y[:, :, :], y2[:, :, :], ALU.add))
                link(dve.scalar_tensor_tensor(y[:, :, :], y[:, :, :], 3.0, x[:, :, :], ALU.mult, ALU.add))
                layer_norm(dve, link, x, y, sq4_in, sq4_out, 0)
                dve.sem_inc(out_in, 1)

            @block.scalar
            def _(act):
                act.wait_ge(logits_in, 1)
                nc.scalar.activation(sig[:, :, :], att[:, :, :], ACT.Sigmoid).then_inc(sig_in, 1)
                act.wait_ge(shifted, 1)
                nc.scalar.activation(att[:, :, :], att[:, :, :], ACT.Exp, scale=1.0 / 3.0).then_inc(expd, 1)
                take_roots(act, sq4_in, sq4_out, 1)

            @block.sync
            def _(sp):
                sp.wait_ge(out_in, 1)
                full, last = node_rows(out)
                sp.dma_start(full, x[:, 0:CHUNKS - 1, :]).then_inc(written, 16)
                sp.dma_start(last, x[0:LAST_NODES, CHUNKS - 1, :]).then_inc(written, 16)
                sp.wait_ge(written, 32)


_INS = (["x", "src", "dst", "edge_attr_64", "edge_weight", "L0_gnn_eps", "L3_gnn_W_att"] + ROWS
        + [w for w, _ in LINEAR] + [b for _, b in LINEAR if b])
_FLAT = set(ROWS) | {"L0_gnn_eps", "L3_gnn_W_att"}


def kernel(**inputs):
    import numpy as _np
    import concourse.bacc as _bacc
    from concourse import mybir as _mybir
    from concourse.bass_utils import run_bass_kernel_spmd as _run

    nc = _bacc.Bacc("TRN2", target_bir_lowering=False, num_devices=1)
    arrays, args = {}, {}
    for name in _INS:
        a = _np.ascontiguousarray(inputs[name])
        if name in _FLAT:
            a = a.reshape(-1)
        arrays[f"in_{name}"] = a
        args[name] = nc.dram_tensor(f"in_{name}", a.shape, _mybir.dt.from_np(a.dtype), kind="ExternalInput").ap()
    out = nc.dram_tensor("out_0", (NODES, D), _mybir.dt.float32, kind="ExternalOutput").ap()
    gnn_program(nc, args, out)
    r = _run(nc, [arrays], core_ids=[0])
    return r.results[0]["out_0"]
```

```python
from contextlib import ExitStack

import concourse.bass as bass
from concourse import mybir

P = 128
D = 64
NODES = 3125
EDGES = 103125
CHUNKS = -(-NODES // P)
NPAD = CHUNKS * P
LAST_NODES = NODES - (CHUNKS - 1) * P
FULL_TILES = EDGES // P
TILES = -(-EDGES // P)
TAIL_EDGES = EDGES - FULL_TILES * P
G = 8
GROUPS = -(-TILES // G)
LAST_TILES = TILES - (GROUPS - 1) * G
U = 4
ROUNDS = (GROUPS - 1) // U
TBLK = -(-TILES // P)
LAST_BLK_TILES = FULL_TILES - (TBLK - 1) * P
TCOLS = TBLK * P
AGG = NPAD + P
BANK = 512
PER_BANK = BANK // P
BANKS = -(-NPAD // BANK)
assert GROUPS == ROUNDS * U + 1 and TCOLS >= (GROUPS + 1) * G

GB = 9
SG = 3
SUBS = GB // SG
WD = 16
KEYS = CHUNKS * WD
NG = -(-TILES // GB)
NS = -(-TILES // SG)
LAST_GB = TILES - (NG - 1) * GB
UB = 4
BROUNDS = (NG - 2) // UB
SCALE = 256.0
W_MAX = 255.0
BOUND = 60000.0
LN_MAX = D ** 0.5
WB = 2
NWB = NG // WB
WBUF = 3
LOADS = WBUF * WB
DB = 512
NDB = NPAD // DB
assert NG == BROUNDS * UB + 2 and NG % WB == 0 and NWB % WBUF == 0 and KEYS <= BANK
assert NS == NG * SUBS - 1 and LAST_GB == SG + 2

F32 = mybir.dt.float32
F16 = mybir.dt.float16
U8 = mybir.dt.uint8
I32 = mybir.dt.int32
ALU = mybir.AluOpType
ACT = mybir.ActivationFunctionType
AX_X = mybir.AxisListType.X
DVE_ONLY = (mybir.EngineType.DVE,)
POOL_ONLY = (mybir.EngineType.Pool,)
PE_ONLY = (mybir.EngineType.PE,)
LN_EPS = 1e-5
IN_RANGE = "a first destination is a node's number"

LINEAR = [("L0_gnn_W", "L0_gnn_b"), ("L1_gnn_qk_w", "L1_gnn_qk_b"), ("L1_gnn_v_w", "L1_gnn_v_b"),
          ("L3_gnn_W_neigh", "L3_gnn_b_neigh"), ("L3_gnn_W_neigh_high", "L3_gnn_b_neigh_high"),
          ("L3_gnn_W_self", "L3_gnn_b_self"), ("L3_gnn_W_self_high", "L3_gnn_b_self_high"),
          ("L3_gnn_W_id", "L3_gnn_b_id"), ("L1_gnn_o_w", None)]
W_L0, W_QK, W_V, W_NEIGH, W_SELF, W_ID, W_O = 0, 1, 2, 3, 5, 7, 8
ROWS = ["L1_gnn_o_b", "L1_gnn_ln_g", "L1_gnn_ln_b", "L3_gnn_w_att_low", "L3_gnn_w_att_high",
        "L3_gnn_w_att_mlp"]
R_OB, R_LNG, R_LNB, R_ATT = 0, 1, 2, 3


def gnn_program(nc, ins, out):
    with ExitStack() as ctx:
        def sb(name, shape, dt=F32):
            return ctx.enter_context(nc.sbuf_tensor(name, shape, dt))

        def sem(name):
            return ctx.enter_context(nc.semaphore(name))

        qkv_table = nc.dram_tensor("qkv_table", [NPAD, 2 * D], F32, kind="Internal").ap()
        h0_table = nc.dram_tensor("h0_table", [NPAD, D], F32, kind="Internal").ap()
        h1_table = nc.dram_tensor("h1_table", [NPAD, D], F32, kind="Internal").ap()
        neigh_table = nc.dram_tensor("neigh_table", [NPAD, 2 * D], F32, kind="Internal").ap()

        weights_d = nc.dram_tensor("weight_matrix", [NG, P, SUBS * KEYS], F32, kind="Internal").ap()

        ident = sb("ident", [P, P])
        ident2 = sb("ident2", [P, D])
        ones = sb("ones", [1, P])
        iota_i = sb("iota_i", [P, P], I32)
        iota = sb("iota", [P, P])
        src_idx = sb("src_idx", [P, TCOLS], I32)
        dst_rel = sb("dst_rel", [P, TCOLS])
        weight = sb("weight", [P, TCOLS])
        first_dst = sb("first_dst", [1, GROUPS * G + 4], I32)
        sub_dst = sb("sub_dst", [1, NS + 3], I32)
        flag = sb("flag", [1, 1], I32)
        w_t = sb("w_t", [D + 1, 8, D])
        w_qk2 = sb("w_qk2", [D + 1, 2 * D])
        w_l0 = sb("w_l0", [D + 3, D])
        o_t = sb("o_t", [D + 1, D + 1])
        rows = sb("rows", [P, len(ROWS), D])
        w_att = sb("w_att", [P, 9])
        eps0 = sb("eps0", [P, 1])
        eps0_p1 = sb("eps0_p1", [P, 1])
        x = sb("x", [P, CHUNKS, D])
        stat = sb("stat", [P, 9, CHUNKS])
        att = sb("att", [P, 3, CHUNKS])
        sig = sb("sig", [P, 3, CHUNKS])
        degs = sb("degs", [P, CHUNKS, 2])
        norm2 = sb("norm2", [P, CHUNKS])
        norm3 = sb("norm3", [P, CHUNKS])
        rdeg = sb("rdeg", [P, CHUNKS])
        agg = sb("agg", [P, AGG])
        arena = sb("arena", [P, CHUNKS * NPAD // 4])
        adj = arena[:, :].bitcast(U8).rearrange("p (c n) -> p c n", n=NPAD)
        taken = [0]

        def ring(*shape):
            n = 1
            for d in shape:
                n *= d
            names = "abcd"[:len(shape)]
            view = arena[:, taken[0]:taken[0] + n].rearrange(
                f"p ({' '.join(names)}) -> p {' '.join(names)}", **dict(zip(names, shape)))
            taken[0] += n
            return view

        idx = [sb(f"idx{k}", [P, max(G, GB)], I32) for k in range(U)]
        rows_g = ring(U, G, 2 * D + 1)
        attr = ring(U, G, D)
        msg = ring(U, G, D + 2)
        onehot = ring(U, G, P)
        src_t = ring(G, P)[0:D, :, :]
        scores = ring(G, P)
        probs = ring(G, P)
        qk_t = ring(AGG)[0:D, :]

        ps = ctx.enter_context(nc.psum_tensor("ps", [P, 8 * BANK], F32))

        src_d, dst_d, w_d = ins["src"], ins["dst"], ins["edge_weight"]

        def edge_blocks(a):
            full = (TBLK - 1) * P * P
            return (a[0:full].rearrange("(b r e) -> r b e", r=P, e=P),
                    a[full:FULL_TILES * P].rearrange("(r e) -> r e", e=P),
                    a[FULL_TILES * P:EDGES].rearrange("(r e) -> r e", r=1))

        def node_rows(a):
            full = (CHUNKS - 1) * P
            return a[0:full, :].rearrange("(c p) d -> p c d", p=P), a[full:NODES, :]

        def over_features(a):
            return a.unsqueeze(2).broadcast_to([P, CHUNKS, D])

        def over_chunks(a):
            return a.unsqueeze(1).broadcast_to([P, CHUNKS, D])

        chain_done, chain_count = sem("chain_done"), [0]

        def chained(dve):
            def link(instruction):
                chain_count[0] += 1
                instruction.then_inc(chain_done, 1)
                dve.wait_ge(chain_done, chain_count[0])
            return link

        GENERAL, USUAL = 1, 0

        def when(eng, way):
            return eng.If(eng.value_load(flag[0:1, 0:1], min_val=0, max_val=1) == way)

        build = ExitStack()

        def build_sb(name, shape, dt=F32):
            return build.enter_context(nc.sbuf_tensor(name, shape, dt))

        src_p = build_sb("src_p", [P, TCOLS])
        key = build_sb("key", [P, NG * GB])
        dst_s = build_sb("dst_s", [P, NG * GB])
        w_hi = build_sb("w_hi", [P, TCOLS])
        w_lo = build_sb("w_lo", [P, TCOLS])
        iota_k = build_sb("iota_k", [P, KEYS], F16)

        rows_b = build_sb("rows_b", [P, 2, GB, D])
        gathered = [sem(f"b_gathered{k}") for k in range(2)]
        staged = sem("b_staged")

        def stage(pool, g, k):
            pool.tensor_copy(idx[k % UB][:, 0:GB], src_idx[:, bass.ds(g * GB, GB)]).then_inc(staged, 1)

        def gather(pool, k, tiles=GB):
            for j in range(tiles):
                pool.indirect_dma_start(rows_b[:, k % 2, j, :], None, ins["x"],
                                        bass.IndirectOffsetOnAxis(ap=idx[k % UB][:, j:j + 1], axis=0)
                                        ).then_inc(gathered[k % 2], 16)

        ld_edges, ld_w, ld_x, ld_base = sem("ld_edges"), sem("ld_w"), sem("ld_x"), sem("ld_base")
        cleared, consts, made = sem("cleared"), sem("consts"), sem("made")
        numbers_in, edges_t, edges_in, w_done, base0 = (sem("numbers_in"), sem("edges_t"), sem("edges_in"),
                                                        sem("w_done"), sem("base0"))
        counted, sizes_in, x_turned, x_taken, arena_zero = sem("counted"), sem("sizes_in"), sem("x_turned"), sem("x_taken"), sem("arena_zero")
        with ExitStack() as setup:
            def setup_sb(name, shape, dt=F32):
                return setup.enter_context(nc.sbuf_tensor(name, shape, dt))

            stage_i = setup_sb("stage_i", [P, 2, TBLK, P], I32)
            stage_f = setup_sb("stage_f", [P, 4, TBLK, P])
            w_stage = setup_sb("w_stage", [D, len(LINEAR), D])
            firsts = setup_sb("firsts", [1, 2 * TILES])
            wmax = setup_sb("wmax", [P, 2])
            w16 = setup_sb("w16", [P, TCOLS], F16)
            block_first = setup_sb("block_first", [P, TBLK])
            checks = setup_sb("checks", [1, 8])
            zero = setup_sb("zero", [P, 1])
            sizes = setup_sb("sizes", [D + 1, 8, D])
            reach = setup_sb("reach", [D + 1, P])
            stage_w = stage_f[:, 2, :, :]
            counts_i = setup_sb("counts_i", [P, KEYS], I32)
            src_bits = setup_sb("src_bits", [P, 2, TCOLS], I32)
            PS_EDGE = [0, 2 * BANK, 4 * BANK, 0]
            PS_GROUP, PS_WMAX = 2 * BANK, 4 * BANK
            PS_W = 6 * BANK
            PS_REACH = 0
            FREE = [1, 3, 5, 6, 7]

            def free_bank(b):
                return ps[:, FREE[b % len(FREE)] * BANK:(FREE[b % len(FREE)] + 1) * BANK]

            with nc.Block() as block:
                @block.sync
                def _(sp):
                    sp.wait_ge(cleared, 3)
                    for a, stage in ((src_d, stage_i[:, 0, :, :]), (dst_d, stage_i[:, 1, :, :]), (w_d, stage_w)):
                        full, part, tail = edge_blocks(a)
                        sp.dma_start(stage[:, 0:TBLK - 1, :], full).then_inc(ld_edges, 16)
                        sp.dma_start(stage[0:LAST_BLK_TILES, TBLK - 1, :], part).then_inc(ld_edges, 16)
                        sp.dma_start(stage[LAST_BLK_TILES:LAST_BLK_TILES + 1, TBLK - 1, 0:TAIL_EDGES],
                                     tail).then_inc(ld_edges, 16)
                    for n, (w, b) in enumerate(LINEAR):
                        sp.dma_start(w_stage[:, n, :], ins[w]).then_inc(ld_w, 16)
                        if b:
                            sp.dma_start(w_t[D:D + 1, n, :], ins[b].rearrange("(a d) -> a d", a=1)).then_inc(ld_w, 16)
                    sp.dma_start(w_l0[D + 2:D + 3, :], ins["L0_gnn_b"].rearrange("(a d) -> a d", a=1)).then_inc(ld_w, 16)
                    full, last = node_rows(ins["x"])
                    sp.wait_ge(cleared, 4)
                    sp.dma_start(x[:, 0:CHUNKS - 1, :], full).then_inc(ld_x, 16)
                    sp.dma_start(x[0:LAST_NODES, CHUNKS - 1, :], last).then_inc(ld_x, 16)
                    sp.wait_ge(ld_x, 32)

                @block.scalar
                def _(act):
                    act.wait_ge(base0, 1)
                    with nc.allow_non_contiguous_dma(reason="one element of each tile, once"):
                        act.dma_start(first_dst[0:1, 0:FULL_TILES],
                                      dst_d[0:FULL_TILES * P].rearrange("(t e) -> e t", e=P)[0:1, :]
                                      ).then_inc(ld_base, 16)
                        act.dma_start(sub_dst[0:1, 0:NS - 1],
                                      dst_d[0:(NS - 1) * SG * P].rearrange("(g e) -> e g", e=SG * P)[0:1, :]
                                      ).then_inc(ld_base, 16)
                    for to, at in ((first_dst[0:1, FULL_TILES:FULL_TILES + 1], FULL_TILES * P),
                                   (sub_dst[0:1, NS - 1:NS], (NS - 1) * SG * P),
                                   (sub_dst[0:1, NS:NS + 1], EDGES - 1)):
                        act.dma_start(to, dst_d[at:at + 1].rearrange("(a e) -> a e", a=1)).then_inc(ld_base, 16)
                    for n, name in enumerate(ROWS):
                        act.dma_start(rows[:, n, :], ins[name].partition_broadcast(P)).then_inc(ld_w, 16)
                    act.dma_start(w_att[:, :], ins["L3_gnn_W_att"].partition_broadcast(P)).then_inc(ld_w, 16)
                    act.dma_start(eps0[:, :], ins["L0_gnn_eps"].partition_broadcast(P)).then_inc(ld_w, 16)
                    act.wait_ge(base0, 1)
                    nc.scalar.copy(arena[:, :], zero[:, :].broadcast_to([P, CHUNKS * NPAD // 4])).then_inc(arena_zero, 1)
                    act.wait_ge(arena_zero, 1)
                    act.wait_ge(ld_base, 5 * 16)
                    act.wait_ge(sizes_in, 1)
                    act.wait_ge(made, 6)
                    for b in range(BANKS):
                        end = min((b + 1) * BANK, NPAD)
                        act.wait_ge(x_turned, b + 1)
                        nc.scalar.activation(agg[0:D, b * BANK:end], free_bank(b)[0:D, 0:end - b * BANK], ACT.Copy,
                                             scale=eps0_p1[0:D, 0:1]).then_inc(x_taken, 1)
                    act.wait_ge(x_taken, BANKS)

                LD_W = 16 * (2 * len(LINEAR) + len(ROWS) + 2)

                @block.gpsimd
                def _(pool):
                    pool.memset(ident[:, :], 0.0).then_inc(consts, 1)
                    pool.wait_ge(consts, 1)
                    pool.iota(iota_i[:, :], pattern=[[1, P]], base=0, channel_multiplier=0).then_inc(consts, 1)
                    pool.wait_ge(consts, 2)
                    pool.affine_select(out=ident[:, :], in_=ident[:, :], compare_op=ALU.not_equal, fill=1.0,
                                       base=0, pattern=[[-1, P]], channel_multiplier=1).then_inc(made, 1)
                    pool.wait_ge(made, 1)
                    pool.iota(counts_i[:, :], pattern=[[1, KEYS]], base=0, channel_multiplier=0).then_inc(counted, 1)
                    pool.wait_ge(counted, 1)
                    pool.memset(o_t[:, :], 0.0).then_inc(consts, 1)
                    pool.wait_ge(consts, 3)
                    for n, (view, value) in enumerate(((ones[:, :], 1.0), (o_t[D:D + 1, D:D + 1], 1.0),
                                                       (agg[:, :], 0.0), (agg[D:D + 3, :], 1.0),
                                                       (agg[D:D + 2, :], 0.0))):
                        pool.memset(view, value).then_inc(made, 1)
                        pool.wait_ge(made, n + 2)
                    pool.wait_ge(edges_in, 1)
                    stage(pool, 0, 0)
                    stage(pool, 1, 1)
                    for k in range(2):
                        pool.wait_ge(staged, k + 1)
                        gather(pool, k)

                @block.vector
                def _(dve):
                    link = chained(dve)
                    dve.memset(zero[:, :], 0.0)
                    dve.memset(first_dst[:, :], 0)
                    dve.memset(sub_dst[:, :], 0).then_inc(base0, 1)
                    dve.memset(stage_i[:, :, TBLK - 1, :], -1).then_inc(cleared, 1)
                    dve.memset(stage_w[:, TBLK - 1, :], 0.0).then_inc(cleared, 1)
                    dve.memset(w_t[:, :, :], 0.0)
                    dve.memset(w_l0[:, :], 0.0).then_inc(cleared, 1)
                    dve.memset(x[:, CHUNKS - 1, :], 0.0).then_inc(cleared, 1)
                    dve.wait_ge(ld_edges, 9 * 16)
                    dve.tensor_scalar(stage_f[:, 0, :, :], stage_i[:, 0, :, :], 0.0, None, ALU.max
                                      ).then_inc(numbers_in, 1)
                    dve.tensor_copy(stage_f[:, 1, :, :], stage_i[:, 1, :, :]).then_inc(numbers_in, 1)
                    dve.wait_ge(numbers_in, 2)
                    link(dve.tensor_copy(block_first[:, :], stage_f[:, 1, :, 0]))
                    for b in range(TBLK):
                        last = dve.tensor_scalar(stage_f[:, 3, b, :], stage_f[:, 1, b, :], block_first[:, b:b + 1],
                                                 None, ALU.subtract)
                    last.then_inc(numbers_in, 1)
                    dve.wait_ge(consts, 2)
                    dve.tensor_copy(iota[:, :], iota_i[:, :])
                    dve.wait_ge(made, 1)
                    dve.tensor_copy(ident2[0:D, :], ident[0:D, 0:D])
                    dve.tensor_copy(ident2[D:P, :], ident[D:P, D:P])
                    dve.wait_ge(counted, 1)
                    link(dve.tensor_copy(iota_k[:, :], counts_i[:, :]))
                    dve.wait_ge(edges_t, 1)
                    dve.tensor_copy(src_idx[:, :], ps[:, PS_EDGE[0]:PS_EDGE[0] + TCOLS]).then_inc(edges_in, 1)
                    dve.wait_ge(edges_in, 1)
                    dve.tensor_scalar(src_bits[:, 0, :], src_idx[:, :], 7, None, ALU.arith_shift_right)
                    link(dve.tensor_scalar(src_bits[:, 1, :], src_idx[:, :], P - 1, None, ALU.bitwise_and))
                    dve.tensor_copy(key[:, :], src_bits[:, 0, 0:NG * GB])
                    link(dve.tensor_copy(src_p[:, :], src_bits[:, 1, :]))
                    dve.wait_ge(edges_t, 2)
                    dve.tensor_copy(dst_s[:, :], ps[:, PS_EDGE[1]:PS_EDGE[1] + NG * GB]).then_inc(edges_in, 1)
                    dve.wait_ge(edges_t, 3)
                    link(dve.tensor_copy(weight[:, :], ps[:, PS_EDGE[2]:PS_EDGE[2] + TCOLS]))
                    link(dve.tensor_scalar(w_lo[:, :], weight[:, :], SCALE, None, ALU.mult))
                    link(dve.tensor_copy(w16[:, :], w_lo[:, :]))
                    link(dve.tensor_copy(w_hi[:, :], w16[:, :]))
                    link(dve.tensor_tensor(w_lo[:, :], w_lo[:, :], w_hi[:, :], ALU.subtract))
                    link(dve.tensor_reduce(wmax[:, 0:1], weight[:, :], AX_X, ALU.max))
                    link(dve.tensor_reduce(wmax[:, 1:2], weight[:, :], AX_X, ALU.min))
                    link(dve.tensor_scalar(wmax[:, 1:2], wmax[:, 1:2], -1e9, None, ALU.mult))
                    dve.tensor_tensor(wmax[:, 0:1], wmax[:, 0:1], wmax[:, 1:2], ALU.max).then_inc(edges_in, 1)
                    dve.wait_ge(edges_t, 4)
                    link(dve.tensor_copy(dst_rel[:, :], ps[:, PS_EDGE[3]:PS_EDGE[3] + TCOLS]))
                    dve.wait_ge(w_done, 1)
                    dve.wait_ge(made, 3)
                    link(dve.tensor_copy(w_t[0:D, :, :], ps[0:D, PS_W:PS_W + 8 * D].rearrange("p (n d) -> p n d", d=D)))
                    dve.tensor_copy(o_t[0:D, 0:D], ps[0:D, PS_W + BANK:PS_W + BANK + D])
                    dve.tensor_copy(w_l0[0:D, :], w_t[0:D, W_L0, :])
                    dve.tensor_copy(w_qk2[:, 0:D], w_t[:, W_QK, :])
                    dve.tensor_copy(w_qk2[:, D:2 * D], w_t[:, W_QK, :])
                    dve.memset(reach[0:D, :], LN_MAX)
                    dve.memset(reach[D:D + 1, :], 1.0)
                    dve.tensor_scalar(eps0_p1[:, :], eps0[:, :], 1.0, None, ALU.add)
                    dve.scalar_tensor_tensor(sizes[:, :, :], w_t[:, :, :], -1.0, w_t[:, :, :], ALU.mult, ALU.max
                                             ).then_inc(sizes_in, 1)
                    dve.wait_ge(ld_base, 5 * 16)
                    numbers, subs = firsts[0:1, 0:TILES], firsts[0:1, TILES:TILES + NS + 1]
                    link(dve.tensor_copy(numbers, first_dst[0:1, 0:TILES]))
                    dve.tensor_copy(subs, sub_dst[0:1, 0:NS + 1]).then_inc(numbers_in, 1)
                    steps = stage_i[0:1, 0, :, :].rearrange("p b e -> p (b e)").bitcast(F32)
                    link(dve.tensor_tensor(steps[0:1, 0:TILES - 1], numbers[0:1, 1:TILES], numbers[0:1, 0:TILES - 1],
                                           ALU.subtract))
                    link(dve.tensor_reduce(checks[0:1, 0:1], steps[0:1, 0:TILES - 1], AX_X, ALU.min))
                    link(dve.tensor_scalar(checks[0:1, 4:5], checks[0:1, 0:1], 1.0, None, ALU.is_lt))
                    dve.wait_ge(numbers_in, 4)
                    link(dve.tensor_tensor(steps[0:1, 0:NS], subs[0:1, 1:NS + 1], subs[0:1, 0:NS], ALU.subtract))
                    link(dve.tensor_reduce(checks[0:1, 1:2], steps[0:1, 0:NS], AX_X, ALU.max))
                    link(dve.tensor_scalar(checks[0:1, 5:6], checks[0:1, 1:2], float(WD - 1), None, ALU.is_gt))
                    dve.wait_ge(edges_t, 6)
                    link(dve.tensor_reduce(checks[0:1, 2:3], ps[0:1, PS_WMAX:PS_WMAX + P], AX_X, ALU.max))
                    link(dve.tensor_scalar(checks[0:1, 6:7], checks[0:1, 2:3], W_MAX, None, ALU.is_gt))
                    dve.wait_ge(edges_t, 7)
                    link(dve.tensor_reduce(checks[0:1, 0:1], ps[0:1, PS_REACH:PS_REACH + 8 * D], AX_X, ALU.max))
                    link(dve.tensor_scalar(checks[0:1, 7:8], checks[0:1, 0:1], BOUND, None, ALU.is_gt))
                    link(dve.tensor_reduce(checks[0:1, 3:4], checks[0:1, 4:8], AX_X, ALU.max))
                    link(dve.tensor_copy(flag[:, :], checks[0:1, 3:4]))
                    sub_cols = ps[:, PS_GROUP:PS_GROUP + NS + 1].unsqueeze(2).broadcast_to([P, NS + 1, SG])
                    by_sub = dst_s[:, :].rearrange("p (g j) -> p g j", j=SG)
                    link(dve.tensor_tensor(by_sub, by_sub, sub_cols, ALU.subtract))
                    link(dve.scalar_tensor_tensor(key[:, :], key[:, :], float(WD), dst_s[:, :], ALU.mult, ALU.add))

                @block.tensor
                def _(pe):
                    def turn(n):
                        for b in range(TBLK):
                            t = pe.transpose(ps[:, PS_EDGE[n] + b * P:PS_EDGE[n] + (b + 1) * P],
                                             stage_f[:, n, b, :], ident[:, :])
                        t.then_inc(edges_t, 1)

                    pe.wait_ge(made, 1)
                    pe.wait_ge(numbers_in, 2)
                    turn(0)
                    turn(1)
                    turn(2)
                    pe.wait_ge(ld_w, LD_W)
                    for n in range(len(LINEAR)):
                        t = pe.transpose(ps[0:D, PS_W + n * D:PS_W + (n + 1) * D], w_stage[:, n, :],
                                         ident[0:D, 0:D])
                    t.then_inc(w_done, 1)
                    pe.wait_ge(numbers_in, 3)
                    pe.wait_ge(edges_in, 1)
                    turn(3)
                    pe.wait_ge(numbers_in, 4)
                    pe.wait_ge(made, 2)
                    pe.wait_ge(edges_in, 2)
                    pe.matmul(ps[:, PS_GROUP:PS_GROUP + NS + 1], lhsT=ones[0:1, :],
                              rhs=firsts[0:1, TILES:TILES + NS + 1],
                              start=True, stop=True).then_inc(edges_t, 1)
                    pe.wait_ge(edges_in, 3)
                    pe.transpose(ps[0:1, PS_WMAX:PS_WMAX + P], wmax[:, 0:1], ident[:, :]).then_inc(edges_t, 1)
                    pe.wait_ge(sizes_in, 1)
                    pe.matmul(ps[:, PS_REACH:PS_REACH + 8 * D], lhsT=reach[:, :],
                              rhs=sizes[:, :, :].rearrange("p n d -> p (n d)"), start=True, stop=True
                              ).then_inc(edges_t, 1)
                    pe.wait_ge(ld_x, 32)
                    for b in range(BANKS):
                        if b >= len(FREE):
                            pe.wait_ge(x_taken, b - len(FREE) + 1)
                        for c in range(b * PER_BANK, min((b + 1) * PER_BANK, CHUNKS)):
                            at = (c - b * PER_BANK) * P
                            t = pe.transpose(free_bank(b)[0:D, at:at + P], x[:, c, :], ident[:, :])
                        t.then_inc(x_turned, 1)

        pass_sems = {}

        def pass_sem(name):
            if name not in pass_sems:
                pass_sems[name] = sem(name)
            return pass_sems[name]

        def clear_pass_sems():
            with nc.Block() as block:
                @block.sync
                def _(sp):
                    with when(sp, GENERAL):
                        for s in pass_sems.values():
                            sp.sem_clear(s)

        gathered_rows = [sem(f"general_gathered{k}") for k in range(U)]

        def before(k, passes):
            return passes * (ROUNDS + (1 if k == 0 else 0)) * 16 * G

        def edge_pass(passes, source, width, with_attr=False, weighted=False):
            gathered = gathered_rows
            attr_in = [pass_sem(f"general_attr_in{k}") for k in range(U)]
            tail_in = pass_sem("general_tail_in")
            staged, mm_done, onehot_in, hot, agg_free, added = (
                pass_sem("general_staged"), pass_sem("general_mm_done"), pass_sem("general_onehot_in"), pass_sem("general_hot"),
                pass_sem("general_agg_free"), pass_sem("general_added"))
            summed, msg_in, relu_in = pass_sem("general_summed"), pass_sem("general_msg_in"), pass_sem("general_relu_in")
            out_rows = D + 2 if with_attr else width
            lhs = msg if with_attr else rows_g

            def window_sums(b):
                return ps[0:out_rows, (b % 2) * G * P:(b % 2 + 1) * G * P]

            with nc.Block() as block:
                @block.gpsimd
                def _(pool):
                    with when(pool, GENERAL):
                        def stage(g, k):
                            pool.tensor_copy(idx[k][:, 0:G], src_idx[:, bass.ds(g * G, G)]).then_inc(staged, 1)

                        def gather(g, k):
                            for j in range(G):
                                pool.indirect_dma_start(rows_g[:, k, j, 0:width], None, source,
                                                        bass.IndirectOffsetOnAxis(ap=idx[k][:, j:j + 1], axis=0)
                                                        ).then_inc(gathered[k], 16)

                        stage(0, 0)
                        with pool.Fori(0, ROUNDS) as r:
                            for k in range(U):
                                g = r * U + k
                                pool.wait_ge(mm_done, g + 1)
                                pool.wait_ge(staged, g + 1)
                                stage(g + 1, (k + 1) % U)
                                gather(g, k)
                        pool.wait_ge(mm_done, GROUPS)
                        pool.wait_ge(staged, GROUPS)
                        gather(GROUPS - 1, 0)

                if with_attr:
                    @block.sync
                    def _(sp):
                        with when(sp, GENERAL):
                            by_tile = ins["edge_attr_64"][0:FULL_TILES * P, :].rearrange("(t p) d -> p t d", p=P)
                            with sp.Fori(0, ROUNDS) as r:
                                for k in range(U):
                                    g = r * U + k
                                    sp.wait_ge(msg_in, g + 1)
                                    sp.dma_start(attr[:, k, :, :], by_tile[:, bass.ds(g * G, G), :]
                                                 ).then_inc(attr_in[k], 16)
                            sp.wait_ge(msg_in, GROUPS)
                            sp.dma_start(attr[0:TAIL_EDGES, 0, LAST_TILES - 1, :],
                                         ins["edge_attr_64"][FULL_TILES * P:EDGES, :]).then_inc(tail_in, 16)
                            sp.wait_ge(tail_in, 16)
                            sp.dma_start(attr[:, 0, 0:LAST_TILES - 1, :], by_tile[:, (GROUPS - 1) * G:FULL_TILES, :]
                                         ).then_inc(attr_in[0], 16)

                    @block.scalar
                    def _(act):
                        with when(act, GENERAL):
                            act.sem_inc(msg_in, U)

                            def relu_group(g, k):
                                act.wait_ge(summed, g + 1)
                                act.wait_ge(mm_done, g + 1)
                                nc.scalar.activation(msg[:, k, :, 0:D], attr[:, k, :, :], ACT.Relu).then_inc(relu_in, 1)
                                act.wait_ge(relu_in, g + 1)
                                nc.scalar.copy(msg[:, k, :, D + 1:D + 2],
                                               weight[:, bass.ds(g * G, G)].unsqueeze(2)).then_inc(msg_in, 1)

                            with act.Fori(0, ROUNDS) as r:
                                for k in range(U):
                                    relu_group(r * U + k, k)
                            relu_group(GROUPS - 1, 0)

                @block.tensor
                def _(pe):
                    with when(pe, GENERAL):
                        pe.sem_inc(mm_done, 3)

                        def products(g, k, r, tiles):
                            if with_attr:
                                pe.wait_ge(msg_in, g + 1 + U)
                            else:
                                pe.wait_ge(gathered[k], before(k, passes) + (r + 1) * 16 * G)
                            pe.wait_ge(onehot_in, g + 1)
                            pe.wait_ge(agg_free, g + 1)
                            for j in range(tiles):
                                mm = pe.matmul(window_sums(k)[:, j * P:(j + 1) * P], lhsT=lhs[:, k, j, 0:out_rows],
                                               rhs=onehot[:, k, j, :], start=True, stop=True)
                            mm.then_inc(mm_done, 1)

                        with pe.Fori(0, ROUNDS) as r:
                            for k in range(U):
                                products(r * U + k, k, r, G)
                        products(GROUPS - 1, 0, ROUNDS, LAST_TILES)

                @block.vector
                def _(dve):
                    with when(dve, GENERAL):
                        dve.sem_inc(agg_free, 2)

                        def prepare(g, k, r):
                            if with_attr:
                                dve.wait_ge(gathered[k], before(k, passes) + (r + 1) * 16 * G)
                                dve.wait_ge(attr_in[k], (r + 1) * 16)
                                dve.tensor_tensor(attr[:, k, :, :], attr[:, k, :, :], rows_g[:, k, :, 0:D],
                                                  ALU.add).then_inc(summed, 1)
                            dve.wait_ge(mm_done, g + 1)
                            hot_k = onehot[:, k, :, :]
                            eq = dve.tensor_tensor(hot_k, iota[:, :].unsqueeze(1).broadcast_to([P, G, P]),
                                                   dst_rel[:, bass.ds(g * G, G)].unsqueeze(2).broadcast_to([P, G, P]),
                                                   ALU.is_equal)
                            if weighted:
                                eq.then_inc(hot, 1)
                                dve.wait_ge(hot, g + 1)
                                dve.tensor_tensor(hot_k, hot_k,
                                                  weight[:, bass.ds(g * G, G)].unsqueeze(2).broadcast_to([P, G, P]),
                                                  ALU.mult).then_inc(onehot_in, 1)
                            else:
                                eq.then_inc(onehot_in, 1)

                        def accumulate(g, k, tiles):
                            _, bases = nc.values_load_multi_w_load_instructions(
                                first_dst[0:1, bass.ds(g * G, tiles)], engines=DVE_ONLY, min_val=0,
                                max_val=NODES - 1, skip_runtime_bounds_check_because=IN_RANGE)
                            dve.wait_ge(mm_done, g + 4)
                            for j in range(tiles):
                                window = agg[0:out_rows, bass.ds(bases[j], P)]
                                add = dve.tensor_tensor(window, window, window_sums(k)[:, j * P:(j + 1) * P], ALU.add)
                                if j < tiles - 1:
                                    add.then_inc(added, 1)
                                    dve.wait_ge(added, g * (G - 1) + (j + 1))
                            add.then_inc(agg_free, 1)
                            dve.wait_ge(agg_free, g + 3)

                        prepare(0, 0, 0)
                        with dve.Fori(0, ROUNDS) as r:
                            for k in range(U):
                                g = r * U + k
                                k1 = (k + 1) % U
                                prepare(g + 1, k1, r + (k + 1) // U)
                                accumulate(g, k, G)
                        accumulate(GROUPS - 1, 0, LAST_TILES)

        def attention_pass(passes, source):
            gathered = gathered_rows
            staged, mm_done, hot, agg_free, added = (
                pass_sem("general_staged"), pass_sem("general_mm_done"), pass_sem("general_hot"),
                pass_sem("general_agg_free"), pass_sem("general_added"))
            t_done, src_t_in, s_done, clipped, exped, probs_in = (
                pass_sem("general_t_done"), pass_sem("general_src_t_in"), pass_sem("general_s_done"), pass_sem("general_clipped"),
                pass_sem("general_exped"), pass_sem("general_probs_in"))
            ps_t = ps[:, 0:G * P]
            ps_s = ps[:, G * P:2 * G * P]
            ps_o = ps[0:D + 1, 2 * G * P:3 * G * P]

            with nc.Block() as block:
                @block.gpsimd
                def _(pool):
                    with when(pool, GENERAL):
                        def stage(g, k):
                            pool.tensor_copy(idx[k][:, 0:G], src_idx[:, bass.ds(g * G, G)]).then_inc(staged, 1)

                        def gather(g, k):
                            for j in range(G):
                                pool.indirect_dma_start(rows_g[:, k, j, 0:2 * D], None, source,
                                                        bass.IndirectOffsetOnAxis(ap=idx[k][:, j:j + 1], axis=0)
                                                        ).then_inc(gathered[k], 16)

                        stage(0, 0)
                        with pool.Fori(0, ROUNDS) as r:
                            for k in range(U):
                                g = r * U + k
                                pool.wait_ge(mm_done, g + 1)
                                pool.wait_ge(staged, g + 1)
                                stage(g + 1, (k + 1) % U)
                                gather(g, k)
                        pool.wait_ge(mm_done, GROUPS)
                        pool.wait_ge(staged, GROUPS)
                        gather(GROUPS - 1, 0)

                @block.tensor
                def _(pe):
                    with when(pe, GENERAL):
                        pe.sem_inc(mm_done, 3)

                        def turn(g, k, r):
                            pe.wait_ge(gathered[k], before(k, passes) + (r + 1) * 16 * G)
                            pe.wait_ge(src_t_in, g + 1)
                            for j in range(G):
                                t = pe.transpose(ps_t[:, j * P:(j + 1) * P], rows_g[:, k, j, 0:P], ident[:, :])
                            t.then_inc(t_done, 1)

                        def score(g):
                            _, bases = nc.values_load_multi_w_load_instructions(
                                first_dst[0:1, bass.ds(g * G, G)], engines=PE_ONLY, min_val=0,
                                max_val=NODES - 1, skip_runtime_bounds_check_because=IN_RANGE)
                            pe.wait_ge(src_t_in, g + 2)
                            pe.wait_ge(clipped, g + 1)
                            for j in range(G):
                                mm = pe.matmul(ps_s[:, j * P:(j + 1) * P], lhsT=src_t[:, j, :],
                                               rhs=qk_t[:, bass.ds(bases[j], P)], start=True, stop=True)
                            mm.then_inc(s_done, 1)

                        def products(g, k, tiles):
                            pe.wait_ge(probs_in, g + 1)
                            pe.wait_ge(agg_free, g + 1)
                            for j in range(tiles):
                                mm = pe.matmul(ps_o[:, j * P:(j + 1) * P], lhsT=rows_g[:, k, j, D:2 * D + 1],
                                               rhs=probs[:, j, :], start=True, stop=True)
                            mm.then_inc(mm_done, 1)

                        turn(0, 0, 0)
                        score(0)
                        with pe.Fori(0, ROUNDS) as r:
                            for k in range(U):
                                g = r * U + k
                                turn(g + 1, (k + 1) % U, r + (k + 1) // U)
                                score(g + 1)
                                products(g, k, G)
                        products(GROUPS - 1, 0, LAST_TILES)

                @block.scalar
                def _(act):
                    with when(act, GENERAL):
                        act.sem_inc(src_t_in, 1)

                        def group(g):
                            act.wait_ge(t_done, g + 1)
                            act.wait_ge(s_done, g + 1)
                            nc.scalar.copy(src_t[:, :, :], ps_t[0:D, :].rearrange("p (j e) -> p j e", e=P)).then_inc(src_t_in, 1)
                            act.wait_ge(clipped, g + 2)
                            nc.scalar.activation(scores[:, :, :], scores[:, :, :], ACT.Exp, scale=1.0 / 8.0
                                                 ).then_inc(exped, 1)

                        group(0)
                        with act.Fori(1, GROUPS) as g:
                            group(g)

                @block.vector
                def _(dve):
                    with when(dve, GENERAL):
                        dve.sem_inc(agg_free, 1)
                        dve.sem_inc(clipped, 1)
                        dve.sem_inc(s_done, 1)

                        def clip(g, k):
                            dve.tensor_tensor(onehot[:, k, :, :], iota[:, :].unsqueeze(1).broadcast_to([P, G, P]),
                                              dst_rel[:, bass.ds(g * G, G)].unsqueeze(2).broadcast_to([P, G, P]),
                                              ALU.is_equal).then_inc(hot, 1)
                            dve.wait_ge(s_done, g + 2)
                            dve.tensor_scalar(scores[:, :, :], ps_s.rearrange("p (j e) -> p j e", e=P), 40.0, -40.0,
                                              ALU.min, ALU.max).then_inc(clipped, 1)

                        def pick(g, k):
                            dve.wait_ge(exped, g + 1)
                            dve.wait_ge(hot, g + 1)
                            dve.tensor_tensor(probs[:, :, :], scores[:, :, :], onehot[:, k, :, :], ALU.mult
                                              ).then_inc(probs_in, 1)

                        def accumulate(g, tiles):
                            _, bases = nc.values_load_multi_w_load_instructions(
                                first_dst[0:1, bass.ds(g * G, tiles)], engines=DVE_ONLY, min_val=0,
                                max_val=NODES - 1, skip_runtime_bounds_check_because=IN_RANGE)
                            dve.wait_ge(mm_done, g + 4)
                            for j in range(tiles):
                                window = agg[0:D + 1, bass.ds(bases[j], P)]
                                add = dve.tensor_tensor(window, window, ps_o[:, j * P:(j + 1) * P], ALU.add)
                                if j < tiles - 1:
                                    add.then_inc(added, 1)
                                    dve.wait_ge(added, g * (G - 1) + (j + 1))
                            add.then_inc(agg_free, 1)
                            dve.wait_ge(agg_free, g + 2)

                        clip(0, 0)
                        pick(0, 0)
                        with dve.Fori(0, ROUNDS) as r:
                            for k in range(U):
                                g = r * U + k
                                dve.wait_ge(probs_in, g + 1)
                                clip(g + 1, (k + 1) % U)
                                accumulate(g, G)
                                pick(g + 1, (k + 1) % U)
                        accumulate(GROUPS - 1, LAST_TILES)

        def ring_memsets():
            ones_in = sem("ones_in")
            with nc.Block() as block:
                @block.vector
                def _(dve):
                    with when(dve, GENERAL):
                        dve.memset(msg, 1.0).then_inc(ones_in, 1)
                        dve.memset(rows_g, 1.0).then_inc(ones_in, 1)
                        dve.wait_ge(ones_in, 2)

        def build_pass():
            hot_p = build_sb("hot_p", [P, SUBS, SG, 3, P], F16)
            hot_key = build_sb("hot_key", [P, SUBS, SG, KEYS], F16)
            hot_dst = build_sb("hot_dst", [P, 2, GB, WD])
            attr_b = build_sb("attr_b", [P, 2, GB, D])
            msg_b = build_sb("msg_b", [P, 2, GB, D + 2])
            w_out = build_sb("w_out", [P, 2, SUBS, KEYS])
            attr_in = [sem(f"b_attr_in{k}") for k in range(2)]
            stored = [sem(f"b_stored{k}") for k in range(2)]
            summed, msg_in, tail_in, ones_b = (
                sem("b_summed"), sem("b_msg_in"), sem("b_tail_in"), sem("b_ones"))
            hot_in, rows_in, cols_in, lo_in, products_done = (
                sem("b_hot_in"), sem("b_rows_in"), sem("b_cols_in"), sem("b_lo_in"), sem("b_products_done"))
            w_taken, moved, w_free, agg_mm, agg_in = (
                sem("b_w_taken"), sem("b_moved"), sem("b_w_free"), sem("b_agg_mm"), sem("b_agg_in"))
            ps_count = [ps[:, 2 * s * BANK:2 * s * BANK + KEYS] for s in range(SUBS)]
            ps_weight = [ps[:, (2 * s + 1) * BANK:(2 * s + 1) * BANK + KEYS] for s in range(SUBS)]
            ps_agg = ps[0:D + 2, 7 * BANK:7 * BANK + SUBS * WD].rearrange("p (s n) -> p s n", n=WD)

            def parity_count(r, k):
                return r * (UB // 2) + k // 2 + 1

            with nc.Block() as block:
                @block.gpsimd
                def _(pool):
                    with when(pool, USUAL):
                        pool.sem_inc(summed, 2)

                        def gather_group(g, k, tiles=GB):
                            pool.wait_ge(summed, g + 1)
                            pool.wait_ge(staged, g + 1)
                            stage(pool, g + 1, k + 1)
                            gather(pool, k, tiles)

                        stage(pool, 2, 2)
                        with pool.Fori(0, BROUNDS - 1) as r:
                            for k in range(2, UB + 2):
                                gather_group(r * UB + k, k)
                        for k in range(2, UB + 1):
                            gather_group((BROUNDS - 1) * UB + k, k)
                        gather_group(NG - 1, UB + 1, LAST_GB)

                @block.sync
                def _(sp):
                    with when(sp, USUAL):
                        by_tile = ins["edge_attr_64"][0:FULL_TILES * P, :].rearrange("(t p) d -> p t d", p=P)

                        def load(g, k):
                            sp.wait_ge(msg_in, g + 1)
                            sp.dma_start(attr_b[:, k % 2, :, :], by_tile[:, bass.ds(g * GB, GB), :]
                                         ).then_inc(attr_in[k % 2], 16)

                        def store(g, k, r):
                            sp.wait_ge(w_taken, SUBS * g + 2 * SUBS)
                            sp.dma_start(weights_d[bass.ds(g, 1), :, :].rearrange("a p n -> p (a n)"),
                                         w_out[:, k % 2, :, :].rearrange("p s n -> p (s n)")
                                         ).then_inc(stored[k % 2], 16)
                            sp.wait_ge(stored[k % 2], 16 * parity_count(r, k))
                            sp.sem_inc(w_free, 1)

                        load(0, 0)
                        with sp.Fori(0, BROUNDS) as r:
                            for k in range(UB):
                                g = r * UB + k
                                load(g + 1, k + 1)
                                store(g, k, r)
                        sp.wait_ge(msg_in, NG)
                        sp.dma_start(attr_b[0:TAIL_EDGES, 1, LAST_GB - 1, :],
                                     ins["edge_attr_64"][FULL_TILES * P:EDGES, :]).then_inc(tail_in, 16)
                        sp.wait_ge(tail_in, 16)
                        sp.dma_start(attr_b[:, 1, 0:LAST_GB - 1, :], by_tile[:, (NG - 1) * GB:FULL_TILES, :]
                                     ).then_inc(attr_in[1], 16)
                        store(NG - 2, 0, BROUNDS)
                        store(NG - 1, 1, BROUNDS)

                @block.scalar
                def _(act):
                    with when(act, USUAL):
                        act.sem_inc(msg_in, 2)
                        act.sem_inc(w_free, 2)
                        act.sem_inc(w_taken, SUBS)

                        def times_lo(g, s, tiles=SG):
                            act.wait_ge(rows_in, SUBS * g + s + 1)
                            for j in range(tiles):
                                last = nc.scalar.activation(hot_p[:, s, j, 2, :], hot_p[:, s, j, 0, :], ACT.Copy,
                                                            scale=w_lo[:, bass.ds(g * GB + s * SG + j, 1)])
                            last.then_inc(lo_in, 1)

                        def take(g, k, s):
                            if s == 0:
                                act.wait_ge(w_free, g + 1)
                            act.wait_ge(products_done, SUBS * g + s + 1 + SUBS)
                            nc.scalar.copy(w_out[:, k % 2, s, :], ps_weight[s]).then_inc(w_taken, 1)

                        def relu(g, k, tiles=GB):
                            act.wait_ge(summed, g + 3)
                            act.wait_ge(agg_mm, g + 1)
                            nc.scalar.activation(msg_b[:, k % 2, 0:tiles, 0:D], attr_b[:, k % 2, 0:tiles, :], ACT.Relu)
                            nc.scalar.copy(msg_b[:, k % 2, 0:tiles, D + 1:D + 2],
                                           weight[:, bass.ds(g * GB, tiles)].unsqueeze(2)).then_inc(msg_in, 1)

                        times_lo(0, 0)
                        with act.Fori(0, BROUNDS) as r:
                            for k in range(UB):
                                g = r * UB + k
                                times_lo(g, 1)
                                take(g, k, 0)
                                times_lo(g, 2)
                                take(g, k, 1)
                                times_lo(g + 1, 0)
                                take(g, k, 2)
                                relu(g, k)
                        g = NG - 2
                        times_lo(g, 1)
                        take(g, 0, 0)
                        times_lo(g, 2)
                        take(g, 0, 1)
                        times_lo(g + 1, 0)
                        take(g, 0, 2)
                        relu(g, 0)
                        g = NG - 1
                        times_lo(g, 1, LAST_GB - SG)
                        take(g, 1, 0)
                        take(g, 1, 1)
                        act.wait_ge(w_taken, SUBS * NG + SUBS - 1)
                        nc.scalar.activation(w_out[:, 1, 2, :], w_out[:, 1, 1, :], ACT.Copy, scale=0.0
                                             ).then_inc(w_taken, 1)
                        relu(g, 1, LAST_GB)

                @block.tensor
                def _(pe):
                    with when(pe, USUAL):
                        pe.sem_inc(products_done, SUBS)
                        pe.sem_inc(agg_mm, 2)

                        def products(g, s, tiles=SG):
                            n = SUBS * g + s
                            pe.wait_ge(cols_in, n + 1)
                            pe.wait_ge(moved, n + 1)
                            for j in range(tiles):
                                pe.matmul(ps_count[s], lhsT=hot_p[:, s, j, 0, :], rhs=hot_key[:, s, j, :],
                                          start=(j == 0), stop=(j == tiles - 1))
                            pe.wait_ge(lo_in, n + 1)
                            pe.wait_ge(w_taken, n + 1)
                            for j in range(tiles):
                                for part in (1, 2):
                                    mm = pe.matmul(ps_weight[s], lhsT=hot_p[:, s, j, part, :], rhs=hot_key[:, s, j, :],
                                                   start=(j == 0 and part == 1), stop=(j == tiles - 1 and part == 2))
                            mm.then_inc(products_done, 1)

                        def sums(g, k, tiles):
                            pe.wait_ge(msg_in, g + 3)
                            pe.wait_ge(hot_in, g + 1)
                            pe.wait_ge(agg_in, SUBS * g + 1)
                            for j in range(tiles):
                                mm = pe.matmul(ps_agg[:, j // SG, :], lhsT=msg_b[:, k % 2, j, :],
                                               rhs=hot_dst[:, k % 2, j, :], start=(j == 0),
                                               stop=(j % SG == SG - 1 or j == tiles - 1), skip_group_check=True)
                            mm.then_inc(agg_mm, 1)

                        with pe.Fori(0, BROUNDS) as r:
                            for k in range(UB):
                                g = r * UB + k
                                for s in range(SUBS):
                                    products(g, s)
                                sums(g, k, GB)
                        for s in range(SUBS):
                            products(NG - 2, s)
                        sums(NG - 2, 0, GB)
                        products(NG - 1, 0)
                        products(NG - 1, 1, LAST_GB - SG)
                        sums(NG - 1, 1, LAST_GB)

                @block.vector
                def _(dve):
                    with when(dve, USUAL):
                        dve.memset(msg_b[:, :, :, :], 1.0).then_inc(ones_b, 1)
                        dve.wait_ge(ones_b, 1)
                        dve.sem_inc(moved, SUBS)
                        dve.sem_inc(agg_in, 1)

                        def destinations(g, k):
                            dve.tensor_tensor(hot_dst[:, k % 2, :, :], iota[:, 0:WD].unsqueeze(1).broadcast_to([P, GB, WD]),
                                              dst_s[:, bass.ds(g * GB, GB)].unsqueeze(2).broadcast_to([P, GB, WD]),
                                              ALU.is_equal).then_inc(hot_in, 1)

                        def columns(g, s, tiles=SG):
                            n = SUBS * g + s
                            if not (isinstance(g, int) and n < SUBS):
                                dve.wait_ge(products_done, n + 1)
                            for j in range(tiles):
                                t = g * GB + s * SG + j
                                p_t = src_p[:, bass.ds(t, 1)]
                                dve.tensor_scalar(hot_p[:, s, j, 0, :], iota_k[:, 0:P], p_t, None, ALU.is_equal)
                                last = dve.tensor_scalar(hot_p[:, s, j, 1, :], iota_k[:, 0:P], p_t,
                                                         w_hi[:, bass.ds(t, 1)], ALU.is_equal, ALU.mult)
                                if j == tiles - 1:
                                    last.then_inc(rows_in, 1)
                                last = dve.tensor_scalar(hot_key[:, s, j, :], iota_k[:, :], key[:, bass.ds(t, 1)], None,
                                                         ALU.is_equal)
                            last.then_inc(cols_in, 1)

                        def move(g, s, base):
                            n = SUBS * g + s
                            dve.wait_ge(products_done, n + 1 + SUBS)
                            dve.wait_ge(moved, n + SUBS)
                            window = adj[:, :, bass.ds(base, WD)]
                            dve.tensor_tensor(window, window, ps_count[s].rearrange("p (c n) -> p c n", n=WD), ALU.add
                                              ).then_inc(moved, 1)

                        def add_rows(r, k, rows_now, tiles=GB):
                            dve.wait_ge(gathered[k % 2], rows_now)
                            dve.wait_ge(attr_in[k % 2], 16 * parity_count(r, k))
                            dve.tensor_tensor(attr_b[:, k % 2, 0:tiles, :], attr_b[:, k % 2, 0:tiles, :],
                                              rows_b[:, k % 2, 0:tiles, :], ALU.add).then_inc(summed, 1)

                        def add_sums(g, bases):
                            dve.wait_ge(agg_mm, g + 3)
                            for s, base in enumerate(bases):
                                dve.wait_ge(agg_in, SUBS * g + s + 1)
                                window = agg[0:D + 2, bass.ds(base, WD)]
                                dve.tensor_tensor(window, window, ps_agg[:, s, :], ALU.add).then_inc(agg_in, 1)

                        def bases_of(g, n):
                            return nc.values_load_multi_w_load_instructions(
                                sub_dst[0:1, bass.ds(g * SUBS, n)], engines=DVE_ONLY, min_val=0, max_val=NODES - 1,
                                skip_runtime_bounds_check_because=IN_RANGE)[1]

                        destinations(0, 0)
                        columns(0, 0)
                        add_rows(0, 0, 16 * GB)
                        columns(0, 1)
                        with dve.Fori(0, BROUNDS) as r:
                            bases = bases_of(r * UB, UB * SUBS)
                            for k in range(UB):
                                g = r * UB + k
                                mine = bases[k * SUBS:(k + 1) * SUBS]
                                columns(g, 2)
                                move(g, 0, mine[0])
                                columns(g + 1, 0)
                                move(g, 1, mine[1])
                                columns(g + 1, 1)
                                move(g, 2, mine[2])
                                add_rows(r, k + 1, 16 * GB * parity_count(r, k + 1))
                                destinations(g + 1, k + 1)
                                add_sums(g, mine)
                        bases = bases_of(NG - 2, 2 * SUBS - 1)
                        g = NG - 2
                        columns(g, 2)
                        move(g, 0, bases[0])
                        columns(g + 1, 0)
                        move(g, 1, bases[1])
                        columns(g + 1, 1, LAST_GB - SG)
                        move(g, 2, bases[2])
                        destinations(g + 1, 1)
                        add_sums(g, bases[0:SUBS])
                        add_rows(BROUNDS, 1, 16 * GB * parity_count(BROUNDS, -1) + 16 * LAST_GB, LAST_GB)
                        move(g + 1, 0, bases[3])
                        move(g + 1, 1, bases[4])
                        add_sums(g + 1, bases[SUBS:])

        def dense_attention():
            SR = 5
            LAG = 4
            biased = sem("biased")
            s_done, clipped, exped, probs_in, sum_mm, sum_in = (
                sem("d1_s_done"), sem("d1_clipped"), sem("d1_exped"), sem("d1_probs_in"), sem("d1_sum_mm"),
                sem("d1_sum_in"))
            with ExitStack() as scope:
                sc = scope.enter_context(nc.sbuf_tensor("sc", [P, SR, DB], F32))
                ps_s = [ps[:, n * BANK:(n + 1) * BANK] for n in range(SR)]
                ps_v = [ps[0:D + 1, n * BANK:n * BANK + DB] for n in (SR, SR + 1)]

                last_w = NPAD - NDB * DB

                def over_dests(eng, block):
                    with eng.Fori(0, NDB // 2 - 1) as r:
                        for h in range(2):
                            block(r * 2 + h, h, DB, DB)
                    block(NDB - 2, 0, DB, DB)
                    block(NDB - 1, 1, DB, last_w)
                    block(NDB, 0, last_w, 0)

                def ahead(step, b, c, w, w_next):
                    if c < CHUNKS:
                        step(b, c, w)
                    elif w_next:
                        step(b + 1, c - CHUNKS, w_next)

                with nc.Block() as block:
                    @block.tensor
                    def _(pe):
                        with when(pe, USUAL):
                            def score(b, c, w):
                                pe.wait_ge(clipped, b * CHUNKS + c + 1)
                                for n, other in enumerate((qk_hh, qk_ll)):
                                    mm = pe.matmul(ps_s[c % SR][:, 0:w], lhsT=qk_hl[:, c * P:(c + 1) * P],
                                                   rhs=other[:, bass.ds(b * DB, w)], start=(n == 0), stop=(n == 1))
                                mm.then_inc(s_done, 1)

                            def total(b, h, c, w):
                                if c == 0:
                                    pe.wait_ge(sum_in, b + 1)
                                pe.wait_ge(probs_in, b * CHUNKS + c + 1 + SR)
                                pe.matmul(ps_v[h][:, 0:w], lhsT=v_one[:, c, :], rhs=sc[:, c % SR, 0:w],
                                          start=(c == 0), stop=(c == CHUNKS - 1)).then_inc(sum_mm, 1)

                            def body(b, h, w, w_next):
                                for c in range(CHUNKS):
                                    ahead(score, b, c + LAG, w, w_next)
                                    total(b, h, c, w)

                            for c in range(LAG):
                                score(0, c, DB)
                            over_dests(pe, body)

                    @block.gpsimd
                    def _(pool):
                        for n, (into, row) in enumerate(((h01, R_OB), (y2, R_LNB))):
                            pool.tensor_tensor(into[:, :, :], x[:, :, :], over_chunks(rows[:, row, :]), ALU.add
                                               ).then_inc(biased, 1)
                            pool.wait_ge(biased, n + 1)

                    @block.scalar
                    def _(act):
                        with when(act, USUAL):
                            act.sem_inc(sum_in, 2)

                            def exponential(b, c, w):
                                act.wait_ge(clipped, b * CHUNKS + c + 1 + SR)
                                nc.scalar.activation(sc[:, c % SR, 0:w], sc[:, c % SR, 0:w], ACT.Exp,
                                                     scale=1.0 / 8.0).then_inc(exped, 1)

                            def body(b, h, w, w_next):
                                for c in range(CHUNKS):
                                    ahead(exponential, b, c + LAG, w, w_next)
                                act.wait_ge(sum_mm, (b + 1) * CHUNKS + SR)
                                nc.scalar.copy(agg[0:D + 1, bass.ds(b * DB, w)], ps_v[h][:, 0:w]).then_inc(sum_in, 1)

                            for c in range(LAG):
                                exponential(0, c, DB)
                            over_dests(act, body)
                            act.wait_ge(sum_in, NDB + 3)

                    @block.vector
                    def _(dve):
                        with when(dve, USUAL):
                            dve.sem_inc(clipped, SR)
                            dve.sem_inc(probs_in, SR)
                            dve.sem_inc(sum_mm, SR)

                            def clip(b, c, w):
                                s = b * CHUNKS + c
                                dve.wait_ge(s_done, s + 1)
                                dve.wait_ge(sum_mm, s + 1)
                                dve.tensor_scalar(sc[:, c % SR, 0:w], ps_s[c % SR][:, 0:w], 40.0, -40.0,
                                                  ALU.min, ALU.max).then_inc(clipped, 1)

                            def pick(b, c, w):
                                s = b * CHUNKS + c
                                dve.wait_ge(exped, s + 1)
                                dve.tensor_tensor(sc[:, c % SR, 0:w], sc[:, c % SR, 0:w],
                                                  adj[:, c, bass.ds(b * DB, w)], ALU.mult).then_inc(probs_in, 1)

                            def body(b, h, w, w_next):
                                for c in range(CHUNKS):
                                    ahead(clip, b, c + 2, w, w_next)
                                    pick(b, c, w)

                            clip(0, 0, DB)
                            clip(0, 1, DB)
                            over_dests(dve, body)

        loaded = [sem(f"w_loaded{k}") for k in range(LOADS)]

        def dense_weighted(name, passes):
            wh_in, wl_in, wp_in, mm_done, added, free = (
                sem(f"{name}_wh_in"), sem(f"{name}_wl_in"), sem(f"{name}_wp_in"), sem(f"{name}_mm_done"),
                sem(f"{name}_added"), sem(f"{name}_free"))
            COLS = WB * SUBS * WD
            with ExitStack() as scope:
                wm = scope.enter_context(nc.sbuf_tensor(f"{name}_wm", [P, LOADS, SUBS, CHUNKS, WD], F32))
                wh = scope.enter_context(nc.sbuf_tensor(f"{name}_wh", [P, WBUF, WB * SUBS, CHUNKS, WD], F16))
                wl = scope.enter_context(nc.sbuf_tensor(f"{name}_wl", [P, WBUF, WB * SUBS, CHUNKS, WD], F16))
                ps_w = [ps[:, n * BANK:n * BANK + COLS] for n in range(WBUF)]

                def blocks(eng, body, count=WBUF):
                    with eng.Fori(0, NWB // WBUF) as r:
                        for k in range(count):
                            body(r * count + k, k, r)

                with nc.Block() as block:
                    @block.sync
                    def _(sp):
                        with when(sp, USUAL):
                            def load(q, k, r):
                                sp.wait_ge(wl_in, q + 1)
                                sp.wait_ge(wp_in, q + 1)
                                sp.dma_start(wm[:, k, :, :, :].rearrange("p s c n -> p (s c n)"),
                                             weights_d[bass.ds(q, 1), :, :].rearrange("g p n -> p (g n)")
                                             ).then_inc(loaded[k], 16)
                            blocks(sp, load, LOADS)

                    @block.scalar
                    def _(act):
                        with when(act, USUAL):
                            def take_hi(q, k, r):
                                act.wait_ge(loaded[k], 16 * (passes * (NWB // WBUF) + r + 1))
                                if k % WB == 0:
                                    act.wait_ge(mm_done, r * WBUF + k // WB + 1)
                                windows = slice(k % WB * SUBS, (k % WB + 1) * SUBS)
                                nc.scalar.copy(wh[:, k // WB, windows, :, :], wm[:, k, :, :, :]).then_inc(wh_in, 1)
                            blocks(act, take_hi, LOADS)

                    @block.tensor
                    def _(pe):
                        with when(pe, USUAL):
                            pe.sem_inc(mm_done, WBUF)

                            def products(n, k, r):
                                pe.wait_ge(wl_in, WB * (n + 1) + LOADS)
                                pe.wait_ge(wp_in, WB * (n + 1) + LOADS)
                                pe.wait_ge(free, n + 1)
                                for c in range(CHUNKS):
                                    for h, half in enumerate((wh, wl)):
                                        mm = pe.matmul(ps_w[k % WBUF].rearrange("p (g n) -> p g n", n=WD),
                                                       lhsT=nodes16[:, c, :], rhs=half[:, k % WBUF, :, c, :],
                                                       start=(c == 0 and h == 0), stop=(c == CHUNKS - 1 and h == 1))
                                mm.then_inc(mm_done, 1)
                            blocks(pe, products)

                    @block.gpsimd
                    def _(pool):
                        with when(pool, USUAL):
                            pool.sem_inc(wp_in, LOADS)

                            def take_lo(q, k, r):
                                pool.wait_ge(wh_in, q + 1)
                                j = k % WB * SUBS + SUBS - 1
                                pool.tensor_tensor(wl[:, k // WB, j, :, :], wm[:, k, SUBS - 1, :, :],
                                                   wh[:, k // WB, j, :, :], ALU.subtract).then_inc(wp_in, 1)
                            blocks(pool, take_lo, LOADS)

                    @block.vector
                    def _(dve):
                        with when(dve, USUAL):
                            dve.sem_inc(wl_in, LOADS)
                            dve.sem_inc(free, WBUF)
                            dve.sem_inc(added, 1)

                            def take_lo(n, k, j):
                                if j % SUBS == 0:
                                    dve.wait_ge(wh_in, WB * n + j // SUBS + 1)
                                lo = dve.tensor_tensor(wl[:, k % WBUF, j, :, :], wm[:, k % WBUF * WB + j // SUBS, j % SUBS, :, :],
                                                       wh[:, k % WBUF, j, :, :], ALU.subtract)
                                if j % SUBS == SUBS - 2:
                                    lo.then_inc(wl_in, 1)

                            def bases_of(n):
                                return nc.values_load_multi_w_load_instructions(
                                    sub_dst[0:1, bass.ds(n * WB * SUBS, WBUF * WB * SUBS)], engines=DVE_ONLY, min_val=0,
                                    max_val=NODES - 1, skip_runtime_bounds_check_because=IN_RANGE)[1]

                            def add_sums(n, k, bases, ahead):
                                for j in range(WB * SUBS):
                                    if ahead and j % SUBS < SUBS - 1:
                                        take_lo(n + 2, k + 2, j)
                                    if j == 0:
                                        dve.wait_ge(mm_done, n + 1 + WBUF)
                                    dve.wait_ge(added, n * WB * SUBS + j + 1)
                                    window = agg[:, bass.ds(bases[k * WB * SUBS + j], WD)]
                                    dve.scalar_tensor_tensor(window, ps_w[k % WBUF][:, j * WD:(j + 1) * WD], 1.0 / SCALE,
                                                             window, ALU.mult, ALU.add).then_inc(added, 1)
                                dve.wait_ge(added, (n + 1) * WB * SUBS + 1)
                                dve.sem_inc(free, 1)

                            for k in range(2):
                                for j in range(WB * SUBS):
                                    if j % SUBS < SUBS - 1:
                                        take_lo(k, k, j)
                            with dve.Fori(0, NWB // WBUF - 1) as r:
                                bases = bases_of(r * WBUF)
                                for k in range(WBUF):
                                    add_sums(r * WBUF + k, k, bases, True)
                            bases = bases_of(NWB - WBUF)
                            for k in range(WBUF):
                                add_sums(NWB - WBUF + k, k, bases, k < WBUF - 2)

        def dense_neighbours():
            CR = 5
            EVEN, ODD = (CHUNKS + 1) // 2, CHUNKS // 2
            logit_in = sem("logit_in")
            counts_a, counts_v, mm_done, out_in = sem("d4_counts_a"), sem("d4_counts_v"), sem("d4_mm"), sem("d4_out")
            with ExitStack() as scope:
                cf = scope.enter_context(nc.sbuf_tensor("cf", [P, CR, DB], F16))
                with nc.Block() as block:
                    @block.gpsimd
                    def _(pool):
                        pool.tensor_tensor(y2[:, :, :], low[:, 2, :, :], over_chunks(rows[:, R_ATT + 2, :]), ALU.mult
                                           ).then_inc(logit_in, 1)
                        pool.wait_ge(logit_in, 1)

                    @block.scalar
                    def _(act):
                        with when(act, USUAL):
                            act.sem_inc(out_in, 2)

                            def dests(b, w, h):
                                for c in range(0, CHUNKS, 2):
                                    act.wait_ge(mm_done, b * CHUNKS + c + 1)
                                    nc.scalar.copy(cf[:, c % CR, 0:w], adj[:, c, bass.ds(b * DB, w)]
                                                   ).then_inc(counts_a, 1)
                                act.wait_ge(mm_done, (b + 1) * CHUNKS + CR)
                                nc.scalar.copy(agg[:, bass.ds(b * DB, w)], ps[:, h * BANK:h * BANK + w]).then_inc(out_in, 1)

                            with act.Fori(0, NDB // 2) as r:
                                for h in range(2):
                                    dests(r * 2 + h, DB, h)
                            dests(NDB, NPAD - NDB * DB, 0)
                            act.wait_ge(out_in, NDB + 3)

                    @block.vector
                    def _(dve):
                        with when(dve, USUAL):
                            def dests(b, w, h):
                                for c in range(1, CHUNKS, 2):
                                    dve.wait_ge(mm_done, b * CHUNKS + c + 1)
                                    dve.tensor_copy(cf[:, c % CR, 0:w], adj[:, c, bass.ds(b * DB, w)]
                                                    ).then_inc(counts_v, 1)

                            with dve.Fori(0, NDB // 2) as r:
                                for h in range(2):
                                    dests(r * 2 + h, DB, h)
                            dests(NDB, NPAD - NDB * DB, 0)
                        dve.wait_ge(logit_in, 1)
                        dve.tensor_reduce(att[:, 2, :], y2[:, :, :], AX_X, ALU.add).then_inc(logit_in, 1)
                        dve.wait_ge(logit_in, 2)

                    @block.tensor
                    def _(pe):
                        with when(pe, USUAL):
                            pe.sem_inc(mm_done, CR)

                            def dests(b, w, h):
                                pe.wait_ge(out_in, b + 1)
                                for c in range(CHUNKS):
                                    if c % 2 == 0:
                                        pe.wait_ge(counts_a, b * EVEN + c // 2 + 1)
                                    else:
                                        pe.wait_ge(counts_v, b * ODD + c // 2 + 1)
                                    for n, half in enumerate((table_hi, table_lo)):
                                        mm = pe.matmul(ps[:, h * BANK:h * BANK + w], lhsT=half[:, c, :], rhs=cf[:, c % CR, 0:w],
                                                       start=(c == 0 and n == 0), stop=(c == CHUNKS - 1 and n == 1))
                                    mm.then_inc(mm_done, 1)

                            with pe.Fori(0, NDB // 2) as r:
                                for h in range(2):
                                    dests(r * 2 + h, DB, h)
                            dests(NDB, NPAD - NDB * DB, 0)

        def layer_norm(dve, link, into, of, sqrt_in, sqrt_out, n, bank_in=None):
            mean, var, rstd = stat[:, 1, :], stat[:, 2, :], stat[:, 3, :]
            link(dve.tensor_reduce(mean, of[:, :, :], AX_X, ALU.add))
            link(dve.tensor_scalar(mean, mean, 1.0 / D, None, ALU.mult))
            link(dve.tensor_tensor(of[:, :, :], of[:, :, :], over_features(mean), ALU.subtract))
            link(dve.tensor_tensor(y3[:, :, :], of[:, :, :], of[:, :, :], ALU.mult))
            link(dve.tensor_reduce(var, y3[:, :, :], AX_X, ALU.add))
            dve.tensor_scalar(var, var, 1.0 / D, LN_EPS, ALU.mult, ALU.add).then_inc(sqrt_in, 1)
            dve.wait_ge(sqrt_out, n + 1)
            link(dve.reciprocal(rstd, stat[:, 4, :]))
            if bank_in is None:
                link(dve.tensor_tensor(into[:, :, :], of[:, :, :], over_features(rstd), ALU.mult))
                return
            for c0, c1 in BANK_CHUNKS:
                dve.tensor_tensor(into[:, c0:c1, :], of[:, c0:c1, :],
                                  rstd[:, c0:c1].unsqueeze(2).broadcast_to([P, c1 - c0, D]), ALU.mult
                                  ).then_inc(bank_in, 1)

        BANK_CHUNKS = [(b * PER_BANK, min((b + 1) * PER_BANK, CHUNKS)) for b in range(BANKS)]
        banks = [(c0 * P, c1 * P) for c0, c1 in BANK_CHUNKS]

        def take_roots(act, sqrt_in, sqrt_out, count):
            for n in range(count):
                act.wait_ge(sqrt_in, n + 1)
                nc.scalar.activation(stat[:, 4, :], stat[:, 2, :], ACT.Sqrt).then_inc(sqrt_out, 1)

        ring_memsets()
        edge_pass(0, ins["x"], D, with_attr=True)
        clear_pass_sems()
        build_pass()
        build.close()
        h01 = sb("h01", [P, CHUNKS, D])
        y = sb("y", [P, CHUNKS, D])
        y2 = sb("y2", [P, CHUNKS, D])
        nodes16 = sb("nodes16", [P, CHUNKS, 2 * D], F16)
        layers01 = ExitStack()
        x_t = layers01.enter_context(nc.sbuf_tensor("x_t", [D + 1, NPAD], F32))
        y3 = layers01.enter_context(nc.sbuf_tensor("y3", [P, CHUNKS, D], F32))
        layer1 = ExitStack()
        v_one = layer1.enter_context(nc.sbuf_tensor("v_one", [P, CHUNKS, D + 1], F32))
        qk_hh = layer1.enter_context(nc.sbuf_tensor("qk_hh", [P, NPAD], F16))
        qk_ll = layer1.enter_context(nc.sbuf_tensor("qk_ll", [P, NPAD], F16))
        qk_hl = layer1.enter_context(nc.sbuf_tensor("qk_hl", [P, NPAD], F16))
        t_done, t_copied, qt_done, hi_in1, lo_in1, v_done, v_in = (
            sem("l1_t_done"), sem("l1_t_copied"), sem("l1_qt_done"), sem("l1_hi_in"), sem("l1_lo_in"), sem("l1_v_done"),
            sem("l1_v_in"))
        hl_in = sem("l1_hl_in")
        mm0, sq_in, sq_out, deg_in, deg_out, x1_in, ones1_in, cleared0 = (
            sem("mm0"), sem("n0_sq_in"), sem("n0_sq_out"), sem("deg_in"), sem("deg_out"), sem("x1_in"), sem("ones1_in"),
            sem("cleared0"))
        PS_DEG = 4 * BANK
        with nc.Block() as block:
            @block.tensor
            def _(pe):
                for c in range(CHUNKS):
                    t = pe.matmul(ps[:, c * D:(c + 1) * D], lhsT=agg[0:D + 3, c * P:(c + 1) * P], rhs=w_l0[:, :],
                                  start=True, stop=True)
                t.then_inc(mm0, 1)
                for c in range(CHUNKS):
                    t = pe.transpose(ps[:, PS_DEG + 2 * c:PS_DEG + 2 * c + 2], agg[D:D + 2, c * P:(c + 1) * P],
                                     ident[D:D + 2, D:D + 2])
                t.then_inc(mm0, 1)
                pe.wait_ge(ones1_in, 1)
                for b, (c0, c1) in enumerate(BANK_CHUNKS):
                    pe.wait_ge(x1_in, b + 1)
                    for c in range(c0, c1):
                        t = pe.transpose(ps[0:D, c * P:(c + 1) * P], x[:, c, :], ident[:, :])
                    t.then_inc(t_done, 1)
                for b, (start, end) in enumerate(banks):
                    pe.wait_ge(t_copied, b + 1)
                    pe.matmul(ps[:, start:end], lhsT=w_qk2[:, :], rhs=x_t[:, start:end], start=True, stop=True
                              ).then_inc(qt_done, 1)
                for b, (start, end) in enumerate(banks):
                    pe.wait_ge(lo_in1, b + 1)
                    for at in range(start, end, P):
                        mm = pe.matmul(ps[:, at:at + D], lhsT=x_t[:, at:at + P], rhs=w_t[:, W_V, :],
                                       start=True, stop=True)
                    mm.then_inc(v_done, 1)

            @block.scalar
            def _(act):
                act.wait_ge(deg_in, 1)
                nc.scalar.activation(stat[:, 7, :], stat[:, 5, :], ACT.Sqrt).then_inc(deg_out, 1)
                nc.scalar.activation(stat[:, 8, :], stat[:, 6, :], ACT.Sqrt).then_inc(deg_out, 1)
                take_roots(act, sq_in, sq_out, 1)

                def take(b):
                    start, end = banks[b]
                    act.wait_ge(qt_done, b + 1)
                    nc.scalar.copy(qk_hh[:, start:end], ps[:, start:end]).then_inc(hi_in1, 1)
                    act.wait_ge(hi_in1, b + 1)
                    nc.scalar.copy(qk_hl[0:D, start:end], qk_hh[0:D, start:end]).then_inc(hl_in, 1)

                for b, (start, end) in enumerate(banks):
                    act.wait_ge(t_done, b + 1)
                    nc.scalar.copy(x_t[0:D, start:end], ps[0:D, start:end]).then_inc(t_copied, 1)
                    if b:
                        take(b - 1)
                take(BANKS - 1)
                act.wait_ge(hl_in, BANKS)

            @block.gpsimd
            def _(pool):
                pool.memset(x_t[D:D + 1, :], 1.0).then_inc(ones1_in, 1)
                pool.wait_ge(ones1_in, 1)
                pool.memset(v_one[:, :, D:D + 1], 1.0).then_inc(ones1_in, 1)
                pool.wait_ge(ones1_in, 2)
                pool.wait_ge(mm0, 2)
                pool.memset(agg[:, :], 0.0).then_inc(cleared0, 1)
                pool.wait_ge(cleared0, 1)

            @block.vector
            def _(dve):
                link = chained(dve)
                dve.wait_ge(mm0, 1)
                link(dve.scalar_tensor_tensor(y[:, :, :], ps[:, 0:CHUNKS * D].rearrange("p (c d) -> p c d", d=D), 0.0,
                                              x[:, :, :], ALU.max, ALU.add))
                dve.wait_ge(mm0, 2)
                link(dve.tensor_copy(degs[:, :, :],
                                     ps[:, PS_DEG:PS_DEG + 2 * CHUNKS].rearrange("p (c k) -> p c k", k=2)))
                edges_n, weights_n = stat[:, 5, :], stat[:, 6, :]
                link(dve.tensor_scalar(edges_n, degs[:, :, 0], 1.0, None, ALU.max))
                dve.tensor_scalar(weights_n, degs[:, :, 1], 1.0, None, ALU.max).then_inc(deg_in, 1)
                link(dve.reciprocal(rdeg[:, :], edges_n))
                layer_norm(dve, link, x, y, sq_in, sq_out, 0, x1_in)
                dve.wait_ge(deg_out, 2)
                dve.reciprocal(norm3[:, :], stat[:, 7, :])
                link(dve.reciprocal(norm2[:, :], stat[:, 8, :]))
                for b, (start, end) in enumerate(banks):
                    dve.wait_ge(hi_in1, b + 1)
                    dve.tensor_tensor(qk_ll[:, start:end], ps[:, start:end], qk_hh[:, start:end], ALU.subtract
                                      ).then_inc(lo_in1, 1)
                for b, (start, end) in enumerate(banks):
                    dve.wait_ge(lo_in1, b + 1)
                    dve.tensor_copy(qk_hl[D:P, start:end], qk_ll[D:P, start:end])
                    dve.wait_ge(v_done, b + 1)
                    dve.tensor_copy(v_one[:, start // P:end // P, 0:D],
                                    ps[:, start:end].rearrange("p (c d) -> p c d", d=P)[:, :, 0:D]).then_inc(v_in, 1)
                dve.wait_ge(v_in, BANKS)

        with nc.sbuf_tensor("table1", [P, CHUNKS, 2 * D], F32) as table:
            lin, lin_in, written1 = sem("qkv_lin"), sem("qkv_lin_in"), sem("qkv_written")
            with nc.Block() as block:
                @block.tensor
                def _(pe):
                    with when(pe, GENERAL):
                        for c in range(CHUNKS):
                            t = pe.matmul(ps[:, c * P:(c + 1) * P], lhsT=x_t[:, c * P:(c + 1) * P],
                                          rhs=w_t[:, W_QK:W_QK + 2, :], start=True, stop=True)
                        t.then_inc(lin, 1)

                @block.vector
                def _(dve):
                    with when(dve, GENERAL):
                        dve.wait_ge(lin, 1)
                        dve.tensor_copy(table[:, :, :], ps[:, 0:NPAD].rearrange("p (c d) -> p c d", d=P)
                                        ).then_inc(lin_in, 1)

                @block.sync
                def _(sp):
                    with when(sp, GENERAL):
                        sp.wait_ge(lin_in, 1)
                        sp.dma_start(qkv_table.rearrange("(c p) d -> p c d", p=P), table[:, :, :]).then_inc(written1, 16)
                        sp.wait_ge(written1, 16)

        gqt_done, gqt_in, pad_in = sem("general_qt_done"), sem("general_qt_in"), sem("general_qt_pad")
        with nc.Block() as block:
            @block.tensor
            def _(pe):
                with when(pe, GENERAL):
                    for start, end in banks:
                        pe.matmul(ps[0:D, start:end], lhsT=w_t[:, W_QK, :], rhs=x_t[:, start:end],
                                  start=True, stop=True).then_inc(gqt_done, 1)

            @block.scalar
            def _(act):
                with when(act, GENERAL):
                    for b, (start, end) in enumerate(banks):
                        act.wait_ge(gqt_done, b + 1)
                        nc.scalar.copy(qk_t[:, start:end], ps[0:D, start:end]).then_inc(gqt_in, 1)
                    act.wait_ge(gqt_in, len(banks))

            @block.vector
            def _(dve):
                with when(dve, GENERAL):
                    dve.memset(qk_t[:, NPAD:AGG], 0.0).then_inc(pad_in, 1)
                    dve.wait_ge(pad_in, 1)

        attention_pass(1, qkv_table)
        clear_pass_sems()
        dense_attention()
        layer1.close()

        halves_in, hi0_in, hi1_in, cleared1, cleared2, cleared3, h01_in = (
            sem("halves_in"), sem("hi0_in"), sem("hi1_in"), sem("cleared1"), sem("cleared2"), sem("cleared3"), sem("h01_in"))

        def upper_halves(act, y2_in, hi_in):
            act.wait_ge(y2_in, 1)
            nc.scalar.copy(nodes16[:, :, 0:D], y2[:, :, :]).then_inc(hi_in, 1)

        def lower_halves(dve, hi_in):
            dve.wait_ge(hi_in, 1)
            dve.tensor_tensor(nodes16[:, :, D:2 * D], y2[:, :, :], nodes16[:, :, 0:D], ALU.subtract
                              ).then_inc(halves_in, 1)

        def clear_agg(pool, read, cleared):
            pool.wait_ge(read, 1)
            pool.memset(agg[:, :], 0.0).then_inc(cleared, 1)
            pool.wait_ge(cleared, 1)

        mm1, sq1_in, sq1_out, h0_in, h0_written = (sem("mm1"), sem("n1_sq_in"), sem("n1_sq_out"),
                                                           sem("h0_in"), sem("h0_written"))
        with nc.Block() as block:
            @block.tensor
            def _(pe):
                for c in range(CHUNKS):
                    t = pe.matmul(ps[:, c * P:c * P + D + 1], lhsT=agg[0:D + 1, c * P:(c + 1) * P], rhs=o_t[:, :],
                                  start=True, stop=True)
                t.then_inc(mm1, 1)

            @block.vector
            def _(dve):
                link = chained(dve)
                view = ps[:, 0:NPAD].rearrange("p (c d) -> p c d", d=P)
                den = stat[:, 5, :]
                dve.wait_ge(mm1, 1)
                link(dve.tensor_scalar(den, view[:, :, D], 1e-3, None, ALU.max))
                link(dve.reciprocal(den, den))
                link(dve.tensor_tensor(y[:, :, :], view[:, :, 0:D], over_features(den), ALU.mult))
                link(dve.tensor_tensor(y[:, :, :], y[:, :, :], h01[:, :, :], ALU.add))
                layer_norm(dve, link, y, y, sq1_in, sq1_out, 0)
                link(dve.tensor_tensor(y[:, :, :], y[:, :, :], over_chunks(rows[:, R_LNG, :]), ALU.mult))
                link(dve.tensor_tensor(y[:, :, :], y[:, :, :], y2[:, :, :], ALU.add))
                layer_norm(dve, link, x, y, sq1_in, sq1_out, 1)
                dve.tensor_tensor(y2[:, :, :], x[:, :, :], over_features(norm2[:, :]), ALU.mult).then_inc(h0_in, 1)
                dve.wait_ge(h0_in, 1)
                lower_halves(dve, hi0_in)
                dve.wait_ge(halves_in, 1)

            @block.scalar
            def _(act):
                take_roots(act, sq1_in, sq1_out, 2)
                upper_halves(act, h0_in, hi0_in)

            @block.gpsimd
            def _(pool):
                clear_agg(pool, mm1, cleared1)

            @block.sync
            def _(sp):
                with when(sp, GENERAL):
                    sp.wait_ge(h0_in, 1)
                    sp.dma_start(h0_table.rearrange("(c p) d -> p c d", p=P), y2[:, :, :]).then_inc(h0_written, 16)
                    sp.wait_ge(h0_written, 16)

        def agg_by_node(pe, done, features):
            for c in range(CHUNKS):
                t = pe.transpose(ps[:, c * P:c * P + features], agg[0:features, c * P:(c + 1) * P],
                                 ident[0:features, 0:features])
            t.then_inc(done, 1)

        def agg_halves_by_node(pe, done):
            for c in range(CHUNKS):
                t = pe.matmul(ps[:, c * P:c * P + D], lhsT=agg[:, c * P:(c + 1) * P], rhs=ident2[:, :],
                              start=True, stop=True)
            t.then_inc(done, 1)

        layers01.close()
        edge_pass(2, h0_table, D, weighted=True)
        clear_pass_sems()
        dense_weighted("d2", 0)
        turned2, h1_in, h1_written = sem("turned2"), sem("h1_in"), sem("h1_written")
        with nc.Block() as block:
            @block.tensor
            def _(pe):
                agg_halves_by_node(pe, turned2)

            @block.vector
            def _(dve):
                link = chained(dve)
                dve.wait_ge(turned2, 1)
                view = ps[:, 0:NPAD].rearrange("p (c d) -> p c d", d=P)[:, :, 0:D]
                link(dve.tensor_tensor(y[:, :, :], view, over_features(norm2[:, :]), ALU.mult))
                dve.tensor_tensor(y2[:, :, :], y[:, :, :], over_features(norm2[:, :]), ALU.mult).then_inc(h1_in, 1)
                dve.wait_ge(h1_in, 1)
                lower_halves(dve, hi1_in)
                dve.wait_ge(halves_in, 2)

            @block.scalar
            def _(act):
                upper_halves(act, h1_in, hi1_in)

            @block.gpsimd
            def _(pool):
                clear_agg(pool, turned2, cleared2)
                pool.wait_ge(h1_in, 1)
                pool.tensor_tensor(h01[:, :, :], x[:, :, :], y[:, :, :], ALU.add).then_inc(h01_in, 1)
                pool.wait_ge(h01_in, 1)

            @block.sync
            def _(sp):
                with when(sp, GENERAL):
                    sp.wait_ge(h1_in, 1)
                    sp.dma_start(h1_table.rearrange("(c p) d -> p c d", p=P), y2[:, :, :]).then_inc(h1_written, 16)
                    sp.wait_ge(h1_written, 16)

        edge_pass(3, h1_table, D, weighted=True)
        clear_pass_sems()
        dense_weighted("d3", 1)
        y3 = sb("y3_", [P, CHUNKS, D])
        low = sb("low", [P, 3, CHUNKS, D])
        x_t = sb("x_t3", [D + 1, NPAD])
        tables = ExitStack()
        table = tables.enter_context(nc.sbuf_tensor("table3", [P, CHUNKS, 2 * D], F32))
        table_hi = nodes16
        table_lo = tables.enter_context(nc.sbuf_tensor("table_lo", [P, CHUNKS, 2 * D], F16))
        x3_in, t3_done, t3_copied, own_mm, own_in, neigh_mm, table_in, hi_in, lo_in, ones3_in, neigh_written = (
            sem("x3_in"), sem("t3_done"), sem("t3_copied"), sem("own_mm"), sem("own_in"), sem("neigh_mm"), sem("table_in"),
            sem("table_hi_in"), sem("table_lo_in"), sem("ones3_in"), sem("neigh_written"))
        PER_OWN = 2
        OWN_BANKS = -(-CHUNKS // PER_OWN)

        def own_bank(c):
            at = c // PER_OWN % 4 * BANK + c % PER_OWN * 3 * D
            return ps[:, at:at + 3 * D]

        def neigh_bank(c):
            at = (4 + c // PER_BANK % 4) * BANK + c % PER_BANK * P
            return ps[:, at:at + P]

        turned3, sq3_in, sq3_out = sem("turned3"), sem("n3_sq_in"), sem("n3_sq_out")
        with nc.Block() as block:
            @block.tensor
            def _(pe):
                agg_halves_by_node(pe, turned3)
                for b, (c0, c1) in enumerate(BANK_CHUNKS):
                    pe.wait_ge(x3_in, b + 1)
                    for c in range(c0, c1):
                        t = pe.transpose(ps[0:D, c * P:(c + 1) * P], x[:, c, :], ident[:, :])
                    t.then_inc(t3_done, 1)
                pe.wait_ge(ones3_in, 1)
                pe.wait_ge(t3_copied, BANKS)
                for c in range(CHUNKS):
                    if c % PER_OWN == 0 and c >= 4 * PER_OWN:
                        pe.wait_ge(own_in, c // PER_OWN - 3)
                    if c % PER_BANK == 0 and c >= 4 * PER_BANK:
                        pe.wait_ge(table_in, c // PER_BANK - 3)
                    x_c = x_t[:, c * P:(c + 1) * P]
                    own = pe.matmul(own_bank(c), lhsT=x_c, rhs=w_t[:, W_SELF:W_SELF + 3, :], start=True, stop=True)
                    if c % PER_OWN == PER_OWN - 1 or c == CHUNKS - 1:
                        own.then_inc(own_mm, 1)
                    neigh = pe.matmul(neigh_bank(c), lhsT=x_c, rhs=w_t[:, W_NEIGH:W_NEIGH + 2, :],
                                      start=True, stop=True)
                    if c % PER_BANK == PER_BANK - 1 or c == CHUNKS - 1:
                        neigh.then_inc(neigh_mm, 1)

            @block.vector
            def _(dve):
                link = chained(dve)
                dve.wait_ge(turned3, 1)
                view = ps[:, 0:NPAD].rearrange("p (c d) -> p c d", d=P)[:, :, 0:D]
                link(dve.tensor_tensor(y[:, :, :], view, over_features(norm2[:, :]), ALU.mult))
                link(dve.tensor_tensor(y[:, :, :], y[:, :, :], h01[:, :, :], ALU.add))
                link(dve.scalar_tensor_tensor(y[:, :, :], y[:, :, :], 1.0 / 3.0, x[:, :, :], ALU.mult, ALU.add))
                layer_norm(dve, link, x, y, sq3_in, sq3_out, 0, x3_in)
                def lower(b):
                    c0, c1 = BANK_CHUNKS[b]
                    dve.wait_ge(hi_in, b + 1)
                    dve.tensor_tensor(table_lo[:, c0:c1, :], table[:, c0:c1, :], table_hi[:, c0:c1, :], ALU.subtract
                                      ).then_inc(lo_in, 1)

                for b, (c0, c1) in enumerate(BANK_CHUNKS):
                    dve.wait_ge(neigh_mm, b + 1)
                    for c in range(c0, c1):
                        last = dve.tensor_scalar(table[:, c, :], neigh_bank(c), 0.0, norm3[:, c:c + 1], ALU.max, ALU.mult)
                    last.then_inc(table_in, 1)
                    if b:
                        lower(b - 1)
                lower(BANKS - 1)
                dve.wait_ge(lo_in, BANKS)

            @block.scalar
            def _(act):
                take_roots(act, sq3_in, sq3_out, 1)
                for b, (start, end) in enumerate(banks):
                    act.wait_ge(t3_done, b + 1)
                    nc.scalar.copy(x_t[0:D, start:end], ps[0:D, start:end]).then_inc(t3_copied, 1)

                def take_own(n):
                    c0, c1 = n * PER_OWN, min((n + 1) * PER_OWN, CHUNKS)
                    act.wait_ge(own_mm, n + 1)
                    at = n % 4 * BANK
                    nc.scalar.activation(low[:, :, c0:c1, :].rearrange("p n c d -> p c n d"),
                                         ps[:, at:at + (c1 - c0) * 3 * D].rearrange("p (c n d) -> p c n d", n=3, d=D),
                                         ACT.Relu).then_inc(own_in, 1)

                for b, (c0, c1) in enumerate(BANK_CHUNKS):
                    for n in range(b * 2, min(b * 2 + 2, OWN_BANKS)):
                        take_own(n)
                    act.wait_ge(table_in, b + 1)
                    nc.scalar.copy(table_hi[:, c0:c1, :], table[:, c0:c1, :]).then_inc(hi_in, 1)
                act.wait_ge(own_in, OWN_BANKS)

            @block.gpsimd
            def _(pool):
                pool.memset(x_t[D:D + 1, :], 1.0).then_inc(ones3_in, 1)
                pool.wait_ge(ones3_in, 1)
                clear_agg(pool, turned3, cleared3)

            @block.sync
            def _(sp):
                with when(sp, GENERAL):
                    sp.wait_ge(table_in, BANKS)
                    sp.dma_start(neigh_table.rearrange("(c p) d -> p c d", p=P), table[:, :, :]).then_inc(neigh_written, 16)
                    sp.wait_ge(neigh_written, 16)


        edge_pass(4, neigh_table, 2 * D)
        clear_pass_sems()
        dense_neighbours()
        tables.close()
        turned4, sq4_in, sq4_out, logits_in, sig_in, shifted, expd, out_in, written = (
            sem("turned4"), sem("n4_sq_in"), sem("n4_sq_out"), sem("logits_in"), sem("sig_in"), sem("shifted"),
            sem("expd"), sem("out_in"), sem("out_written"))
        with nc.Block() as block:
            @block.tensor
            def _(pe):
                agg_by_node(pe, turned4, 2 * D)

            @block.vector
            def _(dve):
                link = chained(dve)
                dve.wait_ge(turned4, 1)
                view = ps[:, 0:NPAD].rearrange("p (c d) -> p c d", d=P)
                for n, op in enumerate((ALU.add, ALU.subtract)):
                    link(dve.tensor_tensor(y[:, :, :], view[:, :, n * D:(n + 1) * D], over_features(rdeg[:, :]),
                                           ALU.mult))
                    link(dve.tensor_tensor(low[:, n, :, :], low[:, n, :, :], y[:, :, :], op))
                for n in range(2):
                    link(dve.tensor_tensor(y[:, :, :], low[:, n, :, :], over_chunks(rows[:, R_ATT + n, :]), ALU.mult))
                    red = dve.tensor_reduce(att[:, n, :], y[:, :, :], AX_X, ALU.add)
                    if n < 1:
                        link(red)
                red.then_inc(logits_in, 1)
                dve.wait_ge(sig_in, 1)
                for k in range(3):
                    link(dve.tensor_scalar(att[:, k, :], sig[:, 0, :], w_att[:, 3 * k:3 * k + 1], None, ALU.mult))
                    for j in range(1, 3):
                        link(dve.scalar_tensor_tensor(att[:, k, :], sig[:, j, :], w_att[:, 3 * k + j:3 * k + j + 1],
                                                      att[:, k, :], ALU.mult, ALU.add))
                top, total = stat[:, 5, :], stat[:, 6, :]
                link(dve.tensor_tensor(top, att[:, 0, :], att[:, 1, :], ALU.max))
                link(dve.tensor_tensor(top, top, att[:, 2, :], ALU.max))
                dve.tensor_tensor(att[:, :, :], att[:, :, :], top.unsqueeze(1).broadcast_to([P, 3, CHUNKS]),
                                  ALU.subtract).then_inc(shifted, 1)
                dve.wait_ge(expd, 1)
                link(dve.tensor_tensor(total, att[:, 0, :], att[:, 1, :], ALU.add))
                link(dve.tensor_tensor(total, total, att[:, 2, :], ALU.add))
                link(dve.reciprocal(total, total))
                link(dve.tensor_tensor(att[:, :, :], att[:, :, :], total.unsqueeze(1).broadcast_to([P, 3, CHUNKS]),
                                       ALU.mult))
                link(dve.tensor_tensor(y[:, :, :], low[:, 0, :, :], over_features(att[:, 0, :]), ALU.mult))
                for n in range(1, 3):
                    link(dve.tensor_tensor(y2[:, :, :], low[:, n, :, :], over_features(att[:, n, :]), ALU.mult))
                    link(dve.tensor_tensor(y[:, :, :], y[:, :, :], y2[:, :, :], ALU.add))
                link(dve.scalar_tensor_tensor(y[:, :, :], y[:, :, :], 3.0, x[:, :, :], ALU.mult, ALU.add))
                layer_norm(dve, link, x, y, sq4_in, sq4_out, 0, out_in)

            @block.scalar
            def _(act):
                act.wait_ge(logits_in, 1)
                nc.scalar.activation(sig[:, :, :], att[:, :, :], ACT.Sigmoid).then_inc(sig_in, 1)
                act.wait_ge(shifted, 1)
                nc.scalar.activation(att[:, :, :], att[:, :, :], ACT.Exp, scale=1.0 / 3.0).then_inc(expd, 1)
                take_roots(act, sq4_in, sq4_out, 1)

            @block.sync
            def _(sp):
                full, last = node_rows(out)
                half = BANKS // 2 * PER_BANK
                sp.wait_ge(out_in, BANKS // 2)
                sp.dma_start(full[:, 0:half, :], x[:, 0:half, :]).then_inc(written, 16)
                sp.wait_ge(out_in, BANKS)
                sp.dma_start(full[:, half:, :], x[:, half:CHUNKS - 1, :]).then_inc(written, 16)
                sp.dma_start(last, x[0:LAST_NODES, CHUNKS - 1, :]).then_inc(written, 16)
                sp.wait_ge(written, 48)


_INS = (["x", "src", "dst", "edge_attr_64", "edge_weight", "L0_gnn_eps", "L3_gnn_W_att"] + ROWS
        + [w for w, _ in LINEAR] + [b for _, b in LINEAR if b])
_FLAT = set(ROWS) | {"L0_gnn_eps", "L3_gnn_W_att"}


def kernel(**inputs):
    import numpy as _np
    import concourse.bacc as _bacc
    from concourse import mybir as _mybir
    from concourse.bass_utils import run_bass_kernel_spmd as _run

    nc = _bacc.Bacc("TRN2", target_bir_lowering=False, num_devices=1)
    arrays, args = {}, {}
    for name in _INS:
        a = _np.ascontiguousarray(inputs[name])
        if name in _FLAT:
            a = a.reshape(-1)
        arrays[f"in_{name}"] = a
        args[name] = nc.dram_tensor(f"in_{name}", a.shape, _mybir.dt.from_np(a.dtype), kind="ExternalInput").ap()
    out = nc.dram_tensor("out_0", (NODES, D), _mybir.dt.float32, kind="ExternalOutput").ap()
    gnn_program(nc, args, out)
    r = _run(nc, [arrays], core_ids=[0])
    return r.results[0]["out_0"]
```
